# Optimizing a Trainium2 kernel written in Bass

```python
import numpy as np
import jax
import jax.numpy as jnp

def _softmax(x, axis=-1):
    return jax.nn.softmax(x, axis=axis)

def _gelu(x):
    return jax.nn.gelu(x, approximate=True)

def _silu(x):
    return jax.nn.silu(x)

def _sigmoid(x):
    return jax.nn.sigmoid(x)

def _layernorm(x, axis=-1, eps=1e-05):
    m = jnp.mean(x, axis=axis, keepdims=True)
    v = jnp.var(x, axis=axis, keepdims=True)
    return (x - m) / jnp.sqrt(v + eps)

def _scatter_add(tgt, idx, src, axis=0):
    return tgt.at[idx].add(src)

def _segment_sum(src, seg, n):
    return jax.ops.segment_sum(src, seg, n)
kernel_name = 'mk_conv_attn_hybrid_d2_conv_nhwc512_r2_f02397'

def setup_inputs(seed: int=0):
    np.random.seed(seed)
    _w = jnp.asarray

    def _rec_inputs():
        import jax
        import jax.numpy as jnp
        _gk = jax.random.key(seed)
        x = -0.0003957 + 1 * jax.random.normal(jax.random.fold_in(_gk, 1), (8, 56, 56, 256), jnp.float32)
        return x
    x = _rec_inputs()

    def _L0_conv_setup():
        import jax, jax.numpy as jnp
        import numpy as np
        EMBED_DIM = 256
        NUM_HEADS = 8
        EXPAND = 2
        D1 = EXPAND * EMBED_DIM
        HEAD_DIM = D1 // NUM_HEADS
        RPE_DIM = 256
        RPE_LAYERS = 3
        N = 56
        M = 56
        BATCH = 8
        EPS = 1e-08

        def simple_rms(x):
            d = x.shape[-1]
            norm = jnp.linalg.norm(x, axis=-1, keepdims=True)
            return x / (norm * d ** (-0.5) + EPS)
        _DP = np.arange(-(N - 1), N, dtype=np.float32)
        _DQ = np.arange(-(M - 1), M, dtype=np.float32)
        _COORDS = np.stack(np.meshgrid(_DP, _DQ, indexing='ij'), axis=-1)
        _RI = (np.arange(2 * N - 1) - (N - 1)) % (2 * N)
        _CI = (np.arange(2 * M - 1) - (M - 1)) % (2 * M)

        def rpe_coeffs(rpe_in_w, rpe_in_b, rpe_h_w, rpe_h_b, rpe_out_w, rpe_out_b):
            t = jnp.asarray(_COORDS) @ rpe_in_w.T + rpe_in_b
            for i in range(RPE_LAYERS):
                t = jax.nn.relu(simple_rms(t)) @ rpe_h_w[i].T + rpe_h_b[i]
            g = jax.nn.relu(simple_rms(t)) @ rpe_out_w.T + rpe_out_b
            g = g.reshape(2 * N - 1, 2 * M - 1, NUM_HEADS, HEAD_DIM)
            return g.transpose(2, 0, 1, 3)

        def tno2d(v, g):
            a = jnp.zeros((NUM_HEADS, 2 * N, 2 * M, HEAD_DIM), dtype=g.dtype)
            a = a.at[:, _RI[:, None], _CI[None, :], :].set(g)
            vf = jnp.fft.rfft2(v, s=(2 * N, 2 * M), axes=(2, 3))
            af = jnp.fft.rfft2(a, axes=(1, 2))
            y = jnp.fft.irfft2(vf * af[None], s=(2 * N, 2 * M), axes=(2, 3))
            return y[:, :, :N, :M, :]
        key = jax.random.key(seed)
        ks = jax.random.split(key, 16)

        def nrm(k, shape, std=0.02):
            return jax.random.normal(k, shape, dtype=jnp.float32) * std
        return {'x': jax.random.normal(ks[0], (BATCH, N, M, EMBED_DIM), dtype=jnp.float32), 'W_u': nrm(ks[1], (D1, EMBED_DIM)), 'b_u': nrm(ks[2], (D1,)), 'W_v': nrm(ks[3], (D1, EMBED_DIM)), 'b_v': nrm(ks[4], (D1,)), 'W_o': nrm(ks[5], (EMBED_DIM, D1)), 'b_o': nrm(ks[6], (EMBED_DIM,)), 'rpe_in_w': nrm(ks[7], (RPE_DIM, 2), 0.5), 'rpe_in_b': nrm(ks[8], (RPE_DIM,), 0.5), 'rpe_h_w': nrm(ks[9], (RPE_LAYERS, RPE_DIM, RPE_DIM), 0.05), 'rpe_h_b': nrm(ks[10], (RPE_LAYERS, RPE_DIM), 0.05), 'rpe_out_w': nrm(ks[11], (NUM_HEADS * HEAD_DIM, RPE_DIM), 0.05), 'rpe_out_b': nrm(ks[12], (NUM_HEADS * HEAD_DIM,), 0.05), 'H': N, 'W': M}
    _L0_conv_all = _L0_conv_setup()
    _L0_conv_in = {k: v for k, v in _L0_conv_all.items() if k in ('W_u', 'b_u', 'W_v', 'b_v', 'W_o', 'b_o', 'rpe_in_w', 'rpe_in_b', 'rpe_h_w', 'rpe_h_b', 'rpe_out_w', 'rpe_out_b')}
    del _L0_conv_all

    def _L1_attn_setup():
        import jax, jax.numpy as jnp
        import numpy as np
        B, N, C = (4, 4096, 256)
        H, D = (8, 32)
        EPS = 1e-06
        key = jax.random.key(seed)
        k1, k2, k3 = jax.random.split(key, 3)
        x = jax.random.normal(k1, (B, N, C), dtype=jnp.float32)
        W_qkv = jax.random.normal(k2, (3 * H * D, C), dtype=jnp.float32) * C ** (-0.5)
        W_proj = jax.random.normal(k3, (C, H * D), dtype=jnp.float32) * (H * D) ** (-0.5)
        b_proj = jnp.zeros((C,), dtype=jnp.float32)
        return {'x': x, 'W_qkv': W_qkv, 'W_proj': W_proj, 'b_proj': b_proj}
    _L1_attn_all = _L1_attn_setup()
    _L1_attn_in = {k: v for k, v in _L1_attn_all.items() if k in ('W_qkv', 'W_proj', 'b_proj')}
    del _L1_attn_all

    def _L1_ffn_setup():
        import jax, jax.numpy as jnp
        import numpy as np

        def _haar_dwt2(x):
            a = x[:, ::2, ::2]
            b = x[:, ::2, 1::2]
            c = x[:, 1::2, ::2]
            d = x[:, 1::2, 1::2]
            ll = (a + b + c + d) * 0.5
            lh = (a + b - c - d) * 0.5
            hl = (a - b + c - d) * 0.5
            hh = (a - b - c + d) * 0.5
            return (ll, lh, hl, hh)

        def _haar_idwt2(ll, lh, hl, hh):
            a = (ll + lh + hl + hh) * 0.5
            b = (ll + lh - hl - hh) * 0.5
            c = (ll - lh + hl - hh) * 0.5
            d = (ll - lh - hl + hh) * 0.5
            B, H2, W2 = ll.shape
            out = jnp.zeros((B, 2 * H2, 2 * W2), ll.dtype)
            out = out.at[:, ::2, ::2].set(a)
            out = out.at[:, ::2, 1::2].set(b)
            out = out.at[:, 1::2, ::2].set(c)
            out = out.at[:, 1::2, 1::2].set(d)
            return out

        def _interp_linear_last(x, m):
            n = x.shape[-1]
            pos = jnp.linspace(0.0, 1.0, m, dtype=x.dtype) * (n - 1)
            i0 = jnp.clip(jnp.floor(pos).astype(jnp.int32), 0, n - 2)
            w = pos - i0.astype(x.dtype)
            return x[..., i0] * (1.0 - w) + x[..., i0 + 1] * w
        key = jax.random.key(seed)
        k0, k1, k2 = jax.random.split(key, 3)
        b, f, c, hidden = (64, 128, 256, 1024)
        x = jax.random.normal(k0, (b, f, c), dtype=jnp.float32)
        fc1_w = jax.random.normal(k1, (hidden, c), dtype=jnp.float32) * 0.02
        fc1_b = jnp.zeros((hidden,), dtype=jnp.float32)
        fc2_w = jax.random.normal(k2, (c // 2, hidden), dtype=jnp.float32) * 0.02
        fc2_b = jnp.zeros((c // 2,), dtype=jnp.float32)
        return {'x': x, 'fc1_w': fc1_w, 'fc1_b': fc1_b, 'fc2_w': fc2_w, 'fc2_b': fc2_b}
    _L1_ffn_all = _L1_ffn_setup()
    _L1_ffn_in = {k: v for k, v in _L1_ffn_all.items() if k in ('fc1_w', 'fc1_b', 'fc2_w', 'fc2_b')}
    del _L1_ffn_all
    return {'x': x, 'L0_conv_W_u': _L0_conv_in['W_u'], 'L0_conv_b_u': _L0_conv_in['b_u'], 'L0_conv_W_v': _L0_conv_in['W_v'], 'L0_conv_b_v': _L0_conv_in['b_v'], 'L0_conv_W_o': _L0_conv_in['W_o'], 'L0_conv_b_o': _L0_conv_in['b_o'], 'L0_conv_rpe_in_w': _L0_conv_in['rpe_in_w'], 'L0_conv_rpe_in_b': _L0_conv_in['rpe_in_b'], 'L0_conv_rpe_h_w': _L0_conv_in['rpe_h_w'], 'L0_conv_rpe_h_b': _L0_conv_in['rpe_h_b'], 'L0_conv_rpe_out_w': _L0_conv_in['rpe_out_w'], 'L0_conv_rpe_out_b': _L0_conv_in['rpe_out_b'], 'L1_attn_W_qkv': _L1_attn_in['W_qkv'], 'L1_attn_W_proj': _L1_attn_in['W_proj'], 'L1_attn_b_proj': _L1_attn_in['b_proj'], 'L1_ffn_fc1_w': _L1_ffn_in['fc1_w'], 'L1_ffn_fc1_b': _L1_ffn_in['fc1_b'], 'L1_ffn_fc2_w': _L1_ffn_in['fc2_w'], 'L1_ffn_fc2_b': _L1_ffn_in['fc2_b']}

def reference(x, L0_conv_W_u, L0_conv_b_u, L0_conv_W_v, L0_conv_b_v, L0_conv_W_o, L0_conv_b_o, L0_conv_rpe_in_w, L0_conv_rpe_in_b, L0_conv_rpe_h_w, L0_conv_rpe_h_b, L0_conv_rpe_out_w, L0_conv_rpe_out_b, L1_attn_W_qkv, L1_attn_W_proj, L1_attn_b_proj, L1_ffn_fc1_w, L1_ffn_fc1_b, L1_ffn_fc2_w, L1_ffn_fc2_b):
    import jax
    import jax.numpy as jnp

    def _L0_conv_ref(x, W_u, b_u, W_v, b_v, W_o, b_o, rpe_in_w, rpe_in_b, rpe_h_w, rpe_h_b, rpe_out_w, rpe_out_b, H, W):
        import jax, jax.numpy as jnp
        import numpy as np
        EMBED_DIM = 256
        NUM_HEADS = 8
        EXPAND = 2
        D1 = EXPAND * EMBED_DIM
        HEAD_DIM = D1 // NUM_HEADS
        RPE_DIM = 256
        RPE_LAYERS = 3
        N = 56
        M = 56
        BATCH = 8
        EPS = 1e-08

        def simple_rms(x):
            d = x.shape[-1]
            norm = jnp.linalg.norm(x, axis=-1, keepdims=True)
            return x / (norm * d ** (-0.5) + EPS)
        _DP = np.arange(-(N - 1), N, dtype=np.float32)
        _DQ = np.arange(-(M - 1), M, dtype=np.float32)
        _COORDS = np.stack(np.meshgrid(_DP, _DQ, indexing='ij'), axis=-1)
        _RI = (np.arange(2 * N - 1) - (N - 1)) % (2 * N)
        _CI = (np.arange(2 * M - 1) - (M - 1)) % (2 * M)

        def rpe_coeffs(rpe_in_w, rpe_in_b, rpe_h_w, rpe_h_b, rpe_out_w, rpe_out_b):
            t = jnp.asarray(_COORDS) @ rpe_in_w.T + rpe_in_b
            for i in range(RPE_LAYERS):
                t = jax.nn.relu(simple_rms(t)) @ rpe_h_w[i].T + rpe_h_b[i]
            g = jax.nn.relu(simple_rms(t)) @ rpe_out_w.T + rpe_out_b
            g = g.reshape(2 * N - 1, 2 * M - 1, NUM_HEADS, HEAD_DIM)
            return g.transpose(2, 0, 1, 3)

        def tno2d(v, g):
            a = jnp.zeros((NUM_HEADS, 2 * N, 2 * M, HEAD_DIM), dtype=g.dtype)
            a = a.at[:, _RI[:, None], _CI[None, :], :].set(g)
            vf = jnp.fft.rfft2(v, s=(2 * N, 2 * M), axes=(2, 3))
            af = jnp.fft.rfft2(a, axes=(1, 2))
            y = jnp.fft.irfft2(vf * af[None], s=(2 * N, 2 * M), axes=(2, 3))
            return y[:, :, :N, :M, :]
        shortcut = x
        xn = simple_rms(x)
        u = jax.nn.silu(xn @ W_u.T + b_u)
        v = jax.nn.silu(xn @ W_v.T + b_v)
        b = v.shape[0]
        v = v.reshape(b, N, M, NUM_HEADS, HEAD_DIM).transpose(0, 3, 1, 2, 4)
        g = rpe_coeffs(rpe_in_w, rpe_in_b, rpe_h_w, rpe_h_b, rpe_out_w, rpe_out_b)
        y = tno2d(v, g)
        y = y.transpose(0, 2, 3, 1, 4).reshape(b, N, M, D1)
        out = u * y
        return out @ W_o.T + b_o + shortcut

    def _L1_attn_ref(x, W_qkv, W_proj, b_proj):
        import jax, jax.numpy as jnp
        import numpy as np
        B, N, C = (4, 4096, 256)
        H, D = (8, 32)
        EPS = 1e-06
        b, n, c = x.shape
        qkv = x @ W_qkv.T
        q, k, v = jnp.split(qkv, 3, axis=-1)
        to_heads = lambda t: t.reshape(b, n, H, D).transpose(0, 2, 1, 3)
        q, k, v = (to_heads(q), to_heads(k), to_heads(v))
        q = jax.nn.sigmoid(q)
        k = jax.nn.sigmoid(k)
        scale = D ** (-0.5)
        v = v / (scale * c // H)
        k_sum = k.sum(axis=2)
        q_sum = q.sum(axis=2)
        sink_incoming = 1.0 / (((q + EPS) * (k_sum + EPS)[:, :, None, :]).sum(-1) + EPS)
        source_outgoing = 1.0 / (((k + EPS) * (q_sum + EPS)[:, :, None, :]).sum(-1) + EPS)
        conserved_sink = ((q + EPS) * ((k * source_outgoing[..., None]).sum(2) + EPS)[:, :, None, :]).sum(-1) + EPS
        conserved_source = ((k + EPS) * ((q * sink_incoming[..., None]).sum(2) + EPS)[:, :, None, :]).sum(-1) + EPS
        conserved_source = jnp.clip(conserved_source, -1.0, 1.0)
        sink_allocation = jax.nn.sigmoid(conserved_sink * (float(q.shape[2]) / float(k.shape[2])))
        source_competition = jax.nn.softmax(conserved_source, axis=-1) * float(k.shape[2])
        kv = jnp.einsum('bhnd,bhne->bhde', k, v * source_competition[..., None])
        x_update = jnp.einsum('bhnd,bhde->bhne', q, kv) * sink_incoming[..., None] * sink_allocation[..., None]
        out = x_update.transpose(0, 2, 1, 3).reshape(b, n, H * D)
        return out @ W_proj.T + b_proj

    def _L1_ffn_ref(x, fc1_w, fc1_b, fc2_w, fc2_b):
        import jax, jax.numpy as jnp
        import numpy as np

        def _haar_dwt2(x):
            a = x[:, ::2, ::2]
            b = x[:, ::2, 1::2]
            c = x[:, 1::2, ::2]
            d = x[:, 1::2, 1::2]
            ll = (a + b + c + d) * 0.5
            lh = (a + b - c - d) * 0.5
            hl = (a - b + c - d) * 0.5
            hh = (a - b - c + d) * 0.5
            return (ll, lh, hl, hh)

        def _haar_idwt2(ll, lh, hl, hh):
            a = (ll + lh + hl + hh) * 0.5
            b = (ll + lh - hl - hh) * 0.5
            c = (ll - lh + hl - hh) * 0.5
            d = (ll - lh - hl + hh) * 0.5
            B, H2, W2 = ll.shape
            out = jnp.zeros((B, 2 * H2, 2 * W2), ll.dtype)
            out = out.at[:, ::2, ::2].set(a)
            out = out.at[:, ::2, 1::2].set(b)
            out = out.at[:, 1::2, ::2].set(c)
            out = out.at[:, 1::2, 1::2].set(d)
            return out

        def _interp_linear_last(x, m):
            n = x.shape[-1]
            pos = jnp.linspace(0.0, 1.0, m, dtype=x.dtype) * (n - 1)
            i0 = jnp.clip(jnp.floor(pos).astype(jnp.int32), 0, n - 2)
            w = pos - i0.astype(x.dtype)
            return x[..., i0] * (1.0 - w) + x[..., i0 + 1] * w
        b, f, c = x.shape
        ll, lh, hl, hh = _haar_dwt2(x)
        ll_up = _interp_linear_last(ll, c)
        h = jax.nn.gelu(jnp.einsum('bfc,hc->bfh', ll_up, fc1_w) + fc1_b, approximate=False)
        ll_new = jnp.einsum('bfh,oh->bfo', h, fc2_w) + fc2_b
        return _haar_idwt2(ll_new, lh, hl, hh)

    def _gn(v, G=32, eps=1e-05):
        B_, H_, W_, C_ = v.shape
        g = v.reshape(B_, H_, W_, G, C_ // G)
        m = jnp.mean(g, axis=(1, 2, 4), keepdims=True)
        s = jnp.var(g, axis=(1, 2, 4), keepdims=True)
        return ((g - m) / jnp.sqrt(s + eps)).reshape(v.shape)

    def _ln_c(v, eps=1e-06):
        m = jnp.mean(v, axis=-1, keepdims=True)
        s = jnp.var(v, axis=-1, keepdims=True)
        return (v - m) / jnp.sqrt(s + eps)

    def _ln_t(v, eps=1e-05):
        m = jnp.mean(v, axis=-1, keepdims=True)
        s = jnp.var(v, axis=-1, keepdims=True)
        return (v - m) / jnp.sqrt(s + eps)

    def _to_tokens(v):
        B_, H_, W_, C_ = v.shape
        return v.reshape(B_, H_ * W_, C_)

    def _from_tokens(t, like):
        return t.reshape(like.shape)
    x = x + _L0_conv_ref(_gn(x), L0_conv_W_u, L0_conv_b_u, L0_conv_W_v, L0_conv_b_v, L0_conv_W_o, L0_conv_b_o, L0_conv_rpe_in_w, L0_conv_rpe_in_b, L0_conv_rpe_h_w, L0_conv_rpe_h_b, L0_conv_rpe_out_w, L0_conv_rpe_out_b, 56, 56)
    t = _to_tokens(x)
    t = t + _L1_attn_ref(_ln_t(t), L1_attn_W_qkv, L1_attn_W_proj, L1_attn_b_proj)
    t = t + _L1_ffn_ref(_ln_t(t), L1_ffn_fc1_w, L1_ffn_fc1_b, L1_ffn_fc2_w, L1_ffn_fc2_b)
    x = _from_tokens(t, x)
    return x

_drawn_inputs = setup_inputs


def setup_inputs(seed=0):
    import zlib

    import numpy as np

    out = dict(_drawn_inputs(seed))
    spreads = {'L1_attn_b_proj': (0.0, 0.322), 'L1_ffn_fc1_b': (0.0, 0.8), 'L1_ffn_fc2_b': (0.0, 0.678)}
    factors = {'L0_conv_b_o': 8.0,
     'L1_attn_W_qkv': 8.0,
     'L1_attn_W_proj': 8.0,
     'L1_ffn_fc1_w': 5.866,
     'L1_ffn_fc2_w': 5.371}
    for name, (base, spread) in spreads.items():
        noise = np.random.default_rng([zlib.crc32(name.encode()), seed]).standard_normal(out[name].shape)
        drawn = base * np.exp(spread * noise) if base else spread * noise
        out[name] = jnp.asarray(drawn.astype(out[name].dtype))
    for name, factor in factors.items():
        out[name] = (out[name] * factor).astype(out[name].dtype)
    return out
```

```python
from contextlib import ExitStack

import numpy as np

import concourse.bass as bass
from concourse import mybir

F32 = mybir.dt.float32
ACT = mybir.ActivationFunctionType
ALU = mybir.AluOpType
AX = mybir.AxisListType

BATCH, SIDE, CH = 8, 56, 256
TOKENS = SIDE * SIDE
WIDE = 512
POINTS = 2 * SIDE
FREQ = SIDE + 1
ROWS = 2 * FREQ
TAPS = 2 * SIDE - 1
TAPS_PAD = 112
HALVES = CH // 128
CHUNK_ROWS = 8
CHUNK = CHUNK_ROWS * SIDE
CHUNKS = TOKENS // CHUNK
TILE = 2 * SIDE
TILES = CHUNK // TILE
RPE_ROWS = 4
RPE_CHUNK = RPE_ROWS * TAPS
RPE_LAYERS = 3
HEAD = 32
HIDDEN = 1024
V_SCALE = float((HEAD ** -0.5) * CH // 8)
RMS_EPS = 1e-08
GN_EPS = 1e-05
ATT_EPS = 1e-06
LN_EPS = 1e-05


def angles(a, b):
    return 2.0 * np.pi * ((np.outer(a, b) % POINTS) / POINTS)


def shape_constants():
    pos, freq, full = np.arange(SIDE), np.arange(FREQ), np.arange(POINTS)
    tap = np.arange(TAPS) - (SIDE - 1)
    c = {}
    w = angles(pos, freq)
    row = np.concatenate([np.cos(w), -np.sin(w)], 1)
    fwd = np.zeros((TILE, 2, ROWS))
    fwd[:SIDE, 0], fwd[SIDE:, 1] = row, row
    c["row_fwd"] = fwd
    w = angles(tap, freq)
    c["row_taps"] = np.concatenate([np.cos(w), -np.sin(w)], 1)
    w = angles(pos, full)
    c["col_fwd"] = np.stack([np.concatenate([np.cos(w), np.sin(w)], 0), np.concatenate([-np.sin(w), np.cos(w)], 0)], 1)
    w = angles(tap, full)
    c["col_taps"] = np.stack([np.cos(w), np.sin(w), -np.sin(w)], 1)
    w = angles(full, pos)
    c["col_inv"] = np.stack([np.concatenate([np.cos(w), np.sin(w)], 1), np.concatenate([-np.sin(w), np.cos(w)], 1)], 1) / POINTS
    w = angles(freq, pos)
    weight = np.where((freq == 0) | (freq == SIDE), 1.0, 2.0)[:, None] / POINTS
    edge = np.where((freq == 0) | (freq == SIDE), 0.0, 1.0)[:, None]
    c["row_inv"] = np.concatenate([weight * np.cos(w), -weight * edge * np.sin(w)], 0)
    c["ident"] = np.eye(128)
    c["ones"] = np.ones((128, 128))
    c["mean_ch"] = np.full((128, 128), 1.0 / CH)
    c["group_mean"] = np.kron(np.eye(16), np.full((8, 8), 1.0 / 8))
    c["same_head"] = np.kron(np.eye(128 // HEAD), np.ones((HEAD, HEAD)))
    p, q = np.meshgrid(np.arange(TAPS_PAD) - (SIDE - 1), tap, indexing="ij")
    c["coords"] = np.stack([p.ravel(), q.ravel()], 0)
    pair = np.kron(np.eye(CH // 2), np.ones((2, 1))) * 0.5
    c["pair_down"] = pair.reshape(HALVES, 128, 128).transpose(1, 0, 2)
    c["pair_up"] = pair.T
    c["pair_tok"] = np.kron(np.eye(SIDE), np.ones((2, 1)))
    at = np.linspace(0.0, 1.0, CH, dtype=np.float32) * np.float32(CH // 2 - 1)
    lo = np.clip(np.floor(at).astype(np.int32), 0, CH // 2 - 2)
    frac = at - lo.astype(np.float32)
    interp = np.zeros((CH, CH // 2), np.float32)
    interp[np.arange(CH), lo] += np.float32(1.0) - frac
    interp[np.arange(CH), lo + 1] += frac
    c["interp"] = interp.reshape(HALVES, 128, 128).transpose(1, 0, 2)
    return {k: np.ascontiguousarray(v, dtype=np.float32) for k, v in c.items()}


def rows_of_chunk(rows, g):
    return rows.rearrange("k b i c -> k (b i) c")[:, bass.ds(g * CHUNK_ROWS, CHUNK_ROWS), :]


class Tools:

    def __init__(self, nc, tag):
        self.nc, self.tag, self.phase, self.semaphores = nc, tag, ExitStack(), []

    def __enter__(self):
        return self

    def __exit__(self, kind, *a):
        if kind is None:
            self.phase.close()
            self.nc.clear_and_free_semaphores(self.semaphores)
            self.nc.all_engine_barrier()

    def sb(self, name, shape):
        return self.phase.enter_context(self.nc.sbuf_tensor(f"{self.tag}_{name}", shape, F32))

    def ps(self, name, shape):
        return self.phase.enter_context(self.nc.psum_tensor(f"{self.tag}_{name}_ps", shape, F32))

    def sem(self, name):
        self.semaphores.append(self.nc.alloc_semaphore(name=f"{self.tag}_{name}"))
        return self.semaphores[-1]


def kernel_rows_phase(nc, d):
    with Tools(nc, "kr") as T:
        w_in = T.sb("w_in", [2, CH])
        w_h = T.sb("w_h", [128, RPE_LAYERS, HALVES, CH])
        w_out = T.sb("w_out", [128, HALVES, WIDE])
        bias = T.sb("bias", [128, RPE_LAYERS + 1, HALVES])
        out_bias = T.sb("out_bias", [TAPS, WIDE])
        row_taps = T.sb("row_taps", [TAPS, ROWS])
        mean_ch = T.sb("mean_ch", [128, 128])
        coords = T.sb("coords", [2, TAPS_PAD * TAPS])
        square = [T.sb(f"square{u}", [128, HALVES, RPE_CHUNK]) for u in range(2)]
        rect = [T.sb(f"rect{u}", [128, HALVES, RPE_CHUNK]) for u in range(2)]
        act_in = [T.sb(f"act_in{u}", [128, HALVES, RPE_CHUNK]) for u in range(2)]
        root = [T.sb(f"root{u}", [128, RPE_CHUNK]) for u in range(2)]
        guarded = [T.sb(f"guarded{u}", [128, RPE_CHUNK]) for u in range(2)]
        inv = [T.sb(f"inv{u}", [128, RPE_CHUNK]) for u in range(2)]
        coef = [T.sb(f"coef{i}", [TAPS, WIDE]) for i in range(2)]
        rows_out = [T.sb(f"rows_out{u}", [ROWS, RPE_ROWS, WIDE]) for u in range(2)]
        t_ps = [[T.ps(f"t{u}{h}", [128, 512]) for h in range(2)] for u in range(2)]
        ms_ps = [T.ps(f"ms{u}", [128, 512]) for u in range(2)]
        row_ps = [T.ps(f"row{i}", [128, 512]) for i in range(2)]

        consts_in, squared, rectified, rooted, eps_added, inverted, normed = (
            T.sem(n) for n in ("consts_in", "squared", "rectified", "rooted", "eps_added", "inverted", "normed"))
        layer_done, mean_done, coef_mm, coef_done, row_mm, row_out = (
            T.sem(n) for n in ("layer_done", "mean_done", "coef_mm", "coef_done", "row_mm", "row_out"))
        stored = [T.sem(f"stored{u}") for u in range(2)]
        STEPS = TAPS_PAD // RPE_ROWS // 2
        LAYERS = RPE_LAYERS + 1
        PER, TAIL = 2 * LAYERS, 2 * RPE_ROWS
        loads = [(w_in, "rpe_in"), (w_h, "rpe_h"), (w_out, "rpe_out"), (bias, "rpe_bias"), (out_bias, "rpe_out_b"),
                 (row_taps, "row_taps"), (mean_ch, "mean_ch"), (coords, "coords")]
        with nc.Block() as block:
            @block.sync
            def _(sp):
                for tile, name in loads:
                    sp.dma_start(tile[:], d[name]).then_inc(consts_in, 16)
                with sp.Fori(0, STEPS) as s:
                    for u in range(2):
                        sp.wait_ge(row_out, s * TAIL + RPE_ROWS * (u + 1))
                        sp.dma_start(d["kern_rows"][:, bass.ds((s * 2 + u) * RPE_ROWS, RPE_ROWS), :],
                                     rows_out[u][:]).then_inc(stored[u], 16)
                for u in range(2):
                    sp.wait_ge(stored[u], 16 * STEPS)

            @block.tensor
            def _(pe):
                pe.wait_ge(consts_in, 16 * len(loads))
                with pe.Fori(0, STEPS) as s:
                    for layer in range(LAYERS):
                        for u in range(2):
                            n = 2 * layer + u
                            if layer:
                                pe.wait_ge(normed, s * PER + n - 1)
                            else:
                                pe.wait_ge(coef_done, s * TAIL)
                            for h in range(HALVES):
                                if layer == 0:
                                    last = nc.tensor.matmul(t_ps[u][h][:, :RPE_CHUNK], w_in[:, h * 128:(h + 1) * 128],
                                                            coords[:, bass.ds((s * 2 + u) * RPE_CHUNK, RPE_CHUNK)],
                                                            start=True, stop=True)
                                else:
                                    for k in range(HALVES):
                                        last = nc.tensor.matmul(t_ps[u][h][:, :RPE_CHUNK],
                                                                w_h[:, layer - 1, k, h * 128:(h + 1) * 128],
                                                                act_in[u][:, k, :], start=k == 0, stop=k == HALVES - 1)
                            last.then_inc(layer_done, 1)
                        for u in range(2):
                            pe.wait_ge(squared, s * PER + 2 * layer + u + 1)
                            pe.wait_ge(rooted, s * PER + max(2 * layer + u - 1, 0))
                            for h in range(HALVES):
                                last = nc.tensor.matmul(ms_ps[u][:, :RPE_CHUNK], mean_ch[:], square[u][:, h, :],
                                                        start=h == 0, stop=h == HALVES - 1)
                            last.then_inc(mean_done, 1)

                    def row_pass(m):
                        pe.wait_ge(coef_done, s * TAIL + m + 1)
                        if m >= 2:
                            pe.wait_ge(row_out, s * TAIL + m - 1)
                        else:
                            pe.wait_ge(row_out, s * TAIL)
                        nc.tensor.matmul(row_ps[m % 2][:ROWS, :], row_taps[:], coef[m % 2][:],
                                         start=True, stop=True).then_inc(row_mm, 1)

                    for u in range(2):
                        pe.wait_ge(normed, s * PER + PER - 1 + u)
                        for r in range(RPE_ROWS):
                            m = RPE_ROWS * u + r
                            if r >= 2:
                                pe.wait_ge(coef_done, s * TAIL + m - 1)
                            for k in range(HALVES):
                                last = nc.tensor.matmul(t_ps[u][r % 2][:TAPS, :], act_in[u][:, k, r * TAPS:(r + 1) * TAPS],
                                                        w_out[:, k, :], start=k == 0, stop=k == HALVES - 1)
                            last.then_inc(coef_mm, 1)
                            if m:
                                row_pass(m - 1)
                    row_pass(TAIL - 1)

            @block.scalar
            def _(act):
                act.wait_ge(consts_in, 16 * len(loads))
                with act.Fori(0, STEPS) as s:
                    for layer in range(LAYERS):
                        for u in range(2):
                            n = 2 * layer + u
                            act.wait_ge(layer_done, s * PER + n + 1)
                            act.wait_ge(mean_done, s * PER + max(n - 1, 0))
                            for h in range(HALVES):
                                last = nc.scalar.activation(square[u][:, h, :], t_ps[u][h][:, :RPE_CHUNK], ACT.Square,
                                                            bias=bias[:, layer, h:h + 1])
                            last.then_inc(squared, 1)
                        for u in range(2):
                            n = 2 * layer + u
                            act.wait_ge(mean_done, s * PER + n + 1)
                            act.wait_ge(eps_added, s * PER + max(n - 1, 0))
                            nc.scalar.activation(root[u][:], ms_ps[u][:, :RPE_CHUNK], ACT.Sqrt).then_inc(rooted, 1)
                    for m in range(TAIL):
                        u, r = divmod(m, RPE_ROWS)
                        act.wait_ge(row_mm, s * TAIL + m + 1)
                        if r == 0:
                            act.wait_ge(stored[u], s * 16)
                        nc.scalar.activation(rows_out[u][:, r, :], row_ps[m % 2][:ROWS, :], ACT.Copy).then_inc(row_out, 1)

            @block.vector
            def _(dve):
                dve.wait_ge(consts_in, 16 * len(loads))
                with dve.Fori(0, STEPS) as s:
                    for layer in range(LAYERS):
                        for u in range(2):
                            n = 2 * layer + u
                            dve.wait_ge(squared, s * PER + n + 1)
                            for h in range(HALVES):
                                last = nc.vector.tensor_scalar(rect[u][:, h, :], t_ps[u][h][:, :RPE_CHUNK],
                                                               bias[:, layer, h:h + 1], 0.0, ALU.add, ALU.max)
                            last.then_inc(rectified, 1)
                        for u in range(2):
                            n = 2 * layer + u
                            dve.wait_ge(rooted, s * PER + n + 1)
                            nc.vector.tensor_scalar(guarded[u][:], root[u][:], RMS_EPS, None, ALU.add).then_inc(eps_added, 1)
                            dve.wait_ge(eps_added, s * PER + n + 1)
                            nc.vector.reciprocal(inv[u][:], guarded[u][:]).then_inc(inverted, 1)
                            dve.wait_ge(inverted, s * PER + n + 1)
                            dve.wait_ge(rectified, s * PER + n + 1)
                            for h in range(HALVES):
                                last = nc.vector.tensor_tensor(act_in[u][:, h, :], rect[u][:, h, :], inv[u][:], ALU.mult)
                            last.then_inc(normed, 1)
                    for m in range(TAIL):
                        u, r = divmod(m, RPE_ROWS)
                        dve.wait_ge(coef_mm, s * TAIL + m + 1)
                        dve.wait_ge(row_mm, s * TAIL + max(m - 1, 0))
                        nc.vector.tensor_tensor(coef[m % 2][:], t_ps[u][r % 2][:TAPS, :], out_bias[:],
                                                ALU.add).then_inc(coef_done, 1)


def columns_phase(nc, d):
    with Tools(nc, "co") as T:
        col_fwd = T.sb("col_fwd", [2 * SIDE, 2, POINTS])
        col_taps = T.sb("col_taps", [TAPS, 3, POINTS])
        col_inv = T.sb("col_inv", [POINTS, 2, 2 * SIDE])
        taps_in = T.sb("taps_in", [TAPS, 2, WIDE])
        v_in = T.sb("v_in", [2 * SIDE, BATCH, WIDE])
        y_out = T.sb("y_out", [2 * SIDE, BATCH, WIDE])
        spec = [T.sb(f"spec{i}", [POINTS, 3 * WIDE]) for i in range(2)]
        direct = [T.sb(f"direct{i}", [POINTS, 2 * WIDE]) for i in range(2)]
        cross = [T.sb(f"cross{i}", [POINTS, 2 * WIDE]) for i in range(2)]
        prod = [T.sb(f"prod{i}", [POINTS, 2 * WIDE]) for i in range(2)]
        v_ps = [T.ps(f"v{i}", [128, 2 * WIDE]) for i in range(2)]
        taps_ps = T.ps("taps", [128, 2 * WIDE])
        y_ps = [T.ps(f"y{i}", [128, WIDE]) for i in range(2)]
        names = ("consts_in", "taps_loaded", "taps_mm", "spec_ready", "fwd_mm", "multiplied", "combined", "inv_mm", "y_ready")
        consts_in, taps_loaded, taps_mm, spec_ready, fwd_mm, multiplied, combined, inv_mm, y_ready = (T.sem(n) for n in names)
        PAIRS = BATCH // 2
        LAG = 2
        v_loaded = [T.sem(f"v_loaded{i}") for i in range(PAIRS)]
        y_stored = [T.sem(f"y_stored{i}") for i in range(PAIRS)]
        loads = [(col_fwd, "col_fwd"), (col_taps, "col_taps"), (col_inv, "col_inv")]

        def load_taps(eng, k):
            for part in range(2):
                eng.dma_start(taps_in[:, part, :], d["kern_rows"][k + FREQ * part, 0:TAPS, :]).then_inc(taps_loaded, 16)

        def load_v(eng, k, pair):
            for part in range(2):
                eng.dma_start(v_in[part * SIDE:(part + 1) * SIDE, 2 * pair:2 * pair + 2, :],
                              d["v_rows"][k + FREQ * part, 2 * pair:2 * pair + 2, :, :].rearrange("b i c -> i b c")
                              ).then_inc(v_loaded[pair], 16)

        def store_y(eng, k, pair):
            for part in range(2):
                eng.dma_start(d["y_rows"][k + FREQ * part, 2 * pair:2 * pair + 2, :, :].rearrange("b i c -> i b c"),
                              y_out[part * SIDE:(part + 1) * SIDE, 2 * pair:2 * pair + 2, :]).then_inc(y_stored[pair], 16)

        with nc.Block() as block:
            @block.sync
            def _(sp):
                for tile, name in loads:
                    sp.dma_start(tile[:], d[name]).then_inc(consts_in, 16)
                load_taps(sp, 0)
                for pair in range(PAIRS):
                    load_v(sp, 0, pair)

                def step(k, more):
                    if more:
                        sp.wait_ge(taps_mm, k + 1)
                        load_taps(sp, k + 1)
                    for pair in range(PAIRS):
                        if more:
                            sp.wait_ge(fwd_mm, k * BATCH + 2 * pair + 2)
                            load_v(sp, k + 1, pair)
                        sp.wait_ge(y_ready, k * BATCH + 2 * pair + 2)
                        store_y(sp, k, pair)

                with sp.Fori(0, FREQ // 2) as s:
                    for i in range(2):
                        step(s * 2 + i, True)
                step(FREQ - 1, False)
                for pair in range(PAIRS):
                    sp.wait_ge(y_stored[pair], 32 * FREQ)

            @block.tensor
            def _(pe):
                pe.wait_ge(consts_in, 16 * len(loads))

                def spectrum(k):
                    pe.wait_ge(taps_loaded, k * 32 + 32)
                    pe.wait_ge(spec_ready, k)
                    for out, (real, imag) in enumerate(((0, 1), (2, 0))):
                        nc.tensor.matmul(taps_ps[:POINTS, bass.ts(out, WIDE)], col_taps[:, real, :], taps_in[:, 0, :],
                                         start=True, stop=False)
                        last = nc.tensor.matmul(taps_ps[:POINTS, bass.ts(out, WIDE)], col_taps[:, imag, :], taps_in[:, 1, :],
                                                start=False, stop=True)
                    last.then_inc(taps_mm, 1)

                def inverse(k, b):
                    n = k * BATCH + b
                    pe.wait_ge(combined, n + 1)
                    if b >= 2:
                        pe.wait_ge(y_ready, n - 1)
                    else:
                        pe.wait_ge(y_ready, k * BATCH)
                    nc.tensor.matmul(y_ps[b % 2][:2 * SIDE, :], col_inv[:, 0, :], prod[b % 2][:, :WIDE], start=True, stop=False)
                    nc.tensor.matmul(y_ps[b % 2][:2 * SIDE, :], col_inv[:, 1, :], prod[b % 2][:, WIDE:],
                                     start=False, stop=True).then_inc(inv_mm, 1)

                def step(k, more):
                    for b in range(BATCH):
                        if b == BATCH // 2 and more:
                            spectrum(k + 1)
                        if b % 2 == 0:
                            pe.wait_ge(v_loaded[b // 2], k * 32 + 32)
                        pe.wait_ge(multiplied, k * BATCH + max(b - 1, 0))
                        for out in range(2):
                            last = nc.tensor.matmul(v_ps[b % 2][:POINTS, bass.ts(out, WIDE)], col_fwd[:, out, :], v_in[:, b, :],
                                                    start=True, stop=True)
                        last.then_inc(fwd_mm, 1)
                        if b >= LAG:
                            inverse(k, b - LAG)
                    for b in range(BATCH - LAG, BATCH):
                        inverse(k, b)

                spectrum(0)
                with pe.Fori(0, FREQ // 2) as s:
                    for i in range(2):
                        step(s * 2 + i, True)
                step(FREQ - 1, False)

            @block.scalar
            def _(act):
                def spectrum(k, i):
                    act.wait_ge(taps_mm, k + 1)
                    for col, part in ((0, 0), (1, 1), (2, 0)):
                        last = nc.scalar.activation(spec[i][:, bass.ts(col, WIDE)], taps_ps[:POINTS, bass.ts(part, WIDE)], ACT.Copy)
                    last.then_inc(spec_ready, 1)

                def step(k, i, more):
                    for b in range(BATCH):
                        if b == BATCH // 2 and more:
                            spectrum(k + 1, 1 - i)
                        act.wait_ge(inv_mm, k * BATCH + b + 1)
                        if b % 2 == 0:
                            act.wait_ge(y_stored[b // 2], k * 32)
                        nc.scalar.activation(y_out[:, b, :], y_ps[b % 2][:2 * SIDE, :], ACT.Copy).then_inc(y_ready, 1)

                spectrum(0, 0)
                with act.Fori(0, FREQ // 2) as s:
                    for i in range(2):
                        step(s * 2 + i, i, True)
                step(FREQ - 1, 0, False)

            @block.vector
            def _(dve):
                def step(k, i):
                    dve.wait_ge(spec_ready, k + 1)
                    for b in range(BATCH):
                        dve.wait_ge(fwd_mm, k * BATCH + b + 1)
                        dve.wait_ge(combined, k * BATCH + max(b - 1, 0))
                        nc.vector.tensor_tensor(direct[b % 2][:], v_ps[b % 2][:POINTS, :], spec[i][:, :2 * WIDE], ALU.mult)
                        nc.vector.tensor_tensor(cross[b % 2][:], v_ps[b % 2][:POINTS, :], spec[i][:, WIDE:],
                                                ALU.mult).then_inc(multiplied, 1)

                with dve.Fori(0, FREQ // 2) as s:
                    for i in range(2):
                        step(s * 2 + i, i)
                step(FREQ - 1, 0)

            @block.gpsimd
            def _(pool):
                def step(k):
                    for b in range(BATCH):
                        pool.wait_ge(multiplied, k * BATCH + b + 1)
                        pool.wait_ge(inv_mm, k * BATCH + max(b - 1, 0))
                        nc.gpsimd.tensor_tensor(prod[b % 2][:, :WIDE], direct[b % 2][:, :WIDE], direct[b % 2][:, WIDE:], ALU.subtract)
                        nc.gpsimd.tensor_tensor(prod[b % 2][:, WIDE:], cross[b % 2][:, :WIDE], cross[b % 2][:, WIDE:],
                                                ALU.add).then_inc(combined, 1)

                with pool.Fori(0, FREQ // 2) as s:
                    for i in range(2):
                        step(s * 2 + i)
                step(FREQ - 1)


def stats_phase(nc, d):
    with Tools(nc, "st") as T:
        ident, group_mean = T.sb("ident", [128, 128]), T.sb("group_mean", [128, 128])
        x_in = [T.sb(f"x_in{i}", [TILE, TILES, CH]) for i in range(CHUNKS)]
        stats = T.sb("stats", [128, HALVES, CHUNKS, 6])
        moments = T.sb("moments", [128, HALVES, 2])
        off, off2 = T.sb("off", [128, HALVES]), T.sb("off2", [128, HALVES])
        var, root, scale, shift = (T.sb(n, [128, HALVES]) for n in ("var", "root", "scale", "shift"))
        rows = T.sb("rows", [128, 2 * CH])
        x_ps = [[T.ps(f"x{i}{h}", [128, 512]) for h in range(2)] for i in range(2)]
        group_ps, row_ps = T.ps("group", [128, 512]), T.ps("row", [128, 512])
        consts_in, transposed, measured, chain, group_mm, rooted, row_mm, rows_made, rows_stored = (
            T.sem(n) for n in ("consts_in", "transposed", "measured", "chain", "group_mm", "rooted", "row_mm",
                               "rows_made", "rows_stored"))
        seen = T.sem("seen")
        x_loaded = [T.sem(f"x_loaded{i}") for i in range(CHUNKS)]
        LINKS = 8

        with nc.Block() as block:
            @block.sync
            def _(sp):
                sp.dma_start(ident[:], d["ident"]).then_inc(consts_in, 16)
                sp.dma_start(group_mean[:], d["group_mean"]).then_inc(consts_in, 16)
                for j in range(CHUNKS):
                    sp.dma_start(x_in[j][:], d["x_tiles"][j]).then_inc(x_loaded[j], 16)
                with sp.Fori(1, BATCH) as b:
                    for j in range(CHUNKS):
                        sp.wait_ge(transposed, (b - 1) * CHUNKS + j + 1)
                        sp.dma_start(x_in[j][:], d["x_tiles"][b * CHUNKS + j]).then_inc(x_loaded[j], 16)

            @block.tensor
            def _(pe):
                pe.wait_ge(consts_in, 32)
                with pe.Fori(0, BATCH) as b:
                    for j in range(CHUNKS):
                        pe.wait_ge(x_loaded[j], b * 16 + 16)
                        pe.wait_ge(measured, b * CHUNKS + max(j - 1, 0))
                        for t in range(TILES):
                            for h in range(HALVES):
                                last = nc.tensor.transpose(x_ps[j % 2][h][:, t * TILE:(t + 1) * TILE],
                                                           x_in[j][:, t, h * 128:(h + 1) * 128], ident[:TILE, :TILE])
                        last.then_inc(transposed, 1)
                    pe.wait_ge(chain, b * LINKS + 1)
                    nc.tensor.matmul(group_ps[:, 0:4], group_mean[:], moments[:].rearrange("p h m -> p (h m)"),
                                     start=True, stop=True).then_inc(group_mm, 1)
                    pe.wait_ge(chain, b * LINKS + 3)
                    nc.tensor.matmul(group_ps[:, 4:6], group_mean[:], off2[:], start=True, stop=True).then_inc(group_mm, 1)
                    pe.wait_ge(chain, b * LINKS + 8)
                    for i, col in enumerate((scale, shift)):
                        for h in range(HALVES):
                            at = (i * HALVES + h) * 128
                            last = nc.tensor.matmul(row_ps[:, at:at + 128], col[:, h:h + 1].to_broadcast([128, 128]), ident[:],
                                                    start=True, stop=True)
                    last.then_inc(row_mm, 1)

            @block.scalar
            def _(act):
                with act.Fori(0, BATCH) as b:
                    act.wait_ge(chain, b * LINKS + 5)
                    nc.scalar.activation(root[:], var[:], ACT.Sqrt).then_inc(rooted, 1)
                    act.wait_ge(rows_made, b + 1)
                    for j in range(CHUNKS):
                        act.dma_start(d["gn_rows"][b * CHUNKS + j], rows[0:1, :]).then_inc(rows_stored, 16)
                act.wait_ge(rows_stored, 16 * BATCH * CHUNKS)

            @block.vector
            def _(dve):
                with dve.Fori(0, BATCH) as b:
                    for j in range(CHUNKS):
                        dve.wait_ge(transposed, b * CHUNKS + j + 1)
                        for h in range(HALVES):
                            last = nc.vector.bn_stats(stats[:, h, j, :], x_ps[j % 2][h][:, :CHUNK])
                        last.then_inc(measured, 1)
                    dve.wait_ge(measured, b * CHUNKS + CHUNKS)
                    dve.sem_inc(seen, 1)
                    nc.vector.bn_aggr(moments[:, 0, :], stats[:, 0, :, :])
                    nc.vector.bn_aggr(moments[:, 1, :], stats[:, 1, :, :]).then_inc(chain, 1)
                    group = group_ps[:, 0:4].rearrange("p (h m) -> p h m", m=2)
                    dve.wait_ge(group_mm, b * 2 + 1)
                    nc.vector.tensor_tensor(off[:], moments[:, :, 0], group[:, :, 0], ALU.subtract).then_inc(chain, 1)
                    dve.wait_ge(chain, b * LINKS + 2)
                    nc.vector.tensor_tensor(off2[:], off[:], off[:], ALU.mult).then_inc(chain, 1)
                    dve.wait_ge(group_mm, b * 2 + 2)
                    nc.vector.tensor_scalar(var[:], group_ps[:, 4:6], GN_EPS, None, ALU.add).then_inc(chain, 1)
                    dve.wait_ge(chain, b * LINKS + 4)
                    nc.vector.tensor_tensor(var[:], var[:], group[:, :, 1], ALU.add).then_inc(chain, 1)
                    dve.wait_ge(rooted, b + 1)
                    nc.vector.reciprocal(scale[:], root[:]).then_inc(chain, 1)
                    dve.wait_ge(chain, b * LINKS + 6)
                    nc.vector.tensor_tensor(shift[:], scale[:], group[:, :, 0], ALU.mult).then_inc(chain, 1)
                    dve.wait_ge(chain, b * LINKS + 7)
                    nc.vector.tensor_scalar(shift[:], shift[:], -1.0, None, ALU.mult).then_inc(chain, 1)
                    dve.wait_ge(row_mm, b + 1)
                    dve.wait_ge(rows_stored, b * 16 * CHUNKS)
                    nc.vector.tensor_copy(rows[:], row_ps[:, :2 * CH]).then_inc(rows_made, 1)


def project_phase(nc, d):
    with Tools(nc, "pr") as T:
        w_v = T.sb("w_v", [128, HALVES, WIDE])
        v_bias = T.sb("v_bias", [TILE, WIDE])
        ident = T.sb("ident", [128, 128])
        row_fwd = T.sb("row_fwd", [TILE, 2, ROWS])
        x_in = [T.sb(f"x_in{u}", [TILE, TILES, CH]) for u in range(2)]
        gn = [T.sb(f"gn{u}", [TILE, 2, CH]) for u in range(2)]
        gx = [T.sb(f"gx{u}", [TILE, TILES, CH]) for u in range(2)]
        xn = [T.sb(f"xn{u}", [TILE, TILES, CH]) for u in range(2)]
        junk = T.sb("junk", [TILE, TILES, CH])
        ssum, root, guarded, inv = ([T.sb(f"{n}{u}", [TILE, TILES]) for u in range(2)] for n in ("ssum", "root", "guarded", "inv"))
        xn_t = [T.sb(f"xn_t{u}", [128, HALVES, CHUNK]) for u in range(2)]
        v_pre = [T.sb(f"v_pre{i}", [TILE, WIDE]) for i in range(2)]
        v = [T.sb(f"v{i}", [TILE, WIDE]) for i in range(2)]
        rows_out = [T.sb(f"rows_out{u}", [ROWS, CHUNK_ROWS, WIDE]) for u in range(2)]
        xt_ps = [T.ps(f"xt{h}", [128, 512]) for h in range(2)]
        v_ps = [T.ps(f"v{i}", [128, 512]) for i in range(2)]
        row_ps = [[T.ps(f"row{i}{r}", [128, 512]) for r in range(2)] for i in range(2)]
        (consts_in, scaled, gx_ready, squared, rooted, eps_added, inverted, xn_ready, xt_mm, xt0_ready, xt1_ready, v_mm, biased,
         v_ready, row_mm, row0_out, row1_out) = (T.sem(n) for n in (
             "consts_in", "scaled", "gx_ready", "squared", "rooted", "eps_added", "inverted", "xn_ready", "xt_mm", "xt0_ready",
             "xt1_ready", "v_mm", "biased", "v_ready", "row_mm", "row0_out", "row1_out"))
        loaded = [T.sem(f"loaded{u}") for u in range(2)]
        xn_stored = [T.sem(f"xn_stored{u}") for u in range(2)]
        rows_stored = [T.sem(f"rows_stored{u}") for u in range(2)]
        ALL = BATCH * CHUNKS
        loads = [(w_v, "w_v"), (v_bias, "v_bias"), (ident, "ident"), (row_fwd, "row_fwd")]

        def following(s, u):
            return (s, 1) if u == 0 else (s + 1, 0)

        def all_steps(eng, front, step):
            front(0, 0)
            with eng.Fori(0, ALL // 2 - 1) as s:
                for u in range(2):
                    step(s, u, following(s, u))
            step(ALL // 2 - 1, 0, (ALL // 2 - 1, 1))
            step(ALL // 2 - 1, 1, None)

        with nc.Block() as block:
            @block.sync
            def _(sp):
                for tile, name in loads:
                    sp.dma_start(tile[:], d[name]).then_inc(consts_in, 16)
                with sp.Fori(0, ALL // 2) as s:
                    for u in range(2):
                        g = s * 2 + u
                        sp.wait_ge(gx_ready, s * 2)
                        sp.dma_start(x_in[u][:], d["x_tiles"][g]).then_inc(loaded[u], 16)
                        sp.dma_start(gn[u][:].rearrange("p a c -> p (a c)"), d["gn_rows"][g].to_broadcast([TILE, 2 * CH])
                                     ).then_inc(loaded[u], 16)

            @block.gpsimd
            def _(pool):
                with pool.Fori(0, ALL // 2) as s:
                    for u in range(2):
                        g = s * 2 + u
                        pool.wait_ge(xt0_ready, g + 1)
                        pool.wait_ge(xt1_ready, g + 1)
                        pool.dma_start(d["xn_t"][g], xn_t[u][:]).then_inc(xn_stored[u], 16)
                        pool.wait_ge(row0_out, (g + 1) * TILES)
                        pool.wait_ge(row1_out, (g + 1) * TILES)
                        pool.dma_start(rows_of_chunk(d["v_rows"], g), rows_out[u][:]).then_inc(rows_stored[u], 16)
                for u in range(2):
                    pool.wait_ge(xn_stored[u], 16 * (ALL // 2))
                    pool.wait_ge(rows_stored[u], 16 * (ALL // 2))

            @block.tensor
            def _(pe):
                pe.wait_ge(consts_in, 16 * len(loads))

                def front(s, u):
                    g = 2 * s + u
                    pe.wait_ge(xn_ready, g + 1)
                    pe.wait_ge(xt0_ready, g)
                    pe.wait_ge(xt1_ready, g)
                    for h in range(HALVES):
                        for t in range(TILES):
                            last = nc.tensor.transpose(xt_ps[h][:, t * TILE:(t + 1) * TILE], xn[u][:, t, h * 128:(h + 1) * 128],
                                                       ident[:TILE, :TILE])
                    last.then_inc(xt_mm, 1)

                def step(s, u, after):
                    g = 2 * s + u

                    def row_pass(t):
                        pe.wait_ge(v_ready, g * TILES + t + 1)
                        pe.wait_ge(row0_out, g * TILES + max(t - 1, 0))
                        pe.wait_ge(row1_out, g * TILES + max(t - 1, 0))
                        for r in range(2):
                            last = nc.tensor.matmul(row_ps[t % 2][r][:ROWS, :], row_fwd[:, r, :], v[t % 2][:], start=True, stop=True)
                        last.then_inc(row_mm, 1)

                    pe.wait_ge(xt0_ready, g + 1)
                    pe.wait_ge(xt1_ready, g + 1)
                    for t in range(TILES):
                        pe.wait_ge(biased, g * TILES + max(t - 1, 0))
                        for h in range(HALVES):
                            last = nc.tensor.matmul(v_ps[t % 2][:TILE, :], xn_t[u][:, h, t * TILE:(t + 1) * TILE], w_v[:, h, :],
                                                    start=h == 0, stop=h == HALVES - 1)
                        last.then_inc(v_mm, 1)
                        if t:
                            row_pass(t - 1)
                    if after:
                        front(*after)
                    row_pass(TILES - 1)

                all_steps(pe, front, step)

            @block.scalar
            def _(act):
                act.wait_ge(consts_in, 16 * len(loads))

                def squares(s, u):
                    g = 2 * s + u
                    act.wait_ge(gx_ready, g + 1)
                    act.wait_ge(rooted, 2 * s)
                    for t in range(TILES):
                        last = nc.scalar.activation(junk[:, t, :], gx[u][:, t, :], ACT.Square, accum_out=ssum[u][:, t:t + 1])
                    last.then_inc(squared, 1)
                    act.wait_ge(squared, g + 1)
                    nc.scalar.activation(root[u][:], ssum[u][:], ACT.Sqrt, scale=1.0 / CH).then_inc(rooted, 1)

                def scale_rows(s, u):
                    g = 2 * s + u
                    act.wait_ge(inverted, g + 1)
                    act.wait_ge(xt_mm, g)
                    for t in range(TILES):
                        last = nc.scalar.activation(xn[u][:, t, :], gx[u][:, t, :], ACT.Copy, scale=inv[u][:, t:t + 1])
                    last.then_inc(xn_ready, 1)

                def take_xt(s, u):
                    g = 2 * s + u
                    act.wait_ge(xt_mm, g + 1)
                    act.wait_ge(xn_stored[u], s * 16)
                    act.wait_ge(v_mm, g * TILES)
                    nc.scalar.activation(xn_t[u][:, 0, :], xt_ps[0][:, :CHUNK], ACT.Copy).then_inc(xt0_ready, 1)

                def front(s, u):
                    squares(s, u)
                    scale_rows(s, u)
                    take_xt(s, u)

                def step(s, u, after):
                    g = 2 * s + u

                    def take_row(t):
                        act.wait_ge(row_mm, g * TILES + t + 1)
                        if t == 0:
                            act.wait_ge(rows_stored[u], s * 16)
                        nc.scalar.activation(rows_out[u][:, 2 * t, :], row_ps[t % 2][0][:ROWS, :], ACT.Copy).then_inc(row0_out, 1)

                    for t in range(TILES):
                        act.wait_ge(biased, g * TILES + t + 1)
                        act.wait_ge(row_mm, g * TILES + max(t - 1, 0))
                        nc.scalar.activation(v[t % 2][:], v_pre[t % 2][:], ACT.Silu).then_inc(v_ready, 1)
                        if t == 1 and after:
                            squares(*after)
                        if t:
                            take_row(t - 1)
                        if t == 2 and after:
                            scale_rows(*after)
                    if after:
                        take_xt(*after)
                    take_row(TILES - 1)

                all_steps(act, front, step)

            @block.vector
            def _(dve):
                dve.wait_ge(consts_in, 16 * len(loads))

                def normalise(s, u):
                    g = 2 * s + u
                    dve.wait_ge(loaded[u], s * 32 + 32)
                    dve.wait_ge(xn_ready, 2 * s)
                    nc.vector.tensor_tensor(gx[u][:], x_in[u][:], gn[u][:, 0:1, :].to_broadcast([TILE, TILES, CH]),
                                            ALU.mult).then_inc(scaled, 1)
                    dve.wait_ge(scaled, g + 1)
                    nc.vector.tensor_tensor(gx[u][:], gx[u][:], gn[u][:, 1:2, :].to_broadcast([TILE, TILES, CH]),
                                            ALU.add).then_inc(gx_ready, 1)

                def invert(s, u):
                    g = 2 * s + u
                    dve.wait_ge(rooted, g + 1)
                    nc.vector.tensor_scalar(guarded[u][:], root[u][:], RMS_EPS, None, ALU.add).then_inc(eps_added, 1)
                    dve.wait_ge(eps_added, g + 1)
                    nc.vector.reciprocal(inv[u][:], guarded[u][:]).then_inc(inverted, 1)

                def take_xt(s, u):
                    g = 2 * s + u
                    dve.wait_ge(xt_mm, g + 1)
                    dve.wait_ge(xn_stored[u], s * 16)
                    dve.wait_ge(v_mm, g * TILES)
                    nc.vector.tensor_copy(xn_t[u][:, 1, :], xt_ps[1][:, :CHUNK]).then_inc(xt1_ready, 1)

                def front(s, u):
                    normalise(s, u)
                    invert(s, u)
                    take_xt(s, u)

                def step(s, u, after):
                    g = 2 * s + u

                    def take_row(t):
                        dve.wait_ge(row_mm, g * TILES + t + 1)
                        if t == 0:
                            dve.wait_ge(rows_stored[u], s * 16)
                        nc.vector.tensor_copy(rows_out[u][:, 2 * t + 1, :], row_ps[t % 2][1][:ROWS, :]).then_inc(row1_out, 1)

                    for t in range(TILES):
                        dve.wait_ge(v_mm, g * TILES + t + 1)
                        dve.wait_ge(v_ready, g * TILES + max(t - 1, 0))
                        nc.vector.tensor_tensor(v_pre[t % 2][:], v_ps[t % 2][:TILE, :], v_bias[:], ALU.add).then_inc(biased, 1)
                        if t == 0 and after:
                            normalise(*after)
                        if t:
                            take_row(t - 1)
                        if t == 1 and after:
                            invert(*after)
                    if after:
                        take_xt(*after)
                    take_row(TILES - 1)

                all_steps(dve, front, step)


def mix_phase(nc, d):
    with Tools(nc, "mx") as T:
        w_u = T.sb("w_u", [128, HALVES, WIDE])
        u_bias = T.sb("u_bias", [128, WIDE // 128])
        w_o = T.sb("w_o", [128, WIDE // 128, CH])
        o_bias = T.sb("o_bias", [TILE, CH])
        row_inv = T.sb("row_inv", [ROWS, SIDE])
        ident = T.sb("ident", [128, 128])
        y_in = [T.sb(f"y_in{u}", [ROWS, CHUNK_ROWS, WIDE]) for u in range(2)]
        xn_t = [T.sb(f"xn_t{u}", [128, HALVES, CHUNK]) for u in range(2)]
        x_in = [T.sb(f"x_in{u}", [TILE, TILES, CH]) for u in range(2)]
        gn = [T.sb(f"gn{u}", [TILE, 2, CH]) for u in range(2)]
        scale1, shift1 = ([T.sb(f"{n}{u}", [TILE, CH]) for u in range(2)] for n in ("scale1", "shift1"))
        scaled = [T.sb(f"scaled{u}", [TILE, TILES, CH]) for u in range(2)]
        resid = [T.sb(f"resid{u}", [TILE, TILES, CH]) for u in range(2)]
        gate = [T.sb(f"gate{u}", [128, WIDE // 128, CHUNK]) for u in range(2)]
        mixed = [T.sb(f"mixed{u}", [128, WIDE // 128, CHUNK]) for u in range(2)]
        t1 = [T.sb(f"t1{u}", [TILE, TILES, CH]) for u in range(2)]
        stats = T.sb("stats", [TILE, TILES, 6])
        moments = [T.sb(f"moments{u}", [TILE, TILES, 2]) for u in range(2)]
        var, root, inv, shift = ([T.sb(f"{n}{u}", [TILE, TILES]) for u in range(2)] for n in ("var", "root", "inv", "shift"))
        n1 = [T.sb(f"n1{u}", [TILE, TILES, CH]) for u in range(2)]
        n1_t = [T.sb(f"n1_t{u}", [128, HALVES, CHUNK]) for u in range(2)]
        BLOCKS = WIDE // 128
        y_ps = [T.ps(f"y{c}", [128, 512]) for c in range(BLOCKS)]
        u_ps = [T.ps(f"u{i}", [128, 512]) for i in range(2)]
        o_ps = [T.ps(f"o{i}", [128, 512]) for i in range(2)]
        (consts_in, row_prep, scaled_x, resid_ready, u_mm, gate_ready, y_mm, mixed_ready, o_mm, t1_ready, measured, aggregated,
         var_ready, rooted, inverted, shift_ready, n1_ready, nt_mm, nt0_ready, nt1_ready) = (T.sem(n) for n in (
             "consts_in", "row_prep", "scaled_x", "resid_ready", "u_mm", "gate_ready", "y_mm", "mixed_ready", "o_mm", "t1_ready",
             "measured", "aggregated", "var_ready", "rooted", "inverted", "shift_ready", "n1_ready", "nt_mm", "nt0_ready",
             "nt1_ready"))
        xn_loaded, y_loaded, x_loaded, t1_stored, nt_stored = (
            [T.sem(f"{n}{u}") for u in range(2)] for n in ("xn_loaded", "y_loaded", "x_loaded", "t1_stored", "nt_stored"))
        seen = T.sem("seen")
        PAIRS = BATCH * CHUNKS // 2
        loads = [(w_u, "w_u"), (u_bias, "u_bias"), (w_o, "w_o"), (o_bias, "o_bias"), (row_inv, "row_inv"), (ident, "ident")]

        def all_steps(eng, step):
            last = PAIRS - 1
            step(None, (0, 0), (0, 1))
            step((0, 0), (0, 1), (1, 0))
            with eng.Fori(1, last) as s:
                step((s - 1, 1), (s, 0), (s, 1))
                step((s, 0), (s, 1), (s + 1, 0))
            step((last - 1, 1), (last, 0), (last, 1))
            step((last, 0), (last, 1), None)

        with nc.Block() as block:
            @block.sync
            def _(sp):
                for tile, name in loads:
                    sp.dma_start(tile[:], d[name]).then_inc(consts_in, 16)
                with sp.Fori(0, PAIRS) as s:
                    for u in range(2):
                        g = s * 2 + u
                        sp.wait_ge(u_mm, s * 2 * BLOCKS)
                        sp.dma_start(xn_t[u][:], d["xn_t"][g]).then_inc(xn_loaded[u], 16)
                        sp.wait_ge(resid_ready, s * 2)
                        sp.dma_start(x_in[u][:], d["x_tiles"][g]).then_inc(x_loaded[u], 16)
                        sp.dma_start(gn[u][:].rearrange("p a c -> p (a c)"), d["gn_rows"][g].to_broadcast([TILE, 2 * CH])
                                     ).then_inc(x_loaded[u], 16)
                        sp.wait_ge(y_mm, s * 2 * BLOCKS)
                        sp.dma_start(y_in[u][:], rows_of_chunk(d["y_rows"], g)).then_inc(y_loaded[u], 16)

            @block.gpsimd
            def _(pool):
                pool.wait_ge(consts_in, 16 * len(loads))
                with pool.Fori(0, PAIRS) as s:
                    for u in range(2):
                        g = s * 2 + u
                        pool.wait_ge(x_loaded[u], s * 32 + 32)
                        pool.wait_ge(t1_ready, s * 2 * 2)
                        nc.gpsimd.tensor_tensor(shift1[u][:], gn[u][:, 1, :], o_bias[:], ALU.add)
                        nc.gpsimd.tensor_scalar(scale1[u][:], gn[u][:, 0, :], 1.0, 1.0, ALU.mult, ALU.add).then_inc(row_prep, 1)
                        pool.wait_ge(row_prep, g + 1)
                        nc.gpsimd.tensor_tensor(scaled[u][:], x_in[u][:], scale1[u][:].unsqueeze(1).to_broadcast([TILE, TILES, CH]),
                                                ALU.mult).then_inc(scaled_x, 1)
                        pool.wait_ge(scaled_x, g + 1)
                        nc.gpsimd.tensor_tensor(resid[u][:], scaled[u][:], shift1[u][:].unsqueeze(1).to_broadcast([TILE, TILES, CH]),
                                                ALU.add).then_inc(resid_ready, 1)

            @block.tensor
            def _(pe):
                pe.wait_ge(consts_in, 16 * len(loads))

                def gate_mm(s, u, blocks):
                    g = 2 * s + u
                    pe.wait_ge(xn_loaded[u], s * 16 + 16)
                    for c in blocks:
                        pe.wait_ge(gate_ready, g * BLOCKS + max(c - 1, 0))
                        for h in range(HALVES):
                            last = nc.tensor.matmul(u_ps[c % 2][:, :CHUNK], w_u[:, h, c * 128:(c + 1) * 128], xn_t[u][:, h, :],
                                                    start=h == 0, stop=h == HALVES - 1)
                        last.then_inc(u_mm, 1)

                def inverse_rows(s, u, first=False):
                    g = 2 * s + u
                    pe.wait_ge(y_loaded[u], s * 16 + 16)
                    for c in range(BLOCKS):
                        if not first:
                            pe.wait_ge(mixed_ready, (g - 1) * BLOCKS + c + 1)
                        for r in range(CHUNK_ROWS):
                            last = nc.tensor.matmul(y_ps[c][:, r * SIDE:(r + 1) * SIDE], y_in[u][:, r, c * 128:(c + 1) * 128],
                                                    row_inv[:], start=True, stop=True)
                        last.then_inc(y_mm, 1)

                def transpose_norm(s, u):
                    g = 2 * s + u
                    pe.wait_ge(n1_ready, g + 1)
                    pe.wait_ge(t1_ready, 2 * g + 2)
                    for h in range(HALVES):
                        for t in range(TILES):
                            last = nc.tensor.transpose(o_ps[h][:, t * TILE:(t + 1) * TILE], n1[u][:, t, h * 128:(h + 1) * 128],
                                                       ident[:TILE, :TILE])
                    last.then_inc(nt_mm, 1)

                def output_mm(s, u):
                    g = 2 * s + u
                    pe.wait_ge(mixed_ready, (g + 1) * BLOCKS)
                    for pair in range(TILES // 2):
                        pe.wait_ge(nt0_ready if pair == 0 else nt1_ready, g)
                        for t in (2 * pair, 2 * pair + 1):
                            for c in range(BLOCKS):
                                last = nc.tensor.matmul(o_ps[pair][:TILE, (t % 2) * CH:(t % 2 + 1) * CH],
                                                        mixed[u][:, c, t * TILE:(t + 1) * TILE], w_o[:, c, :],
                                                        start=c == 0, stop=c == BLOCKS - 1)
                        last.then_inc(o_mm, 1)

                def step(before, now, after):
                    if after:
                        gate_mm(*after, range(0, 2))
                    if before:
                        transpose_norm(*before)
                    if after:
                        gate_mm(*after, range(2, BLOCKS))
                    output_mm(*now)
                    if after:
                        inverse_rows(*after)

                gate_mm(0, 0, range(BLOCKS))
                inverse_rows(0, 0, first=True)
                all_steps(pe, step)
                transpose_norm(PAIRS - 1, 1)

            @block.scalar
            def _(act):
                act.wait_ge(consts_in, 16 * len(loads))

                def gates(s, u, blocks):
                    g = 2 * s + u
                    for c in blocks:
                        act.wait_ge(u_mm, g * BLOCKS + c + 1)
                        if c == 0:
                            act.wait_ge(mixed_ready, 2 * s * BLOCKS)
                        nc.scalar.activation(gate[u][:, c, :], u_ps[c % 2][:, :CHUNK], ACT.Silu,
                                             bias=u_bias[:, c:c + 1]).then_inc(gate_ready, 1)

                def take_norm(s, u):
                    g = 2 * s + u
                    act.wait_ge(nt_mm, g + 1)
                    act.wait_ge(nt_stored[u], s * 16)
                    nc.scalar.activation(n1_t[u][:, 0, :], o_ps[0][:, :CHUNK], ACT.Copy).then_inc(nt0_ready, 1)

                def store_norm(s, u):
                    g = 2 * s + u
                    act.wait_ge(nt0_ready, g + 1)
                    act.wait_ge(nt1_ready, g + 1)
                    act.dma_start(d["n1_t"][g], n1_t[u][:]).then_inc(nt_stored[u], 16)

                def roots(s, u):
                    g = 2 * s + u
                    act.wait_ge(var_ready, g + 1)
                    nc.scalar.activation(root[u][:], var[u][:], ACT.Sqrt).then_inc(rooted, 1)
                    act.wait_ge(t1_ready, 2 * g + 2)
                    act.dma_start(d["t1_tiles"][g], t1[u][:]).then_inc(t1_stored[u], 16)

                def step(before, now, after):
                    if after:
                        gates(*after, range(0, 2))
                    if before:
                        take_norm(*before)
                    if after:
                        gates(*after, range(2, BLOCKS))
                    if before:
                        store_norm(*before)
                    roots(*now)

                gates(0, 0, range(BLOCKS))
                all_steps(act, step)
                take_norm(PAIRS - 1, 1)
                store_norm(PAIRS - 1, 1)
                for u in range(2):
                    act.wait_ge(t1_stored[u], 16 * PAIRS)
                    act.wait_ge(nt_stored[u], 16 * PAIRS)

            @block.vector
            def _(dve):
                def mixes(s, u):
                    g = 2 * s + u
                    dve.wait_ge(gate_ready, g * BLOCKS + BLOCKS)
                    dve.wait_ge(o_mm, 2 * 2 * s)
                    for c in range(BLOCKS):
                        dve.wait_ge(y_mm, g * BLOCKS + c + 1)
                        nc.vector.tensor_tensor(mixed[u][:, c, :], gate[u][:, c, :], y_ps[c][:, :CHUNK],
                                                ALU.mult).then_inc(mixed_ready, 1)

                def take_norm(s, u):
                    g = 2 * s + u
                    dve.wait_ge(nt_mm, g + 1)
                    dve.wait_ge(nt_stored[u], s * 16)
                    nc.vector.tensor_copy(n1_t[u][:, 1, :], o_ps[1][:, :CHUNK]).then_inc(nt1_ready, 1)

                def residual_norm(s, u):
                    g = 2 * s + u
                    dve.wait_ge(resid_ready, g + 1)
                    dve.wait_ge(t1_stored[u], s * 16)
                    for pair in range(TILES // 2):
                        dve.wait_ge(o_mm, 2 * g + pair + 1)
                        nc.vector.tensor_tensor(t1[u][:, 2 * pair:2 * pair + 2, :],
                                                o_ps[pair][:TILE, :].rearrange("p (t c) -> p t c", t=2),
                                                resid[u][:, 2 * pair:2 * pair + 2, :], ALU.add).then_inc(t1_ready, 1)
                    dve.wait_ge(t1_ready, 2 * g + 2)
                    for t in range(TILES):
                        last = nc.vector.bn_stats(stats[:, t, :], t1[u][:, t, :])
                    last.then_inc(measured, 1)
                    dve.wait_ge(measured, g + 1)
                    dve.sem_inc(seen, 1)
                    for t in range(TILES):
                        last = nc.vector.bn_aggr(moments[u][:, t, :], stats[:, t, :])
                    last.then_inc(aggregated, 1)
                    dve.wait_ge(aggregated, g + 1)
                    nc.vector.tensor_scalar(var[u][:], moments[u][:, :, 1], LN_EPS, None, ALU.add).then_inc(var_ready, 1)

                def normalise(s, u):
                    g = 2 * s + u
                    dve.wait_ge(rooted, g + 1)
                    nc.vector.reciprocal(inv[u][:], root[u][:]).then_inc(inverted, 1)
                    dve.wait_ge(inverted, g + 1)
                    nc.vector.scalar_tensor_tensor(out=shift[u][:], in0=moments[u][:, :, 0], scalar=-1.0, in1=inv[u][:],
                                                   op0=ALU.mult, op1=ALU.mult).then_inc(shift_ready, 1)
                    dve.wait_ge(shift_ready, g + 1)
                    dve.wait_ge(nt_mm, 2 * s)
                    for t in range(TILES):
                        last = nc.vector.tensor_scalar(n1[u][:, t, :], t1[u][:, t, :], inv[u][:, t:t + 1], shift[u][:, t:t + 1],
                                                       ALU.mult, ALU.add)
                    last.then_inc(n1_ready, 1)

                def step(before, now, after):
                    if before:
                        take_norm(*before)
                    residual_norm(*now)
                    if after:
                        mixes(*after)
                    normalise(*now)

                mixes(0, 0)
                all_steps(dve, step)
                take_norm(PAIRS - 1, 1)


def attention_phase(nc, d):
    with Tools(nc, "at") as T:
        NT = CHUNKS * TILES
        HB = 128 // HEAD
        BLOCKS = 4
        w_qkv = T.sb("w_qkv", [128, HALVES, 3 * CH])
        w_proj = T.sb("w_proj", [128, HALVES, CH])
        p_bias = T.sb("p_bias", [TILE, CH])
        ident = T.sb("ident", [128, 128])
        same_head = T.sb("same_head", [128, 128])
        ones = T.sb("ones", [128, 128])
        n_t = [T.sb(f"n_t{i}", [128, HALVES, CHUNK]) for i in range(2)]
        qk = T.sb("qk", [TILE, NT, 2 * CH])
        v = T.sb("v", [TILE, NT, CH])
        qk_t = T.sb("qk_t", [128, BLOCKS, TOKENS])
        part = T.sb("part", [128, BLOCKS, CHUNKS])
        total, total_eps, total2, total2_eps = (T.sb(n, [128, BLOCKS]) for n in ("total", "total_eps", "total2", "total2_eps"))
        sel, sel2, weighted = (T.sb(n, [128, BLOCKS, HB]) for n in ("sel", "sel2", "weighted"))
        const, const2 = T.sb("const", [TILE, BLOCKS * HB]), T.sb("const2", [TILE, BLOCKS * HB])
        flow = T.sb("flow", [TILE, NT, BLOCKS * HB])
        inv_flow = T.sb("inv_flow", [TILE, NT, BLOCKS * HB])
        kept = T.sb("kept", [TILE, NT, BLOCKS * HB])
        clipped, source = T.sb("clipped", [TILE, NT, 2 * HB]), T.sb("source", [TILE, NT, 2 * HB])
        alloc, factor = T.sb("alloc", [TILE, NT, 2 * HB]), T.sb("factor", [TILE, NT, 2 * HB])
        z, z_inv = T.sb("z", [128, 2 * HB]), T.sb("z_inv", [128, 2 * HB])
        kv_scale, kv = T.sb("kv_scale", [128, HALVES, 128]), T.sb("kv", [128, HALVES, 128])
        upd = [T.sb(f"upd{i}", [TILE, CH]) for i in range(2)]
        upd_t = [T.sb(f"upd_t{i}", [128, HALVES, TILE]) for i in range(2)]
        t1 = [T.sb(f"t1{i}", [TILE, TILES, CH]) for i in range(2)]
        t2 = [T.sb(f"t2{i}", [TILE, TILES, CH]) for i in range(2)]
        bank = [T.ps(f"bank{i}", [128, 512]) for i in range(8)]
        qk_ps, v_ps, turn_ps = bank[0:2], bank[2:4], bank[4:8]
        flow_ps, const_ps, sums_ps, kept_ps, const2_ps, z_ps = bank[0], bank[1], bank[2], bank[3], bank[4], bank[5]
        kv_ps = bank[6:8]
        upd_ps, updt_ps, proj_ps = bank[0:2], bank[2:4], bank[4:6]
        (consts_in, qk_mm, v_mm, qk_ready, v_ready, turned, odd_out, even_out, summed, link, flow_mm, sums_mm, kept_mm, z_mm,
         alloc_ready, source_ready, v_scaled, kv_mm, upd_mm, upd_ready, updt_mm, updt_ready, proj_mm, t1_biased, t2_ready) = (
            T.sem(n) for n in (
                "consts_in", "qk_mm", "v_mm", "qk_ready", "v_ready", "turned", "odd_out", "even_out", "summed", "link", "flow_mm",
                "sums_mm", "kept_mm", "z_mm", "alloc_ready", "source_ready", "v_scaled", "kv_mm", "upd_mm", "upd_ready", "updt_mm",
                "updt_ready", "proj_mm", "t1_biased", "t2_ready"))
        n_loaded, t1_loaded, t2_stored = ([T.sem(f"{n}{i}") for i in range(2)] for n in ("n_loaded", "t1_loaded", "t2_stored"))
        PER_SLOT = [(CHUNKS + 1) // 2, CHUNKS // 2]
        LINKS = 18
        ALL_LINKS = {name: i + 1 for i, name in enumerate((
            "total", "total_eps", "sel", "const", "flow", "inv_flow", "weighted", "total2", "total2_eps", "sel2", "const2",
            "kept", "clipped", "factor", "z", "z_inv", "kv_scale", "kv"))}
        loads = [(w_qkv, "w_qkv"), (w_proj, "w_proj"), (p_bias, "p_bias"), (ident, "ident"), (same_head, "same_head"),
                 (ones, "ones")]
        head_mask = same_head[:, 0:128:HEAD]

        def wait_link(eng, b, name):
            eng.wait_ge(link, b * LINKS + ALL_LINKS[name])

        def slot_free(b, j, per=1):
            return (b * CHUNKS + max(j - 1, 0)) * per

        with nc.Block() as block:
            @block.sync
            def _(sp):
                for tile, name in loads:
                    sp.dma_start(tile[:], d[name]).then_inc(consts_in, 16)
                with sp.Fori(0, BATCH) as b:
                    for j in range(CHUNKS):
                        sp.wait_ge(v_mm, slot_free(b, j, TILES))
                        sp.dma_start(n_t[j % 2][:], d["n1_t"][b * CHUNKS + j]).then_inc(n_loaded[j % 2], 16)
                    for j in range(CHUNKS):
                        sp.wait_ge(t2_ready, slot_free(b, j, TILES))
                        sp.dma_start(t1[j % 2][:], d["t1_tiles"][b * CHUNKS + j]).then_inc(t1_loaded[j % 2], 16)

            @block.gpsimd
            def _(pool):
                pool.wait_ge(consts_in, 16 * len(loads))
                with pool.Fori(0, BATCH) as b:
                    for j in range(CHUNKS):
                        pool.wait_ge(t1_loaded[j % 2], (b * PER_SLOT[j % 2] + j // 2 + 1) * 16)
                        nc.gpsimd.tensor_tensor(t1[j % 2][:], t1[j % 2][:], p_bias[:].unsqueeze(1).to_broadcast([TILE, TILES, CH]),
                                                ALU.add).then_inc(t1_biased, 1)

            @block.tensor
            def _(pe):
                pe.wait_ge(consts_in, 16 * len(loads))
                with pe.Fori(0, BATCH) as b:
                    def turn(j):
                        pe.wait_ge(qk_ready, (b * CHUNKS + j + 1) * TILES)
                        pe.wait_ge(odd_out, (b * CHUNKS + j) * 2)
                        pe.wait_ge(even_out, (b * CHUNKS + j) * 2)
                        if j == 0:
                            pe.wait_ge(t2_ready, b * NT)
                        for x in range(BLOCKS):
                            for t in range(TILES):
                                last = nc.tensor.transpose(turn_ps[x][:, t * TILE:(t + 1) * TILE],
                                                           qk[:, j * TILES + t, x * 128:(x + 1) * 128], ident[:TILE, :TILE])
                            last.then_inc(turned, 1)

                    pe.wait_ge(upd_ready, b * NT)
                    pe.wait_ge(updt_ready, b * NT)
                    for j in range(CHUNKS):
                        pe.wait_ge(n_loaded[j % 2], (b * PER_SLOT[j % 2] + j // 2 + 1) * 16)
                        for t in range(TILES):
                            n = j * TILES + t
                            lhs = [n_t[j % 2][:, h, t * TILE:(t + 1) * TILE] for h in range(HALVES)]
                            pe.wait_ge(qk_ready, b * NT + max(n - 1, 0))
                            for h in range(HALVES):
                                last = nc.tensor.matmul(qk_ps[n % 2][:TILE, :], lhs[h], w_qkv[:, h, :2 * CH],
                                                        start=h == 0, stop=h == HALVES - 1)
                            last.then_inc(qk_mm, 1)
                            pe.wait_ge(v_ready, b * NT + max(n - 1, 0))
                            for h in range(HALVES):
                                last = nc.tensor.matmul(v_ps[n % 2][:TILE, :CH], lhs[h], w_qkv[:, h, 2 * CH:],
                                                        start=h == 0, stop=h == HALVES - 1)
                            last.then_inc(v_mm, 1)
                            if t == 0 and j:
                                turn(j - 1)
                    turn(CHUNKS - 1)

                    def head_sums(selection, const_bank, out_bank, done):
                        for x in range(BLOCKS):
                            nc.tensor.matmul(const_bank[:TILE, x * HB:(x + 1) * HB], ones[:, :TILE],
                                             selection[:, (x + 2) % BLOCKS, :], start=True, stop=True)
                        for t in range(NT):
                            for x in range(BLOCKS):
                                last = nc.tensor.matmul(out_bank[:TILE, (t * BLOCKS + x) * HB:(t * BLOCKS + x + 1) * HB],
                                                        qk_t[:, x, t * TILE:(t + 1) * TILE], selection[:, (x + 2) % BLOCKS, :],
                                                        start=True, stop=True)
                        last.then_inc(done, 1)

                    wait_link(pe, b, "sel")
                    pe.wait_ge(qk_ready, (b + 1) * NT)
                    pe.wait_ge(v_ready, (b + 1) * NT)
                    head_sums(sel, const_ps, flow_ps, flow_mm)

                    wait_link(pe, b, "inv_flow")
                    for x in range(BLOCKS):
                        for t in range(NT):
                            last = nc.tensor.matmul(sums_ps[:, x * HB:(x + 1) * HB], qk[:, t, x * 128:(x + 1) * 128],
                                                    inv_flow[:, t, x * HB:(x + 1) * HB], start=t == 0, stop=t == NT - 1)
                    last.then_inc(sums_mm, 1)
                    wait_link(pe, b, "sel2")
                    head_sums(sel2, const2_ps, kept_ps, kept_mm)

                    pe.wait_ge(source_ready, b + 1)
                    nc.tensor.matmul(z_ps[:, :NT * 2 * HB], ones[:TILE, :], source[:].rearrange("p t h -> p (t h)"),
                                     start=True, stop=True).then_inc(z_mm, 1)
                    for j in range(CHUNKS):
                        pe.wait_ge(v_scaled, b * CHUNKS + j + 1)
                        for t in range(j * TILES, (j + 1) * TILES):
                            for h in range(HALVES):
                                last = nc.tensor.matmul(kv_ps[h][:, :128], qk[:, t, (2 + h) * 128:(3 + h) * 128],
                                                        v[:, t, h * 128:(h + 1) * 128], start=t == 0, stop=t == NT - 1)
                    last.then_inc(kv_mm, 1)

                    wait_link(pe, b, "kv")
                    for n in range(NT + 2):
                        if n < NT:
                            pe.wait_ge(upd_ready, b * NT + max(n - 1, 0))
                            for h in range(HALVES):
                                last = nc.tensor.matmul(upd_ps[n % 2][:TILE, h * 128:(h + 1) * 128],
                                                        qk_t[:, h, n * TILE:(n + 1) * TILE], kv[:, h, :], start=True, stop=True)
                            last.then_inc(upd_mm, 1)
                        if 1 <= n <= NT:
                            pe.wait_ge(upd_ready, b * NT + n)
                            pe.wait_ge(updt_ready, b * NT + max(n - 2, 0))
                            for h in range(HALVES):
                                last = nc.tensor.transpose(updt_ps[(n - 1) % 2][:, h * TILE:(h + 1) * TILE],
                                                           upd[(n - 1) % 2][:, h * 128:(h + 1) * 128], ident[:TILE, :TILE])
                            last.then_inc(updt_mm, 1)
                        if n >= 2:
                            pe.wait_ge(updt_ready, b * NT + n - 1)
                            pe.wait_ge(t2_ready, b * NT + max(n - 3, 0))
                            for h in range(HALVES):
                                last = nc.tensor.matmul(proj_ps[n % 2][:TILE, :CH], upd_t[n % 2][:, h, :], w_proj[:, h, :],
                                                        start=h == 0, stop=h == HALVES - 1)
                            last.then_inc(proj_mm, 1)

            @block.scalar
            def _(act):
                with act.Fori(0, BATCH) as b:
                    def take_odd(j):
                        for i, x in enumerate((1, 3)):
                            act.wait_ge(turned, (b * CHUNKS + j) * BLOCKS + x + 1)
                            nc.scalar.activation(qk_t[:, x, j * CHUNK:(j + 1) * CHUNK], turn_ps[x][:, :CHUNK], ACT.Copy,
                                                 accum_out=part[:, x, j:j + 1]).then_inc(odd_out, 1)

                    act.wait_ge(kv_mm, b)
                    act.wait_ge(upd_mm, b * NT)
                    for n in range(NT):
                        j, t = divmod(n, TILES)
                        act.wait_ge(qk_mm, b * NT + n + 1)
                        nc.scalar.activation(qk[:, n, :], qk_ps[n % 2][:TILE, :], ACT.Sigmoid).then_inc(qk_ready, 1)
                        if t == 0 and j:
                            take_odd(j - 1)
                    take_odd(CHUNKS - 1)
                    wait_link(act, b, "kept")
                    nc.scalar.activation(alloc[:], kept[:, :, :2 * HB], ACT.Sigmoid).then_inc(alloc_ready, 1)
                    wait_link(act, b, "clipped")
                    nc.scalar.activation(source[:], clipped[:], ACT.Exp).then_inc(source_ready, 1)
                    for n in range(NT):
                        j = n // TILES
                        act.wait_ge(updt_mm, b * NT + n + 1)
                        act.wait_ge(proj_mm, b * NT + max(n - 1, 0))
                        nc.scalar.activation(upd_t[n % 2][:], updt_ps[n % 2][:, :2 * TILE].rearrange("p (h t) -> p h t", h=2),
                                             ACT.Copy).then_inc(updt_ready, 1)
                        if n % TILES == 1 and j:
                            act.wait_ge(t2_ready, b * NT + j * TILES)
                            act.dma_start(d["t2_tiles"][b * CHUNKS + j - 1], t2[(j - 1) % 2][:]).then_inc(t2_stored[(j - 1) % 2], 16)
                    act.wait_ge(t2_ready, (b + 1) * NT)
                    act.dma_start(d["t2_tiles"][b * CHUNKS + CHUNKS - 1], t2[(CHUNKS - 1) % 2][:]
                                  ).then_inc(t2_stored[(CHUNKS - 1) % 2], 16)
                for i in range(2):
                    act.wait_ge(t2_stored[i], 16 * BATCH * PER_SLOT[i])

            @block.vector
            def _(dve):
                dve.wait_ge(consts_in, 16 * len(loads))
                with dve.Fori(0, BATCH) as b:
                    def take_even(j):
                        for i, x in enumerate((0, 2)):
                            dve.wait_ge(turned, (b * CHUNKS + j) * BLOCKS + x + 1)
                            nc.vector.reduce_sum(part[:, x, j:j + 1], turn_ps[x][:, :CHUNK], axis=AX.X).then_inc(summed, 1)
                            nc.vector.tensor_copy(qk_t[:, x, j * CHUNK:(j + 1) * CHUNK], turn_ps[x][:, :CHUNK]).then_inc(even_out, 1)

                    def step(name, instruction):
                        instruction.then_inc(link, 1)

                    for n in range(NT):
                        j, t = divmod(n, TILES)
                        dve.wait_ge(v_mm, b * NT + n + 1)
                        nc.vector.tensor_copy(v[:, n, :], v_ps[n % 2][:TILE, :CH]).then_inc(v_ready, 1)
                        if t == 0 and j:
                            take_even(j - 1)
                    take_even(CHUNKS - 1)

                    mask3 = head_mask.unsqueeze(1).to_broadcast([128, BLOCKS, HB])

                    def per_block(x):
                        return x[:].unsqueeze(2).to_broadcast([128, BLOCKS, HB])

                    def per_token(x):
                        return x[:].unsqueeze(1).to_broadcast([TILE, NT, BLOCKS * HB])

                    dve.wait_ge(summed, (b + 1) * CHUNKS * 2)
                    dve.wait_ge(odd_out, (b + 1) * CHUNKS * 2)
                    step("total", nc.vector.reduce_sum(total[:], part[:], axis=AX.X))
                    wait_link(dve, b, "total")
                    step("total_eps", nc.vector.tensor_scalar(total_eps[:], total[:], ATT_EPS, None, ALU.add))
                    wait_link(dve, b, "total_eps")
                    step("sel", nc.vector.tensor_tensor(sel[:], mask3, per_block(total_eps), ALU.mult))
                    dve.wait_ge(flow_mm, b + 1)
                    step("const", nc.vector.tensor_scalar(const[:], const_ps[:TILE, :BLOCKS * HB], ATT_EPS, ATT_EPS, ALU.mult, ALU.add))
                    wait_link(dve, b, "const")
                    step("flow", nc.vector.tensor_tensor(flow[:], flow_ps[:TILE, :NT * BLOCKS * HB].rearrange(
                        "p (t x) -> p t x", t=NT), per_token(const), ALU.add))
                    wait_link(dve, b, "flow")
                    step("inv_flow", nc.vector.reciprocal(inv_flow[:], flow[:]))
                    dve.wait_ge(sums_mm, b + 1)
                    step("weighted", nc.vector.tensor_tensor(weighted[:], sums_ps[:, :BLOCKS * HB].rearrange(
                        "p (x h) -> p x h", x=BLOCKS), mask3, ALU.mult))
                    wait_link(dve, b, "weighted")
                    step("total2", nc.vector.reduce_sum(total2[:], weighted[:], axis=AX.X))
                    wait_link(dve, b, "total2")
                    step("total2_eps", nc.vector.tensor_scalar(total2_eps[:], total2[:], ATT_EPS, None, ALU.add))
                    wait_link(dve, b, "total2_eps")
                    step("sel2", nc.vector.tensor_tensor(sel2[:], mask3, per_block(total2_eps), ALU.mult))
                    dve.wait_ge(kept_mm, b + 1)
                    step("const2", nc.vector.tensor_scalar(const2[:], const2_ps[:TILE, :BLOCKS * HB], ATT_EPS, ATT_EPS,
                                                           ALU.mult, ALU.add))
                    wait_link(dve, b, "const2")
                    step("kept", nc.vector.tensor_tensor(kept[:], kept_ps[:TILE, :NT * BLOCKS * HB].rearrange(
                        "p (t x) -> p t x", t=NT), per_token(const2), ALU.add))
                    wait_link(dve, b, "kept")
                    step("clipped", nc.vector.tensor_scalar(clipped[:], kept[:, :, 2 * HB:], 1.0, -1.0, ALU.min, ALU.max))
                    dve.wait_ge(alloc_ready, b + 1)
                    step("factor", nc.vector.tensor_tensor(factor[:], inv_flow[:, :, :2 * HB], alloc[:], ALU.mult))
                    dve.wait_ge(source_ready, b + 1)
                    for j in range(CHUNKS):
                        tiles = slice(j * TILES, (j + 1) * TILES)
                        heads = v[:, tiles, :].rearrange("p t (h c) -> p (t h) c", c=HEAD)
                        each = source[:, tiles, :].rearrange("p t h -> p (t h)").unsqueeze(2).to_broadcast([TILE, TILES * 2 * HB, HEAD])
                        nc.vector.tensor_tensor(heads, heads, each, ALU.mult).then_inc(v_scaled, 1)
                    dve.wait_ge(z_mm, b + 1)
                    step("z", nc.vector.reduce_sum(z[:], z_ps[:, :NT * 2 * HB].rearrange("p (t h) -> p h t", t=NT), axis=AX.X))
                    wait_link(dve, b, "z")
                    step("z_inv", nc.vector.reciprocal(z_inv[:], z[:]))
                    wait_link(dve, b, "z_inv")
                    for h in range(HALVES):
                        last = nc.vector.scalar_tensor_tensor(
                            out=kv_scale[:, h, :].rearrange("p (a c) -> p a c", c=HEAD),
                            in0=z_inv[:, h * HB:(h + 1) * HB].unsqueeze(2).to_broadcast([128, HB, HEAD]), scalar=TOKENS / V_SCALE,
                            in1=same_head[:].rearrange("p (a c) -> p a c", c=HEAD), op0=ALU.mult, op1=ALU.mult)
                    step("kv_scale", last)
                    wait_link(dve, b, "kv_scale")
                    dve.wait_ge(kv_mm, b + 1)
                    for h in range(HALVES):
                        last = nc.vector.tensor_tensor(kv[:, h, :], kv_ps[h][:, :128], kv_scale[:, h, :], ALU.mult)
                    step("kv", last)

                    for n in range(NT + 2):
                        if n < NT:
                            dve.wait_ge(upd_mm, b * NT + n + 1)
                            dve.wait_ge(updt_mm, b * NT + max(n - 1, 0))
                            nc.vector.tensor_tensor(upd[n % 2][:].rearrange("p (h c) -> p h c", c=HEAD),
                                                    upd_ps[n % 2][:TILE, :CH].rearrange("p (h c) -> p h c", c=HEAD),
                                                    factor[:, n, :].unsqueeze(2).to_broadcast([TILE, 2 * HB, HEAD]),
                                                    ALU.mult).then_inc(upd_ready, 1)
                        if n >= 2:
                            m = n - 2
                            j, t = divmod(m, TILES)
                            if t == 0:
                                dve.wait_ge(t1_biased, b * CHUNKS + j + 1)
                                dve.wait_ge(t2_stored[j % 2], (b * PER_SLOT[j % 2] + j // 2) * 16)
                            dve.wait_ge(proj_mm, b * NT + m + 1)
                            nc.vector.tensor_tensor(t2[j % 2][:, t, :], proj_ps[m % 2][:TILE, :CH], t1[j % 2][:, t, :],
                                                    ALU.add).then_inc(t2_ready, 1)


def ffn_phase(nc, d):
    with Tools(nc, "ff") as T:
        NB = HIDDEN // 128
        PAIRS_T = CHUNK // 2
        fc1_raw = T.sb("fc1_raw", [128, HALVES, HIDDEN])
        interp = T.sb("interp", [128, HALVES, 128])
        fc1 = T.sb("fc1", [128, HIDDEN])
        fc1_bias = T.sb("fc1_bias", [128, NB])
        fc2 = T.sb("fc2", [128, NB, 128])
        fc2_bias = T.sb("fc2_bias", [128, 1])
        pair_tok = T.sb("pair_tok", [TILE, SIDE])
        pair_down = T.sb("pair_down", [128, HALVES, 128])
        pair_up = T.sb("pair_up", [128, CH])
        t2 = [T.sb(f"t2{u}", [TILE, TILES, CH]) for u in range(2)]
        stats = T.sb("stats", [TILE, TILES, 6])
        moments = [T.sb(f"moments{u}", [TILE, TILES, 2]) for u in range(2)]
        var, root, inv, shift = ([T.sb(f"{n}{u}", [TILE, TILES]) for u in range(2)] for n in ("var", "root", "inv", "shift"))
        n2 = [T.sb(f"n2{u}", [TILE, TILES, CH]) for u in range(2)]
        base = [T.sb(f"base{u}", [TILE, TILES, CH]) for u in range(2)]
        pairs = [T.sb(f"pairs{u}", [128, HALVES, PAIRS_T]) for u in range(2)]
        low = [T.sb(f"low{u}", [128, PAIRS_T]) for u in range(2)]
        hid = T.sb("hid", [128, NB, PAIRS_T])
        change = T.sb("change", [128, CHUNK])
        out = [T.sb(f"out{u}", [TILE, TILES, CH]) for u in range(2)]
        pairs_ps, low_ps, new_ps = T.ps("pairs", [128, 512]), T.ps("low", [128, 512]), T.ps("new", [128, 512])
        FB = 3
        hid_ps = [T.ps(f"hid{i}", [128, 512]) for i in range(FB)]
        up_ps = [T.ps(f"up{i}", [128, 512]) for i in range(2)]
        (consts_in, fc1_mm, fc1_ready, measured, aggregated, var_ready, rooted, inverted, shift_ready, n2_ready, base_ready,
         pairs_mm, pairs_ready, low_mm, low_ready, hid_mm, hid_ready, new_mm, change_ready, up_mm, out_ready) = (
            T.sem(n) for n in ("consts_in", "fc1_mm", "fc1_ready", "measured", "aggregated", "var_ready", "rooted", "inverted",
                               "shift_ready", "n2_ready", "base_ready", "pairs_mm", "pairs_ready", "low_mm", "low_ready",
                               "hid_mm", "hid_ready", "new_mm", "change_ready", "up_mm", "out_ready"))
        loaded, stored = ([T.sem(f"{n}{u}") for u in range(2)] for n in ("loaded", "stored"))
        seen = T.sem("seen")
        PAIRS = BATCH * CHUNKS // 2
        loads = [(fc1_raw, "fc1"), (interp, "interp"), (fc1_bias, "fc1_bias"), (fc2, "fc2"), (fc2_bias, "fc2_bias"),
                 (pair_tok, "pair_tok"), (pair_down, "pair_down"), (pair_up, "pair_up")]

        def all_steps(eng, front, step):
            front(0, 0)
            with eng.Fori(0, PAIRS - 1) as s:
                step((s, 0), (s, 1))
                step((s, 1), (s + 1, 0))
            step((PAIRS - 1, 0), (PAIRS - 1, 1))
            step((PAIRS - 1, 1), None)

        with nc.Block() as block:
            @block.sync
            def _(sp):
                for tile, name in loads:
                    sp.dma_start(tile[:], d[name]).then_inc(consts_in, 16)
                with sp.Fori(0, PAIRS) as s:
                    for u in range(2):
                        sp.wait_ge(base_ready, s * 2)
                        sp.wait_ge(n2_ready, s * 2)
                        sp.dma_start(t2[u][:], d["t2_tiles"][s * 2 + u]).then_inc(loaded[u], 16)

            @block.gpsimd
            def _(pool):
                with pool.Fori(0, PAIRS) as s:
                    for u in range(2):
                        pool.wait_ge(n2_ready, s * 2 + u + 1)
                        pool.wait_ge(out_ready, s * 2 * 2)
                        nc.gpsimd.tensor_tensor(base[u][:], t2[u][:], n2[u][:], ALU.add).then_inc(base_ready, 1)

            @block.tensor
            def _(pe):
                pe.wait_ge(consts_in, 16 * len(loads))
                for i in range(2):
                    for h in range(HALVES):
                        last = nc.tensor.matmul(up_ps[i][:], interp[:, h, :], fc1_raw[:, h, i * 512:(i + 1) * 512],
                                                start=h == 0, stop=h == HALVES - 1)
                    last.then_inc(fc1_mm, 1)

                def pair_mm(s, u):
                    g = 2 * s + u
                    pe.wait_ge(n2_ready, g + 1)
                    pe.wait_ge(pairs_ready, g)
                    for h in range(HALVES):
                        for t in range(TILES):
                            last = nc.tensor.matmul(pairs_ps[:, (h * TILES + t) * SIDE:(h * TILES + t + 1) * SIDE],
                                                    n2[u][:, t, h * 128:(h + 1) * 128], pair_tok[:], start=True, stop=True)
                    last.then_inc(pairs_mm, 1)

                def low_band(s, u):
                    g = 2 * s + u
                    pe.wait_ge(pairs_ready, g + 1)
                    pe.wait_ge(low_ready, g)
                    for h in range(HALVES):
                        last = nc.tensor.matmul(low_ps[:, :PAIRS_T], pair_down[:, h, :], pairs[u][:, h, :],
                                                start=h == 0, stop=h == HALVES - 1)
                    last.then_inc(low_mm, 1)

                def front(s, u):
                    pair_mm(s, u)
                    low_band(s, u)

                def step(now, after):
                    s, u = now
                    g = 2 * s + u

                    def second(m):
                        pe.wait_ge(hid_ready, g * NB + m + 1)
                        if m == 0:
                            pe.wait_ge(change_ready, g)
                        last = nc.tensor.matmul(new_ps[:, :PAIRS_T], fc2[:, m, :], hid[:, m, :], start=m == 0, stop=m == NB - 1)
                        if m == NB - 1:
                            last.then_inc(new_mm, 1)

                    pe.wait_ge(low_ready, g + 1)
                    for m in range(NB):
                        pe.wait_ge(hid_ready, g * NB + max(m - FB + 1, 0))
                        nc.tensor.matmul(hid_ps[m % FB][:, :PAIRS_T], fc1[:, m * 128:(m + 1) * 128], low[u][:],
                                         start=True, stop=True).then_inc(hid_mm, 1)
                        if m >= FB:
                            second(m - FB)
                    if after:
                        pair_mm(*after)
                    for m in range(NB - FB, NB):
                        second(m)
                    if after:
                        low_band(*after)
                    pe.wait_ge(change_ready, g + 1)
                    for pair in range(TILES // 2):
                        pe.wait_ge(out_ready, 2 * g)
                        for t in (2 * pair, 2 * pair + 1):
                            last = nc.tensor.matmul(up_ps[pair][:TILE, (t % 2) * CH:(t % 2 + 1) * CH],
                                                    change[:, t * TILE:(t + 1) * TILE], pair_up[:], start=True, stop=True)
                        last.then_inc(up_mm, 1)

                pe.wait_ge(fc1_ready, 2)
                all_steps(pe, front, step)

            @block.scalar
            def _(act):
                act.wait_ge(consts_in, 16 * len(loads))
                for i in range(2):
                    act.wait_ge(fc1_mm, i + 1)
                    nc.scalar.activation(fc1[:, i * 512:(i + 1) * 512], up_ps[i][:], ACT.Copy).then_inc(fc1_ready, 1)

                def roots(s, u):
                    act.wait_ge(var_ready, 2 * s + u + 1)
                    nc.scalar.activation(root[u][:], var[u][:], ACT.Sqrt).then_inc(rooted, 1)

                def take_pairs(s, u):
                    act.wait_ge(pairs_mm, 2 * s + u + 1)
                    act.wait_ge(low_mm, 2 * s)
                    nc.scalar.activation(pairs[u][:].rearrange("p h t -> p (h t)"), pairs_ps[:, :CHUNK], ACT.Copy
                                         ).then_inc(pairs_ready, 1)

                def take_low(s, u):
                    act.wait_ge(low_mm, 2 * s + u + 1)
                    act.wait_ge(change_ready, 2 * s)
                    nc.scalar.activation(low[u][:], low_ps[:, :PAIRS_T], ACT.Copy).then_inc(low_ready, 1)

                def front(s, u):
                    roots(s, u)
                    take_pairs(s, u)
                    take_low(s, u)

                def step(now, after):
                    s, u = now
                    g = 2 * s + u
                    if after:
                        roots(*after)
                    act.wait_ge(new_mm, g)
                    for m in range(NB):
                        act.wait_ge(hid_mm, g * NB + m + 1)
                        nc.scalar.activation(hid[:, m, :], hid_ps[m % FB][:, :PAIRS_T], ACT.Gelu,
                                             bias=fc1_bias[:, m:m + 1]).then_inc(hid_ready, 1)
                    if after:
                        take_pairs(*after)
                        take_low(*after)
                    act.wait_ge(out_ready, 2 * g + 2)
                    act.dma_start(d["out"][g], out[u][:]).then_inc(stored[u], 16)

                all_steps(act, front, step)
                for u in range(2):
                    act.wait_ge(stored[u], 16 * PAIRS)

            @block.vector
            def _(dve):
                dve.wait_ge(consts_in, 16 * len(loads))

                def moments_of(s, u):
                    g = 2 * s + u
                    dve.wait_ge(loaded[u], s * 16 + 16)
                    for t in range(TILES):
                        last = nc.vector.bn_stats(stats[:, t, :], t2[u][:, t, :])
                    last.then_inc(measured, 1)
                    dve.wait_ge(measured, g + 1)
                    dve.sem_inc(seen, 1)
                    for t in range(TILES):
                        last = nc.vector.bn_aggr(moments[u][:, t, :], stats[:, t, :])
                    last.then_inc(aggregated, 1)
                    dve.wait_ge(aggregated, g + 1)
                    nc.vector.tensor_scalar(var[u][:], moments[u][:, :, 1], LN_EPS, None, ALU.add).then_inc(var_ready, 1)

                def normalise(s, u):
                    g = 2 * s + u
                    dve.wait_ge(rooted, g + 1)
                    nc.vector.reciprocal(inv[u][:], root[u][:]).then_inc(inverted, 1)
                    dve.wait_ge(inverted, g + 1)
                    nc.vector.scalar_tensor_tensor(out=shift[u][:], in0=moments[u][:, :, 0], scalar=-1.0, in1=inv[u][:],
                                                   op0=ALU.mult, op1=ALU.mult).then_inc(shift_ready, 1)
                    dve.wait_ge(shift_ready, g + 1)
                    dve.wait_ge(pairs_mm, 2 * s)
                    dve.wait_ge(base_ready, 2 * s)
                    for t in range(TILES):
                        last = nc.vector.tensor_scalar(n2[u][:, t, :], t2[u][:, t, :], inv[u][:, t:t + 1], shift[u][:, t:t + 1],
                                                       ALU.mult, ALU.add)
                    last.then_inc(n2_ready, 1)

                def front(s, u):
                    moments_of(s, u)
                    normalise(s, u)

                def step(now, after):
                    s, u = now
                    g = 2 * s + u
                    if after:
                        moments_of(*after)
                        normalise(*after)
                    dve.wait_ge(new_mm, g + 1)
                    dve.wait_ge(up_mm, 2 * g)
                    twice = [128, PAIRS_T, 2]
                    nc.vector.scalar_tensor_tensor(out=change[:].rearrange("p (t r) -> p t r", r=2),
                                                   in0=new_ps[:, :PAIRS_T].unsqueeze(2).to_broadcast(twice), scalar=fc2_bias[:, 0:1],
                                                   in1=low[u][:].unsqueeze(2).to_broadcast(twice), op0=ALU.add, op1=ALU.subtract
                                                   ).then_inc(change_ready, 1)
                    dve.wait_ge(base_ready, g + 1)
                    dve.wait_ge(stored[u], s * 16)
                    for pair in range(TILES // 2):
                        dve.wait_ge(up_mm, 2 * g + pair + 1)
                        nc.vector.tensor_tensor(out[u][:, 2 * pair:2 * pair + 2, :],
                                                up_ps[pair][:TILE, :].rearrange("p (t c) -> p t c", t=2),
                                                base[u][:, 2 * pair:2 * pair + 2, :], ALU.add).then_inc(out_ready, 1)

                all_steps(dve, front, step)


def program(nc, d):
    def scratch(name, shape):
        d[name] = nc.dram_tensor(name, shape, F32, kind="Internal").ap()

    chunks = BATCH * CHUNKS
    scratch("kern_rows", (ROWS, TAPS_PAD, WIDE))
    scratch("gn_rows", (chunks, 1, 2 * CH))
    scratch("xn_t", (chunks, 128, HALVES, CHUNK))
    scratch("v_rows", (ROWS, BATCH, SIDE, WIDE))
    scratch("y_rows", (ROWS, BATCH, SIDE, WIDE))
    scratch("t1_tiles", (chunks, TILE, TILES, CH))
    scratch("n1_t", (chunks, 128, HALVES, CHUNK))
    scratch("t2_tiles", (chunks, TILE, TILES, CH))
    flat = "b i j c -> (b i j) c"
    d["x_tiles"] = d["x"].rearrange(flat).rearrange("(g t p) c -> g p t c", t=TILES, p=TILE)
    d["out"] = d["result"].rearrange(flat).rearrange("(g t p) c -> g p t c", t=TILES, p=TILE)
    for phase in (kernel_rows_phase, stats_phase, project_phase, columns_phase, mix_phase, attention_phase, ffn_phase):
        phase(nc, d)


def kernel(**inputs):
    import concourse.bacc as bacc
    from concourse.bass_utils import run_bass_kernel_spmd

    a = {k: np.asarray(v) for k, v in inputs.items()}

    def on_partitions(w):
        return w.reshape(-1, 128, *w.shape[1:]).swapaxes(0, 1)

    def every_row(b, rows):
        return np.broadcast_to(b, (rows, b.shape[0]))

    conv, att, ffn = "L0_conv_", "L1_attn_", "L1_ffn_"
    rpe_bias = np.concatenate([a[conv + "rpe_in_b"][None], a[conv + "rpe_h_b"]], 0)
    arrays = {
        "x": a["x"],
        "w_u": on_partitions(a[conv + "W_u"].T), "u_bias": a[conv + "b_u"].reshape(-1, 128).T,
        "w_v": on_partitions(a[conv + "W_v"].T), "v_bias": every_row(a[conv + "b_v"], TILE),
        "w_o": on_partitions(a[conv + "W_o"].T), "o_bias": every_row(a[conv + "b_o"], TILE),
        "rpe_in": a[conv + "rpe_in_w"].T,
        "rpe_h": a[conv + "rpe_h_w"].transpose(0, 2, 1).reshape(RPE_LAYERS, HALVES, 128, CH).transpose(2, 0, 1, 3),
        "rpe_bias": rpe_bias.reshape(RPE_LAYERS + 1, HALVES, 128).transpose(2, 0, 1),
        "rpe_out": on_partitions(a[conv + "rpe_out_w"].T), "rpe_out_b": every_row(a[conv + "rpe_out_b"], TAPS),
        "w_qkv": on_partitions(a[att + "W_qkv"].T), "w_proj": on_partitions(a[att + "W_proj"].T),
        "p_bias": every_row(a[att + "b_proj"], TILE),
        "fc1": on_partitions(a[ffn + "fc1_w"].T), "fc1_bias": a[ffn + "fc1_b"].reshape(-1, 128).T,
        "fc2": on_partitions(a[ffn + "fc2_w"].T), "fc2_bias": a[ffn + "fc2_b"][:, None],
        **shape_constants(),
    }
    arrays = {k: np.ascontiguousarray(v) for k, v in arrays.items()}
    nc = bacc.Bacc("TRN2", target_bir_lowering=False, num_devices=1)
    d = {k: nc.dram_tensor(k, v.shape, mybir.dt.from_np(v.dtype), kind="ExternalInput").ap() for k, v in arrays.items()}
    d["result"] = nc.dram_tensor("result", (BATCH, SIDE, SIDE, CH), F32, kind="ExternalOutput").ap()
    program(nc, d)
    return run_bass_kernel_spmd(nc, [arrays], core_ids=[0]).results[0]["result"]
```

```python
from contextlib import ExitStack

import numpy as np

import concourse.bass as bass
from concourse import mybir

F32 = mybir.dt.float32
F32R = mybir.dt.float32r
ACT = mybir.ActivationFunctionType
ALU = mybir.AluOpType
AX = mybir.AxisListType

BATCH, SIDE, CH = 8, 56, 256
TOKENS = SIDE * SIDE
WIDE = 512
POINTS = 2 * SIDE
FREQ = SIDE + 1
ROWS = 2 * FREQ
TAPS = 2 * SIDE - 1
TAPS_PAD = 112
HALVES = CH // 128
CHUNK_ROWS = 8
CHUNK = CHUNK_ROWS * SIDE
CHUNKS = TOKENS // CHUNK
TILE = 2 * SIDE
TILES = CHUNK // TILE
RPE_ROWS = 4
RPE_CHUNK = RPE_ROWS * TAPS
RPE_LAYERS = 3
HEAD = 32
HIDDEN = 1024
V_SCALE = float((HEAD ** -0.5) * CH // 8)
RMS_EPS = 1e-08
GN_EPS = 1e-05
ATT_EPS = 1e-06
LN_EPS = 1e-05


def angles(a, b):
    return 2.0 * np.pi * ((np.outer(a, b) % POINTS) / POINTS)


def shape_constants():
    pos, freq, full = np.arange(SIDE), np.arange(FREQ), np.arange(POINTS)
    tap = np.arange(TAPS) - (SIDE - 1)
    c = {}
    w = angles(pos, freq)
    row = np.concatenate([np.cos(w), -np.sin(w)], 1)
    fwd = np.zeros((TILE, 2, ROWS))
    fwd[:SIDE, 0], fwd[SIDE:, 1] = row, row
    c["row_fwd"] = fwd
    w = angles(tap, freq)
    c["row_taps"] = np.concatenate([np.cos(w), -np.sin(w)], 1)
    w = angles(pos, full)
    c["col_fwd"] = np.stack([np.concatenate([np.cos(w), np.sin(w)], 0), np.concatenate([-np.sin(w), np.cos(w)], 0)], 1)
    w = angles(tap, full)
    c["col_taps"] = np.stack([np.cos(w), np.sin(w), -np.sin(w)], 1)
    w = angles(full, pos)
    c["col_inv"] = np.stack([np.concatenate([np.cos(w), np.sin(w)], 1), np.concatenate([-np.sin(w), np.cos(w)], 1)], 1) / POINTS
    w = angles(freq, pos)
    weight = np.where((freq == 0) | (freq == SIDE), 1.0, 2.0)[:, None] / POINTS
    edge = np.where((freq == 0) | (freq == SIDE), 0.0, 1.0)[:, None]
    c["row_inv"] = np.concatenate([weight * np.cos(w), -weight * edge * np.sin(w)], 0)
    c["ident"] = np.eye(128)
    c["ones"] = np.ones((128, 128))
    c["mean_ch"] = np.full((128, 128), 1.0 / CH)
    c["group_mean"] = np.kron(np.eye(16), np.full((8, 8), 1.0 / 8))
    c["same_head"] = np.kron(np.eye(128 // HEAD), np.ones((HEAD, HEAD)))
    heads = np.kron(np.eye(128 // HEAD), np.ones((1, HEAD)))
    blocks = np.stack([np.kron(np.eye(4)[x][:, None], heads) for x in range(4)], 0)
    c["row_head"] = np.concatenate([np.zeros((12, 128)), np.tile(blocks[0], (CHUNKS, 1))], 0).T
    spread = np.stack([np.kron(np.eye(CHUNKS)[j][:, None], blocks[x]) for j in range(CHUNKS) for x in range(4)], 1)
    c["spread"] = spread
    c["z_rows"] = spread.reshape(-1, CHUNKS, 4, 128).sum(1)[:, 2:]
    p, q = np.meshgrid(np.arange(TAPS_PAD) - (SIDE - 1), tap, indexing="ij")
    c["coords"] = np.stack([p.ravel(), q.ravel()], 0)
    c["pair_up"] = np.kron(np.eye(CH // 2), np.ones((1, 2))) * 0.5
    c["pair_tok"] = np.kron(np.eye(SIDE), np.ones((2, 1))) * 0.5
    at = np.linspace(0.0, 1.0, CH, dtype=np.float32) * np.float32(CH // 2 - 1)
    lo = np.clip(np.floor(at).astype(np.int32), 0, CH // 2 - 2)
    frac = at - lo.astype(np.float32)
    interp = np.zeros((CH, CH // 2), np.float32)
    interp[np.arange(CH), lo] += np.float32(1.0) - frac
    interp[np.arange(CH), lo + 1] += frac
    c["interp"] = interp.reshape(HALVES, 128, 128).transpose(1, 0, 2)
    return {k: np.ascontiguousarray(v, dtype=np.float32) for k, v in c.items()}


def rows_of_chunk(rows, g):
    return rows.rearrange("k b i c -> k (b i) c")[:, bass.ds(g * CHUNK_ROWS, CHUNK_ROWS), :]


def product(nc, out, weights, data, start, stop):
    passes = [(0, 0), (0, 1), (1, 0)]
    for i, (a, b) in enumerate(passes):
        last = nc.tensor.matmul(out, weights[a], data[b], start=start and i == 0, stop=stop and i == len(passes) - 1)
    return last


class Tools:

    def __init__(self, nc, tag):
        self.nc, self.tag, self.phase, self.semaphores = nc, tag, ExitStack(), []

    def __enter__(self):
        return self

    def __exit__(self, kind, *a):
        if kind is None:
            self.phase.close()
            self.nc.clear_and_free_semaphores(self.semaphores)
            self.nc.all_engine_barrier()

    def sb(self, name, shape, dtype=F32):
        return self.phase.enter_context(self.nc.sbuf_tensor(f"{self.tag}_{name}", shape, dtype))

    def ps(self, name, shape):
        return self.phase.enter_context(self.nc.psum_tensor(f"{self.tag}_{name}_ps", shape, F32))

    def sem(self, name):
        self.semaphores.append(self.nc.alloc_semaphore(name=f"{self.tag}_{name}"))
        return self.semaphores[-1]


def kernel_rows_phase(nc, d):
    with Tools(nc, "kr") as T:
        w_in = T.sb("w_in", [2, CH])
        raw_h = T.sb("raw_h", [128, RPE_LAYERS, HALVES, CH])
        raw_out = T.sb("raw_out", [128, HALVES, WIDE])
        w_h = [T.sb(f"w_h_{part}", [128, RPE_LAYERS, HALVES, CH], F32R) for part in ("high", "low")]
        w_out = [T.sb(f"w_out_{part}", [128, HALVES, WIDE], F32R) for part in ("high", "low")]
        bias = T.sb("bias", [128, RPE_LAYERS + 1, HALVES])
        out_bias = T.sb("out_bias", [TAPS, WIDE])
        row_taps = T.sb("row_taps", [TAPS, ROWS])
        mean_ch = T.sb("mean_ch", [128, 128])
        one = T.sb("one", [1, 1])
        coords = T.sb("coords", [2, TAPS_PAD * TAPS])
        t = [T.sb(f"t{u}", [128, HALVES, RPE_CHUNK]) for u in range(2)]
        square = [T.sb(f"square{u}", [128, HALVES, RPE_CHUNK]) for u in range(2)]
        rect = [[T.sb(f"rect{u}_{part}", [128, HALVES, RPE_CHUNK], F32R) for part in ("high", "low")] for u in range(2)]
        root = [T.sb(f"root{u}", [128, RPE_CHUNK]) for u in range(2)]
        scale = [T.sb(f"scale{u}", [128, RPE_CHUNK]) for u in range(2)]
        inv = [T.sb(f"inv{u}", [TAPS, RPE_ROWS]) for u in range(2)]
        coef = [T.sb(f"coef{i}", [TAPS, WIDE]) for i in range(2)]
        rows_out = [T.sb(f"rows_out{u}", [ROWS, RPE_ROWS, WIDE]) for u in range(2)]
        t_ps = [[T.ps(f"t{u}{h}", [128, 512]) for h in range(2)] for u in range(2)]
        ms_ps = [T.ps(f"ms{u}", [128, 512]) for u in range(2)]
        row_ps = [T.ps(f"row{i}", [128, 512]) for i in range(2)]
        COLUMN = 448

        (consts_in, high_consts, low_consts, layer_done, t_ready, high_ready, low_ready, squared, mean_done, rooted,
         scale_ready, column_mm, inverted, coef_mm, coef_done, row_mm, row_out) = (T.sem(n) for n in (
             "consts_in", "high_consts", "low_consts", "layer_done", "t_ready", "high_ready", "low_ready", "squared",
             "mean_done", "rooted", "scale_ready", "column_mm", "inverted", "coef_mm", "coef_done", "row_mm", "row_out"))
        stored = [T.sem(f"stored{u}") for u in range(2)]
        STEPS = TAPS_PAD // RPE_ROWS // 2
        LAYERS = RPE_LAYERS + 1
        PER, TAIL = 2 * LAYERS, 2 * RPE_ROWS
        loads = [(w_in, "rpe_in"), (raw_h, "rpe_h"), (raw_out, "rpe_out"), (bias, "rpe_bias"), (out_bias, "rpe_out_b"),
                 (row_taps, "row_taps"), (mean_ch, "mean_ch"), (coords, "coords")]
        with nc.Block() as block:
            @block.sync
            def _(sp):
                for tile, name in loads:
                    sp.dma_start(tile[:], d[name]).then_inc(consts_in, 16)
                sp.dma_start(one[:], d["ones"][:1, :1]).then_inc(consts_in, 16)
                with sp.Fori(0, STEPS) as s:
                    for u in range(2):
                        sp.wait_ge(row_out, s * TAIL + RPE_ROWS * (u + 1))
                        sp.dma_start(d["kern_rows"][:, bass.ds((s * 2 + u) * RPE_ROWS, RPE_ROWS), :],
                                     rows_out[u][:]).then_inc(stored[u], 16)
                for u in range(2):
                    sp.wait_ge(stored[u], 16 * STEPS)

            @block.tensor
            def _(pe):
                pe.wait_ge(consts_in, 16 * (len(loads) + 1))
                pe.wait_ge(low_consts, 2)
                with pe.Fori(0, STEPS) as s:
                    def mean(n):
                        u = n % 2
                        pe.wait_ge(squared, s * PER + n + 1)
                        if n >= 2:
                            pe.wait_ge(rooted, s * PER + n - 1)
                        for h in range(HALVES):
                            last = nc.tensor.matmul(ms_ps[u][:, :RPE_CHUNK], mean_ch[:], square[u][:, h, :],
                                                    start=h == 0, stop=h == HALVES - 1)
                        last.then_inc(mean_done, 1)

                    for layer in range(LAYERS):
                        for u in range(2):
                            n = 2 * layer + u
                            if layer:
                                mean(n - 2)
                                pe.wait_ge(low_ready, s * PER + n - 1)
                            else:
                                pe.wait_ge(coef_done, s * TAIL)
                            for h in range(HALVES):
                                if layer == 0:
                                    last = nc.tensor.matmul(t_ps[u][h][:, :RPE_CHUNK], w_in[:, h * 128:(h + 1) * 128],
                                                            coords[:, bass.ds((s * 2 + u) * RPE_CHUNK, RPE_CHUNK)],
                                                            start=True, stop=True)
                                else:
                                    for k in range(HALVES):
                                        last = product(nc, t_ps[u][h][:, :RPE_CHUNK],
                                                       [w[:, layer - 1, k, h * 128:(h + 1) * 128] for w in w_h],
                                                       [part[:, k, :] for part in rect[u]], start=k == 0, stop=k == HALVES - 1)
                            last.then_inc(layer_done, 1)

                    def row_pass(m):
                        pe.wait_ge(coef_done, s * TAIL + m + 1)
                        pe.wait_ge(row_out, s * TAIL + max(m - 1, 0))
                        nc.tensor.matmul(row_ps[m % 2][:ROWS, :], row_taps[:], coef[m % 2][:],
                                         start=True, stop=True).then_inc(row_mm, 1)

                    mean(PER - 2)
                    for u in range(2):
                        pe.wait_ge(low_ready, s * PER + PER - 1 + u)
                        for r in range(RPE_ROWS):
                            m = RPE_ROWS * u + r
                            if r >= 2:
                                pe.wait_ge(coef_done, s * TAIL + m - 1)
                            for k in range(HALVES):
                                last = product(nc, t_ps[u][r % 2][:TAPS, :],
                                               [part[:, k, r * TAPS:(r + 1) * TAPS] for part in rect[u]],
                                               [w[:, k, :] for w in w_out], start=k == 0, stop=k == HALVES - 1)
                            last.then_inc(coef_mm, 1)
                            if r == 0:
                                if u == 0:
                                    mean(PER - 1)
                                pe.wait_ge(scale_ready, s * PER + PER - 1 + u)
                                for i in range(RPE_ROWS):
                                    last = nc.tensor.matmul(ms_ps[u][:TAPS, COLUMN + i:COLUMN + i + 1],
                                                            scale[u][:1, i * TAPS:(i + 1) * TAPS], one[:], start=True, stop=True)
                                last.then_inc(column_mm, 1)
                            if m:
                                row_pass(m - 1)
                    row_pass(TAIL - 1)

            @block.scalar
            def _(act):
                act.wait_ge(consts_in, 16 * (len(loads) + 1))
                nc.scalar.activation(w_h[0][:], raw_h[:], ACT.Copy).then_inc(high_consts, 1)
                nc.scalar.activation(w_out[0][:], raw_out[:], ACT.Copy).then_inc(high_consts, 1)
                with act.Fori(0, STEPS) as s:
                    def roots(n):
                        act.wait_ge(mean_done, s * PER + n + 1)
                        nc.scalar.activation(root[n % 2][:], ms_ps[n % 2][:, :RPE_CHUNK], ACT.Sqrt).then_inc(rooted, 1)

                    for layer in range(LAYERS):
                        for u in range(2):
                            n = 2 * layer + u
                            act.wait_ge(t_ready, s * PER + n + 1)
                            nc.scalar.activation(rect[u][0][:], t[u][:], ACT.Relu).then_inc(high_ready, 1)
                            nc.scalar.activation(square[u][:], t[u][:], ACT.Square).then_inc(squared, 1)
                            if n:
                                roots(n - 1)
                    roots(PER - 1)
                    for m in range(TAIL):
                        u, r = divmod(m, RPE_ROWS)
                        act.wait_ge(row_mm, s * TAIL + m + 1)
                        if r == 0:
                            act.wait_ge(stored[u], s * 16)
                        nc.scalar.activation(rows_out[u][:, r, :], row_ps[m % 2][:ROWS, :], ACT.Copy).then_inc(row_out, 1)

            @block.vector
            def _(dve):
                dve.wait_ge(consts_in, 16 * (len(loads) + 1))
                for i, (raw, w) in enumerate(((raw_h, w_h), (raw_out, w_out))):
                    dve.wait_ge(high_consts, i + 1)
                    nc.vector.tensor_tensor(w[1][:], raw[:], w[0][:].bitcast(F32), ALU.subtract).then_inc(low_consts, 1)
                with dve.Fori(0, STEPS) as s:
                    def next_scale(n):
                        u = n % 2
                        dve.wait_ge(rooted, s * PER + n + 1)
                        dve.wait_ge(t_ready, s * PER + n + 1)
                        if n < 2:
                            dve.wait_ge(column_mm, s * 2)
                            nc.vector.tensor_scalar(scale[u][:], root[u][:], RMS_EPS, None, ALU.add).then_inc(scale_ready, 1)
                        else:
                            nc.vector.scalar_tensor_tensor(out=scale[u][:], in0=scale[u][:], scalar=RMS_EPS, in1=root[u][:],
                                                           op0=ALU.mult, op1=ALU.add).then_inc(scale_ready, 1)

                    for layer in range(LAYERS):
                        for u in range(2):
                            n = 2 * layer + u
                            if layer:
                                next_scale(n - 2)
                                dve.wait_ge(scale_ready, s * PER + n - 1)
                            dve.wait_ge(layer_done, s * PER + n + 1)
                            dve.wait_ge(squared, s * PER + max(n - 1, 0))
                            dve.wait_ge(low_ready, s * PER + max(n - 1, 0))
                            for h in range(HALVES):
                                if layer == 0:
                                    last = nc.vector.tensor_scalar(t[u][:, h, :], t_ps[u][h][:, :RPE_CHUNK],
                                                                   bias[:, 0, h:h + 1], None, ALU.add)
                                else:
                                    last = nc.vector.scalar_tensor_tensor(
                                        out=t[u][:, h, :], in0=scale[u][:], scalar=bias[:, layer, h:h + 1],
                                        in1=t_ps[u][h][:, :RPE_CHUNK], op0=ALU.mult, op1=ALU.add)
                            last.then_inc(t_ready, 1)
                            dve.wait_ge(t_ready, s * PER + n + 1)
                            dve.wait_ge(high_ready, s * PER + n + 1)
                            nc.vector.scalar_tensor_tensor(out=rect[u][1][:], in0=t[u][:], scalar=0.0,
                                                           in1=rect[u][0][:].bitcast(F32), op0=ALU.max, op1=ALU.subtract
                                                           ).then_inc(low_ready, 1)
                    next_scale(PER - 2)
                    next_scale(PER - 1)
                    for m in range(TAIL):
                        u, r = divmod(m, RPE_ROWS)
                        if r == 0:
                            dve.wait_ge(column_mm, s * 2 + u + 1)
                            nc.vector.reciprocal(inv[u][:], ms_ps[u][:TAPS, COLUMN:COLUMN + RPE_ROWS]).then_inc(inverted, 1)
                            dve.wait_ge(inverted, s * 2 + u + 1)
                        dve.wait_ge(coef_mm, s * TAIL + m + 1)
                        dve.wait_ge(row_mm, s * TAIL + max(m - 1, 0))
                        nc.vector.scalar_tensor_tensor(out=coef[m % 2][:], in0=t_ps[u][r % 2][:TAPS, :], scalar=inv[u][:, r:r + 1],
                                                       in1=out_bias[:], op0=ALU.mult, op1=ALU.add).then_inc(coef_done, 1)


def columns_phase(nc, d):
    with Tools(nc, "co") as T:
        raw_fwd = T.sb("raw_fwd", [2 * SIDE, 2, POINTS])
        raw_taps = T.sb("raw_taps", [TAPS, 3, POINTS])
        parts = ("high", "low")
        col_fwd = [T.sb(f"col_fwd_{part}", [2 * SIDE, 2, POINTS], F32R) for part in parts]
        col_taps = [T.sb(f"col_taps_{part}", [TAPS, 3, POINTS], F32R) for part in parts]
        col_inv = T.sb("col_inv", [POINTS, 2, 2 * SIDE])
        taps_in = T.sb("taps_in", [TAPS, 2, WIDE])
        taps = [T.sb(f"taps_{part}", [TAPS, 2, WIDE], F32R) for part in parts]
        v_in = T.sb("v_in", [2 * SIDE, BATCH, WIDE])
        v = [T.sb(f"v_{part}", [2 * SIDE, BATCH, WIDE], F32R) for part in parts]
        y_out = T.sb("y_out", [2 * SIDE, BATCH, WIDE])
        spec = [T.sb(f"spec{i}", [POINTS, 3 * WIDE]) for i in range(2)]
        direct = [T.sb(f"direct{i}", [POINTS, 2 * WIDE]) for i in range(2)]
        cross = [T.sb(f"cross{i}", [POINTS, 2 * WIDE]) for i in range(2)]
        prod = [T.sb(f"prod{i}", [POINTS, 2 * WIDE]) for i in range(2)]
        v_ps = [T.ps(f"v{i}", [128, 2 * WIDE]) for i in range(2)]
        taps_ps = T.ps("taps", [128, 2 * WIDE])
        y_ps = [T.ps(f"y{i}", [128, WIDE]) for i in range(2)]
        names = ("consts_in", "high_consts", "low_consts", "taps_loaded", "high_taps", "low_taps", "high_v", "low_v", "taps_mm", "spec_ready", "fwd_mm", "multiplied", "combined", "inv_mm", "y_ready")
        (consts_in, high_consts, low_consts, taps_loaded, high_taps, low_taps, high_v, low_v, taps_mm, spec_ready, fwd_mm,
         multiplied, combined, inv_mm, y_ready) = (T.sem(n) for n in names)
        PAIRS = BATCH // 2
        LAG = 2
        v_loaded = [T.sem(f"v_loaded{i}") for i in range(PAIRS)]
        y_stored = [T.sem(f"y_stored{i}") for i in range(PAIRS)]
        HIGH_AHEAD, LOW_AHEAD = 3, 2
        loads = [(raw_fwd, "col_fwd"), (raw_taps, "col_taps"), (col_inv, "col_inv")]
        splits = [(raw_fwd, col_fwd), (raw_taps, col_taps)]

        SLOTS = 2

        def buffer_free(eng, sem, n):
            eng.wait_ge(sem, n + 1)

        def done(eng, sem, n):
            eng.wait_ge(sem, SLOTS + n + 1)

        def pair_ahead(k, b, more, ahead):
            pair = b // 2 + ahead
            if b % 2 == 0 and pair < PAIRS:
                return k, pair
            return (k + 1, pair - PAIRS) if b % 2 == 0 and more else None

        def load_taps(eng, k):
            for part in range(2):
                eng.dma_start(taps_in[:, part, :], d["kern_rows"][k + FREQ * part, 0:TAPS, :]).then_inc(taps_loaded, 16)

        def load_v(eng, k, pair):
            for part in range(2):
                eng.dma_start(v_in[part * SIDE:(part + 1) * SIDE, 2 * pair:2 * pair + 2, :],
                              d["v_rows"][k + FREQ * part, 2 * pair:2 * pair + 2, :, :].rearrange("b i c -> i b c")
                              ).then_inc(v_loaded[pair], 16)

        def store_y(eng, k, pair):
            for part in range(2):
                eng.dma_start(d["y_rows"][k + FREQ * part, 2 * pair:2 * pair + 2, :, :].rearrange("b i c -> i b c"),
                              y_out[part * SIDE:(part + 1) * SIDE, 2 * pair:2 * pair + 2, :]).then_inc(y_stored[pair], 16)

        with nc.Block() as block:
            @block.sync
            def _(sp):
                for tile, name in loads:
                    sp.dma_start(tile[:], d[name]).then_inc(consts_in, 16)
                load_taps(sp, 0)
                for pair in range(PAIRS):
                    load_v(sp, 0, pair)

                def step(k, more):
                    if more:
                        sp.wait_ge(low_taps, k + 1)
                        load_taps(sp, k + 1)
                    for pair in range(PAIRS):
                        if more:
                            sp.wait_ge(low_v, k * PAIRS + pair + 1)
                            load_v(sp, k + 1, pair)
                        done(sp, y_ready, k * BATCH + 2 * pair + 1)
                        store_y(sp, k, pair)

                with sp.Fori(0, FREQ // 2) as s:
                    for i in range(2):
                        step(s * 2 + i, True)
                step(FREQ - 1, False)
                for pair in range(PAIRS):
                    sp.wait_ge(y_stored[pair], 32 * FREQ)

            @block.tensor
            def _(pe):
                pe.wait_ge(consts_in, 16 * len(loads))
                pe.wait_ge(low_consts, len(splits))

                def spectrum(k):
                    pe.wait_ge(low_taps, k + 1)
                    pe.wait_ge(spec_ready, k)
                    for out, (real, imag) in enumerate(((0, 1), (2, 0))):
                        for part, matrix in enumerate((real, imag)):
                            last = product(nc, taps_ps[:POINTS, bass.ts(out, WIDE)], [w[:, matrix, :] for w in col_taps],
                                           [x[:, part, :] for x in taps], start=part == 0, stop=part == 1)
                    last.then_inc(taps_mm, 1)

                def forward(k, b):
                    n = k * BATCH + b
                    pe.wait_ge(low_v, k * PAIRS + b // 2 + 1)
                    buffer_free(pe, multiplied, n)
                    for out in range(2):
                        last = product(nc, v_ps[b % 2][:POINTS, bass.ts(out, WIDE)], [w[:, out, :] for w in col_fwd],
                                       [x[:, b, :] for x in v], start=True, stop=True)
                    last.then_inc(fwd_mm, 1)

                def inverse(k, b):
                    n = k * BATCH + b
                    done(pe, combined, n)
                    buffer_free(pe, y_ready, n)
                    nc.tensor.matmul(y_ps[b % 2][:2 * SIDE, :], col_inv[:, 0, :], prod[b % 2][:, :WIDE], start=True, stop=False)
                    nc.tensor.matmul(y_ps[b % 2][:2 * SIDE, :], col_inv[:, 1, :], prod[b % 2][:, WIDE:],
                                     start=False, stop=True).then_inc(inv_mm, 1)

                def step(k, more):
                    for b in range(LAG, BATCH):
                        if b == BATCH // 2 and more:
                            spectrum(k + 1)
                        forward(k, b)
                        inverse(k, b - LAG)
                    for b in range(LAG):
                        if more:
                            forward(k + 1, b)
                        inverse(k, BATCH - LAG + b)

                pe.sem_inc(inv_mm, SLOTS)
                spectrum(0)
                for b in range(LAG):
                    forward(0, b)
                with pe.Fori(0, FREQ // 2) as s:
                    for i in range(2):
                        step(s * 2 + i, True)
                step(FREQ - 1, False)

            @block.scalar
            def _(act):
                def split_v(k, pair):
                    act.wait_ge(v_loaded[pair], k * 32 + 32)
                    images = slice(2 * pair, 2 * pair + 2)
                    nc.scalar.activation(v[0][:, images, :], v_in[:, images, :], ACT.Copy).then_inc(high_v, 1)

                def split_taps(k):
                    act.wait_ge(taps_loaded, k * 32 + 32)
                    nc.scalar.activation(taps[0][:], taps_in[:], ACT.Copy).then_inc(high_taps, 1)

                def spectrum(k, i):
                    act.wait_ge(taps_mm, k + 1)
                    for col, part in ((0, 0), (1, 1), (2, 0)):
                        last = nc.scalar.activation(spec[i][:, bass.ts(col, WIDE)], taps_ps[:POINTS, bass.ts(part, WIDE)], ACT.Copy)
                    last.then_inc(spec_ready, 1)

                def step(k, i, more):
                    for b in range(BATCH):
                        if b == 0 and more:
                            split_taps(k + 1)
                        if b == BATCH // 2 and more:
                            spectrum(k + 1, 1 - i)
                        ahead = pair_ahead(k, b, more, HIGH_AHEAD)
                        if ahead:
                            split_v(*ahead)
                        done(act, inv_mm, k * BATCH + b)
                        if b % 2 == 0:
                            act.wait_ge(y_stored[b // 2], k * 32)
                        nc.scalar.activation(y_out[:, b, :], y_ps[b % 2][:2 * SIDE, :], ACT.Copy).then_inc(y_ready, 1)

                act.sem_inc(y_ready, SLOTS)
                act.wait_ge(consts_in, 16 * len(loads))
                for raw, split in splits:
                    nc.scalar.activation(split[0][:], raw[:], ACT.Copy).then_inc(high_consts, 1)
                split_taps(0)
                for pair in range(HIGH_AHEAD):
                    split_v(0, pair)
                spectrum(0, 0)
                with act.Fori(0, FREQ // 2) as s:
                    for i in range(2):
                        step(s * 2 + i, i, True)
                step(FREQ - 1, 0, False)

            @block.vector
            def _(dve):
                def split_v(k, pair):
                    dve.wait_ge(high_v, k * PAIRS + pair + 1)
                    images = slice(2 * pair, 2 * pair + 2)
                    nc.vector.tensor_tensor(v[1][:, images, :], v_in[:, images, :], v[0][:, images, :].bitcast(F32),
                                            ALU.subtract).then_inc(low_v, 1)

                def split_taps(k):
                    dve.wait_ge(high_taps, k + 1)
                    nc.vector.tensor_tensor(taps[1][:], taps_in[:], taps[0][:].bitcast(F32), ALU.subtract).then_inc(low_taps, 1)

                dve.sem_inc(multiplied, SLOTS)
                for i, (raw, split) in enumerate(splits):
                    dve.wait_ge(high_consts, i + 1)
                    nc.vector.tensor_tensor(split[1][:], raw[:], split[0][:].bitcast(F32), ALU.subtract).then_inc(low_consts, 1)
                split_taps(0)
                for pair in range(LOW_AHEAD):
                    split_v(0, pair)

                def step(k, i, more):
                    dve.wait_ge(spec_ready, k + 1)
                    for b in range(BATCH):
                        dve.wait_ge(fwd_mm, k * BATCH + b + 1)
                        buffer_free(dve, combined, k * BATCH + b)
                        nc.vector.tensor_tensor(direct[b % 2][:], v_ps[b % 2][:POINTS, :], spec[i][:, :2 * WIDE], ALU.mult)
                        nc.vector.tensor_tensor(cross[b % 2][:], v_ps[b % 2][:POINTS, :], spec[i][:, WIDE:],
                                                ALU.mult).then_inc(multiplied, 1)
                        if b == 2 and more:
                            split_taps(k + 1)
                        ahead = pair_ahead(k, b, more, LOW_AHEAD)
                        if ahead:
                            split_v(*ahead)

                with dve.Fori(0, FREQ // 2) as s:
                    for i in range(2):
                        step(s * 2 + i, i, True)
                step(FREQ - 1, 0, False)

            @block.gpsimd
            def _(pool):
                pool.sem_inc(combined, SLOTS)

                def step(k):
                    for b in range(BATCH):
                        done(pool, multiplied, k * BATCH + b)
                        buffer_free(pool, inv_mm, k * BATCH + b)
                        nc.gpsimd.tensor_tensor(prod[b % 2][:, :WIDE], direct[b % 2][:, :WIDE], direct[b % 2][:, WIDE:], ALU.subtract)
                        nc.gpsimd.tensor_tensor(prod[b % 2][:, WIDE:], cross[b % 2][:, :WIDE], cross[b % 2][:, WIDE:],
                                                ALU.add).then_inc(combined, 1)

                with pool.Fori(0, FREQ // 2) as s:
                    for i in range(2):
                        step(s * 2 + i)
                step(FREQ - 1)


def stats_phase(nc, d):
    with Tools(nc, "st") as T:
        ident, group_mean = T.sb("ident", [128, 128]), T.sb("group_mean", [128, 128])
        x_in = [T.sb(f"x_in{i}", [TILE, TILES, CH]) for i in range(CHUNKS)]
        stats = T.sb("stats", [128, HALVES, CHUNKS, 6])
        moments = T.sb("moments", [128, HALVES, 2])
        off, off2 = T.sb("off", [128, HALVES]), T.sb("off2", [128, HALVES])
        var, root, scale, shift = (T.sb(n, [128, HALVES]) for n in ("var", "root", "scale", "shift"))
        rows = T.sb("rows", [128, 2 * CH])
        x_ps = [[T.ps(f"x{i}{h}", [128, 512]) for h in range(2)] for i in range(2)]
        group_ps, row_ps = T.ps("group", [128, 512]), T.ps("row", [128, 512])
        consts_in, transposed, measured, chain, group_mm, rooted, row_mm, rows_made, rows_stored = (
            T.sem(n) for n in ("consts_in", "transposed", "measured", "chain", "group_mm", "rooted", "row_mm",
                               "rows_made", "rows_stored"))
        seen = T.sem("seen")
        x_loaded = [T.sem(f"x_loaded{i}") for i in range(CHUNKS)]
        LINKS = 8

        with nc.Block() as block:
            @block.sync
            def _(sp):
                sp.dma_start(ident[:], d["ident"]).then_inc(consts_in, 16)
                sp.dma_start(group_mean[:], d["group_mean"]).then_inc(consts_in, 16)
                for j in range(CHUNKS):
                    sp.dma_start(x_in[j][:], d["x_tiles"][j]).then_inc(x_loaded[j], 16)
                with sp.Fori(1, BATCH) as b:
                    for j in range(CHUNKS):
                        sp.wait_ge(transposed, (b - 1) * CHUNKS + j + 1)
                        sp.dma_start(x_in[j][:], d["x_tiles"][b * CHUNKS + j]).then_inc(x_loaded[j], 16)

            @block.tensor
            def _(pe):
                pe.wait_ge(consts_in, 32)
                with pe.Fori(0, BATCH) as b:
                    for j in range(CHUNKS):
                        pe.wait_ge(x_loaded[j], b * 16 + 16)
                        pe.wait_ge(measured, b * CHUNKS + max(j - 1, 0))
                        for t in range(TILES):
                            for h in range(HALVES):
                                last = nc.tensor.transpose(x_ps[j % 2][h][:, t * TILE:(t + 1) * TILE],
                                                           x_in[j][:, t, h * 128:(h + 1) * 128], ident[:TILE, :TILE])
                        last.then_inc(transposed, 1)
                    pe.wait_ge(chain, b * LINKS + 1)
                    nc.tensor.matmul(group_ps[:, 0:4], group_mean[:], moments[:].rearrange("p h m -> p (h m)"),
                                     start=True, stop=True).then_inc(group_mm, 1)
                    pe.wait_ge(chain, b * LINKS + 3)
                    nc.tensor.matmul(group_ps[:, 4:6], group_mean[:], off2[:], start=True, stop=True).then_inc(group_mm, 1)
                    pe.wait_ge(chain, b * LINKS + 8)
                    for i, col in enumerate((scale, shift)):
                        for h in range(HALVES):
                            at = (i * HALVES + h) * 128
                            last = nc.tensor.matmul(row_ps[:, at:at + 128], col[:, h:h + 1].to_broadcast([128, 128]), ident[:],
                                                    start=True, stop=True)
                    last.then_inc(row_mm, 1)

            @block.scalar
            def _(act):
                with act.Fori(0, BATCH) as b:
                    act.wait_ge(chain, b * LINKS + 5)
                    nc.scalar.activation(root[:], var[:], ACT.Sqrt).then_inc(rooted, 1)
                    act.wait_ge(rows_made, b + 1)
                    for j in range(CHUNKS):
                        act.dma_start(d["gn_rows"][b * CHUNKS + j], rows[0:1, :]).then_inc(rows_stored, 16)
                act.wait_ge(rows_stored, 16 * BATCH * CHUNKS)

            @block.vector
            def _(dve):
                with dve.Fori(0, BATCH) as b:
                    for j in range(CHUNKS):
                        dve.wait_ge(transposed, b * CHUNKS + j + 1)
                        for h in range(HALVES):
                            last = nc.vector.bn_stats(stats[:, h, j, :], x_ps[j % 2][h][:, :CHUNK])
                        last.then_inc(measured, 1)
                    dve.wait_ge(measured, b * CHUNKS + CHUNKS)
                    dve.sem_inc(seen, 1)
                    nc.vector.bn_aggr(moments[:, 0, :], stats[:, 0, :, :])
                    nc.vector.bn_aggr(moments[:, 1, :], stats[:, 1, :, :]).then_inc(chain, 1)
                    group = group_ps[:, 0:4].rearrange("p (h m) -> p h m", m=2)
                    dve.wait_ge(group_mm, b * 2 + 1)
                    nc.vector.tensor_tensor(off[:], moments[:, :, 0], group[:, :, 0], ALU.subtract).then_inc(chain, 1)
                    dve.wait_ge(chain, b * LINKS + 2)
                    nc.vector.tensor_tensor(off2[:], off[:], off[:], ALU.mult).then_inc(chain, 1)
                    dve.wait_ge(group_mm, b * 2 + 2)
                    nc.vector.tensor_scalar(var[:], group_ps[:, 4:6], GN_EPS, None, ALU.add).then_inc(chain, 1)
                    dve.wait_ge(chain, b * LINKS + 4)
                    nc.vector.tensor_tensor(var[:], var[:], group[:, :, 1], ALU.add).then_inc(chain, 1)
                    dve.wait_ge(rooted, b + 1)
                    nc.vector.reciprocal(scale[:], root[:]).then_inc(chain, 1)
                    dve.wait_ge(chain, b * LINKS + 6)
                    nc.vector.tensor_tensor(shift[:], scale[:], group[:, :, 0], ALU.mult).then_inc(chain, 1)
                    dve.wait_ge(chain, b * LINKS + 7)
                    nc.vector.tensor_scalar(shift[:], shift[:], -1.0, None, ALU.mult).then_inc(chain, 1)
                    dve.wait_ge(row_mm, b + 1)
                    dve.wait_ge(rows_stored, b * 16 * CHUNKS)
                    nc.vector.tensor_copy(rows[:], row_ps[:, :2 * CH]).then_inc(rows_made, 1)


def project_phase(nc, d):
    with Tools(nc, "pr") as T:
        w_v = T.sb("w_v", [128, HALVES, WIDE])
        v_bias = T.sb("v_bias", [TILE, WIDE])
        ident = T.sb("ident", [128, 128])
        row_fwd = T.sb("row_fwd", [TILE, 2, ROWS])
        x_in = [T.sb(f"x_in{u}", [TILE, TILES, CH]) for u in range(2)]
        gn = [T.sb(f"gn{u}", [TILE, 2, CH]) for u in range(2)]
        gx = [T.sb(f"gx{u}", [TILE, TILES, CH]) for u in range(2)]
        xn = [T.sb(f"xn{u}", [TILE, TILES, CH]) for u in range(2)]
        junk = T.sb("junk", [TILE, TILES, CH])
        ssum, root, guarded, inv = ([T.sb(f"{n}{u}", [TILE, TILES]) for u in range(2)] for n in ("ssum", "root", "guarded", "inv"))
        xn_t = [T.sb(f"xn_t{u}", [128, HALVES, CHUNK]) for u in range(2)]
        v_pre = [T.sb(f"v_pre{i}", [TILE, WIDE]) for i in range(2)]
        v = [T.sb(f"v{i}", [TILE, WIDE]) for i in range(2)]
        rows_out = [T.sb(f"rows_out{u}", [ROWS, CHUNK_ROWS, WIDE]) for u in range(2)]
        xt_ps = [T.ps(f"xt{h}", [128, 512]) for h in range(2)]
        v_ps = [T.ps(f"v{i}", [128, 512]) for i in range(2)]
        row_ps = [[T.ps(f"row{i}{r}", [128, 512]) for r in range(2)] for i in range(2)]
        (consts_in, scaled, gx_ready, squared, rooted, eps_added, inverted, xn_ready, xt_mm, xt0_ready, xt1_ready, v_mm, biased,
         v_ready, row_mm, row0_out, row1_out) = (T.sem(n) for n in (
             "consts_in", "scaled", "gx_ready", "squared", "rooted", "eps_added", "inverted", "xn_ready", "xt_mm", "xt0_ready",
             "xt1_ready", "v_mm", "biased", "v_ready", "row_mm", "row0_out", "row1_out"))
        loaded = [T.sem(f"loaded{u}") for u in range(2)]
        xn_stored = [T.sem(f"xn_stored{u}") for u in range(2)]
        rows_stored = [T.sem(f"rows_stored{u}") for u in range(2)]
        ALL = BATCH * CHUNKS
        loads = [(w_v, "w_v"), (v_bias, "v_bias"), (ident, "ident"), (row_fwd, "row_fwd")]

        def following(s, u):
            return (s, 1) if u == 0 else (s + 1, 0)

        def all_steps(eng, front, step):
            front(0, 0)
            with eng.Fori(0, ALL // 2 - 1) as s:
                for u in range(2):
                    step(s, u, following(s, u))
            step(ALL // 2 - 1, 0, (ALL // 2 - 1, 1))
            step(ALL // 2 - 1, 1, None)

        with nc.Block() as block:
            @block.sync
            def _(sp):
                for tile, name in loads:
                    sp.dma_start(tile[:], d[name]).then_inc(consts_in, 16)
                with sp.Fori(0, ALL // 2) as s:
                    for u in range(2):
                        g = s * 2 + u
                        sp.wait_ge(gx_ready, s * 2)
                        sp.dma_start(x_in[u][:], d["x_tiles"][g]).then_inc(loaded[u], 16)
                        sp.dma_start(gn[u][:].rearrange("p a c -> p (a c)"), d["gn_rows"][g].to_broadcast([TILE, 2 * CH])
                                     ).then_inc(loaded[u], 16)

            @block.gpsimd
            def _(pool):
                with pool.Fori(0, ALL // 2) as s:
                    for u in range(2):
                        g = s * 2 + u
                        pool.wait_ge(xt0_ready, g + 1)
                        pool.wait_ge(xt1_ready, g + 1)
                        pool.dma_start(d["xn_t"][g], xn_t[u][:]).then_inc(xn_stored[u], 16)
                        pool.wait_ge(row0_out, (g + 1) * TILES)
                        pool.wait_ge(row1_out, (g + 1) * TILES)
                        pool.dma_start(rows_of_chunk(d["v_rows"], g), rows_out[u][:]).then_inc(rows_stored[u], 16)
                for u in range(2):
                    pool.wait_ge(xn_stored[u], 16 * (ALL // 2))
                    pool.wait_ge(rows_stored[u], 16 * (ALL // 2))

            @block.tensor
            def _(pe):
                pe.wait_ge(consts_in, 16 * len(loads))

                def front(s, u):
                    g = 2 * s + u
                    pe.wait_ge(xn_ready, g + 1)
                    pe.wait_ge(xt0_ready, g)
                    pe.wait_ge(xt1_ready, g)
                    for h in range(HALVES):
                        for t in range(TILES):
                            last = nc.tensor.transpose(xt_ps[h][:, t * TILE:(t + 1) * TILE], xn[u][:, t, h * 128:(h + 1) * 128],
                                                       ident[:TILE, :TILE])
                    last.then_inc(xt_mm, 1)

                def step(s, u, after):
                    g = 2 * s + u

                    def row_pass(t):
                        pe.wait_ge(v_ready, g * TILES + t + 1)
                        pe.wait_ge(row0_out, g * TILES + max(t - 1, 0))
                        pe.wait_ge(row1_out, g * TILES + max(t - 1, 0))
                        for r in range(2):
                            last = nc.tensor.matmul(row_ps[t % 2][r][:ROWS, :], row_fwd[:, r, :], v[t % 2][:], start=True, stop=True)
                        last.then_inc(row_mm, 1)

                    pe.wait_ge(xt0_ready, g + 1)
                    pe.wait_ge(xt1_ready, g + 1)
                    for t in range(TILES):
                        pe.wait_ge(biased, g * TILES + max(t - 1, 0))
                        for h in range(HALVES):
                            last = nc.tensor.matmul(v_ps[t % 2][:TILE, :], xn_t[u][:, h, t * TILE:(t + 1) * TILE], w_v[:, h, :],
                                                    start=h == 0, stop=h == HALVES - 1)
                        last.then_inc(v_mm, 1)
                        if t:
                            row_pass(t - 1)
                    if after:
                        front(*after)
                    row_pass(TILES - 1)

                all_steps(pe, front, step)

            @block.scalar
            def _(act):
                act.wait_ge(consts_in, 16 * len(loads))

                def squares(s, u):
                    g = 2 * s + u
                    act.wait_ge(gx_ready, g + 1)
                    act.wait_ge(rooted, 2 * s)
                    for t in range(TILES):
                        last = nc.scalar.activation(junk[:, t, :], gx[u][:, t, :], ACT.Square, accum_out=ssum[u][:, t:t + 1])
                    last.then_inc(squared, 1)
                    act.wait_ge(squared, g + 1)
                    nc.scalar.activation(root[u][:], ssum[u][:], ACT.Sqrt, scale=1.0 / CH).then_inc(rooted, 1)

                def scale_rows(s, u):
                    g = 2 * s + u
                    act.wait_ge(inverted, g + 1)
                    act.wait_ge(xt_mm, g)
                    for t in range(TILES):
                        last = nc.scalar.activation(xn[u][:, t, :], gx[u][:, t, :], ACT.Copy, scale=inv[u][:, t:t + 1])
                    last.then_inc(xn_ready, 1)

                def take_xt(s, u):
                    g = 2 * s + u
                    act.wait_ge(xt_mm, g + 1)
                    act.wait_ge(xn_stored[u], s * 16)
                    act.wait_ge(v_mm, g * TILES)
                    nc.scalar.activation(xn_t[u][:, 0, :], xt_ps[0][:, :CHUNK], ACT.Copy).then_inc(xt0_ready, 1)

                def front(s, u):
                    squares(s, u)
                    scale_rows(s, u)
                    take_xt(s, u)

                def step(s, u, after):
                    g = 2 * s + u

                    def take_row(t):
                        act.wait_ge(row_mm, g * TILES + t + 1)
                        if t == 0:
                            act.wait_ge(rows_stored[u], s * 16)
                        nc.scalar.activation(rows_out[u][:, 2 * t, :], row_ps[t % 2][0][:ROWS, :], ACT.Copy).then_inc(row0_out, 1)

                    for t in range(TILES):
                        act.wait_ge(biased, g * TILES + t + 1)
                        act.wait_ge(row_mm, g * TILES + max(t - 1, 0))
                        nc.scalar.activation(v[t % 2][:], v_pre[t % 2][:], ACT.Silu).then_inc(v_ready, 1)
                        if t == 1 and after:
                            squares(*after)
                        if t:
                            take_row(t - 1)
                        if t == 2 and after:
                            scale_rows(*after)
                    if after:
                        take_xt(*after)
                    take_row(TILES - 1)

                all_steps(act, front, step)

            @block.vector
            def _(dve):
                dve.wait_ge(consts_in, 16 * len(loads))

                def normalise(s, u):
                    g = 2 * s + u
                    dve.wait_ge(loaded[u], s * 32 + 32)
                    dve.wait_ge(xn_ready, 2 * s)
                    nc.vector.tensor_tensor(gx[u][:], x_in[u][:], gn[u][:, 0:1, :].to_broadcast([TILE, TILES, CH]),
                                            ALU.mult).then_inc(scaled, 1)
                    dve.wait_ge(scaled, g + 1)
                    nc.vector.tensor_tensor(gx[u][:], gx[u][:], gn[u][:, 1:2, :].to_broadcast([TILE, TILES, CH]),
                                            ALU.add).then_inc(gx_ready, 1)

                def invert(s, u):
                    g = 2 * s + u
                    dve.wait_ge(rooted, g + 1)
                    nc.vector.tensor_scalar(guarded[u][:], root[u][:], RMS_EPS, None, ALU.add).then_inc(eps_added, 1)
                    dve.wait_ge(eps_added, g + 1)
                    nc.vector.reciprocal(inv[u][:], guarded[u][:]).then_inc(inverted, 1)

                def take_xt(s, u):
                    g = 2 * s + u
                    dve.wait_ge(xt_mm, g + 1)
                    dve.wait_ge(xn_stored[u], s * 16)
                    dve.wait_ge(v_mm, g * TILES)
                    nc.vector.tensor_copy(xn_t[u][:, 1, :], xt_ps[1][:, :CHUNK]).then_inc(xt1_ready, 1)

                def front(s, u):
                    normalise(s, u)
                    invert(s, u)
                    take_xt(s, u)

                def step(s, u, after):
                    g = 2 * s + u

                    def take_row(t):
                        dve.wait_ge(row_mm, g * TILES + t + 1)
                        if t == 0:
                            dve.wait_ge(rows_stored[u], s * 16)
                        nc.vector.tensor_copy(rows_out[u][:, 2 * t + 1, :], row_ps[t % 2][1][:ROWS, :]).then_inc(row1_out, 1)

                    for t in range(TILES):
                        dve.wait_ge(v_mm, g * TILES + t + 1)
                        dve.wait_ge(v_ready, g * TILES + max(t - 1, 0))
                        nc.vector.tensor_tensor(v_pre[t % 2][:], v_ps[t % 2][:TILE, :], v_bias[:], ALU.add).then_inc(biased, 1)
                        if t == 0 and after:
                            normalise(*after)
                        if t:
                            take_row(t - 1)
                        if t == 1 and after:
                            invert(*after)
                    if after:
                        take_xt(*after)
                    take_row(TILES - 1)

                all_steps(dve, front, step)


def mix_phase(nc, d):
    with Tools(nc, "mx") as T:
        w_u = T.sb("w_u", [128, HALVES, WIDE])
        u_bias = T.sb("u_bias", [128, WIDE // 128])
        w_o = T.sb("w_o", [128, WIDE // 128, CH])
        o_bias = T.sb("o_bias", [TILE, CH])
        row_inv = T.sb("row_inv", [ROWS, SIDE])
        ident = T.sb("ident", [128, 128])
        y_in = [T.sb(f"y_in{u}", [ROWS, CHUNK_ROWS, WIDE]) for u in range(2)]
        xn_t = [T.sb(f"xn_t{u}", [128, HALVES, CHUNK]) for u in range(2)]
        x_in = [T.sb(f"x_in{u}", [TILE, TILES, CH]) for u in range(2)]
        gn = [T.sb(f"gn{u}", [TILE, 2, CH]) for u in range(2)]
        scale1, shift1 = ([T.sb(f"{n}{u}", [TILE, CH]) for u in range(2)] for n in ("scale1", "shift1"))
        scaled = [T.sb(f"scaled{u}", [TILE, TILES, CH]) for u in range(2)]
        resid = [T.sb(f"resid{u}", [TILE, TILES, CH]) for u in range(2)]
        gate = [T.sb(f"gate{u}", [128, WIDE // 128, CHUNK]) for u in range(2)]
        mixed = [T.sb(f"mixed{u}", [128, WIDE // 128, CHUNK]) for u in range(2)]
        t1 = [T.sb(f"t1{u}", [TILE, TILES, CH]) for u in range(2)]
        stats = T.sb("stats", [TILE, TILES, 6])
        moments = [T.sb(f"moments{u}", [TILE, TILES, 2]) for u in range(2)]
        var, root, inv, shift = ([T.sb(f"{n}{u}", [TILE, TILES]) for u in range(2)] for n in ("var", "root", "inv", "shift"))
        n1 = [T.sb(f"n1{u}", [TILE, TILES, CH]) for u in range(2)]
        n1_t = [T.sb(f"n1_t{u}", [128, HALVES, CHUNK]) for u in range(2)]
        BLOCKS = WIDE // 128
        y_ps = [T.ps(f"y{c}", [128, 512]) for c in range(BLOCKS)]
        u_ps = [T.ps(f"u{i}", [128, 512]) for i in range(2)]
        o_ps = [T.ps(f"o{i}", [128, 512]) for i in range(2)]
        (consts_in, row_prep, scaled_x, resid_ready, u_mm, gate_ready, y_mm, mixed_ready, o_mm, t1_ready, measured, aggregated,
         var_ready, rooted, inverted, shift_ready, n1_ready, nt_mm, nt0_ready, nt1_ready) = (T.sem(n) for n in (
             "consts_in", "row_prep", "scaled_x", "resid_ready", "u_mm", "gate_ready", "y_mm", "mixed_ready", "o_mm", "t1_ready",
             "measured", "aggregated", "var_ready", "rooted", "inverted", "shift_ready", "n1_ready", "nt_mm", "nt0_ready",
             "nt1_ready"))
        xn_loaded, y_loaded, x_loaded, t1_stored, nt_stored = (
            [T.sem(f"{n}{u}") for u in range(2)] for n in ("xn_loaded", "y_loaded", "x_loaded", "t1_stored", "nt_stored"))
        seen = T.sem("seen")
        PAIRS = BATCH * CHUNKS // 2
        loads = [(w_u, "w_u"), (u_bias, "u_bias"), (w_o, "w_o"), (o_bias, "o_bias"), (row_inv, "row_inv"), (ident, "ident")]

        def all_steps(eng, step):
            last = PAIRS - 1
            step(None, (0, 0), (0, 1))
            step((0, 0), (0, 1), (1, 0))
            with eng.Fori(1, last) as s:
                step((s - 1, 1), (s, 0), (s, 1))
                step((s, 0), (s, 1), (s + 1, 0))
            step((last - 1, 1), (last, 0), (last, 1))
            step((last, 0), (last, 1), None)

        with nc.Block() as block:
            @block.sync
            def _(sp):
                for tile, name in loads:
                    sp.dma_start(tile[:], d[name]).then_inc(consts_in, 16)
                with sp.Fori(0, PAIRS) as s:
                    for u in range(2):
                        g = s * 2 + u
                        sp.wait_ge(u_mm, s * 2 * BLOCKS)
                        sp.dma_start(xn_t[u][:], d["xn_t"][g]).then_inc(xn_loaded[u], 16)
                        sp.wait_ge(resid_ready, s * 2)
                        sp.dma_start(x_in[u][:], d["x_tiles"][g]).then_inc(x_loaded[u], 16)
                        sp.dma_start(gn[u][:].rearrange("p a c -> p (a c)"), d["gn_rows"][g].to_broadcast([TILE, 2 * CH])
                                     ).then_inc(x_loaded[u], 16)
                        sp.wait_ge(y_mm, s * 2 * BLOCKS)
                        sp.dma_start(y_in[u][:], rows_of_chunk(d["y_rows"], g)).then_inc(y_loaded[u], 16)

            @block.gpsimd
            def _(pool):
                pool.wait_ge(consts_in, 16 * len(loads))
                with pool.Fori(0, PAIRS) as s:
                    for u in range(2):
                        g = s * 2 + u
                        pool.wait_ge(x_loaded[u], s * 32 + 32)
                        pool.wait_ge(t1_ready, s * 2 * 2)
                        nc.gpsimd.tensor_tensor(shift1[u][:], gn[u][:, 1, :], o_bias[:], ALU.add)
                        nc.gpsimd.tensor_scalar(scale1[u][:], gn[u][:, 0, :], 1.0, 1.0, ALU.mult, ALU.add).then_inc(row_prep, 1)
                        pool.wait_ge(row_prep, g + 1)
                        nc.gpsimd.tensor_tensor(scaled[u][:], x_in[u][:], scale1[u][:].unsqueeze(1).to_broadcast([TILE, TILES, CH]),
                                                ALU.mult).then_inc(scaled_x, 1)
                        pool.wait_ge(scaled_x, g + 1)
                        nc.gpsimd.tensor_tensor(resid[u][:], scaled[u][:], shift1[u][:].unsqueeze(1).to_broadcast([TILE, TILES, CH]),
                                                ALU.add).then_inc(resid_ready, 1)

            @block.tensor
            def _(pe):
                pe.wait_ge(consts_in, 16 * len(loads))

                def gate_mm(s, u, blocks):
                    g = 2 * s + u
                    pe.wait_ge(xn_loaded[u], s * 16 + 16)
                    for c in blocks:
                        pe.wait_ge(gate_ready, g * BLOCKS + max(c - 1, 0))
                        for h in range(HALVES):
                            last = nc.tensor.matmul(u_ps[c % 2][:, :CHUNK], w_u[:, h, c * 128:(c + 1) * 128], xn_t[u][:, h, :],
                                                    start=h == 0, stop=h == HALVES - 1)
                        last.then_inc(u_mm, 1)

                def inverse_rows(s, u, first=False):
                    g = 2 * s + u
                    pe.wait_ge(y_loaded[u], s * 16 + 16)
                    for c in range(BLOCKS):
                        if not first:
                            pe.wait_ge(mixed_ready, (g - 1) * BLOCKS + c + 1)
                        for r in range(CHUNK_ROWS):
                            last = nc.tensor.matmul(y_ps[c][:, r * SIDE:(r + 1) * SIDE], y_in[u][:, r, c * 128:(c + 1) * 128],
                                                    row_inv[:], start=True, stop=True)
                        last.then_inc(y_mm, 1)

                def transpose_norm(s, u):
                    g = 2 * s + u
                    pe.wait_ge(n1_ready, g + 1)
                    pe.wait_ge(t1_ready, 2 * g + 2)
                    for h in range(HALVES):
                        for t in range(TILES):
                            last = nc.tensor.transpose(o_ps[h][:, t * TILE:(t + 1) * TILE], n1[u][:, t, h * 128:(h + 1) * 128],
                                                       ident[:TILE, :TILE])
                    last.then_inc(nt_mm, 1)

                def output_mm(s, u):
                    g = 2 * s + u
                    pe.wait_ge(mixed_ready, (g + 1) * BLOCKS)
                    for pair in range(TILES // 2):
                        pe.wait_ge(nt0_ready if pair == 0 else nt1_ready, g)
                        for t in (2 * pair, 2 * pair + 1):
                            for c in range(BLOCKS):
                                last = nc.tensor.matmul(o_ps[pair][:TILE, (t % 2) * CH:(t % 2 + 1) * CH],
                                                        mixed[u][:, c, t * TILE:(t + 1) * TILE], w_o[:, c, :],
                                                        start=c == 0, stop=c == BLOCKS - 1)
                        last.then_inc(o_mm, 1)

                def step(before, now, after):
                    if after:
                        gate_mm(*after, range(0, 2))
                    if before:
                        transpose_norm(*before)
                    if after:
                        gate_mm(*after, range(2, BLOCKS))
                    output_mm(*now)
                    if after:
                        inverse_rows(*after)

                gate_mm(0, 0, range(BLOCKS))
                inverse_rows(0, 0, first=True)
                all_steps(pe, step)
                transpose_norm(PAIRS - 1, 1)

            @block.scalar
            def _(act):
                act.wait_ge(consts_in, 16 * len(loads))

                def gates(s, u, blocks):
                    g = 2 * s + u
                    for c in blocks:
                        act.wait_ge(u_mm, g * BLOCKS + c + 1)
                        if c == 0:
                            act.wait_ge(mixed_ready, 2 * s * BLOCKS)
                        nc.scalar.activation(gate[u][:, c, :], u_ps[c % 2][:, :CHUNK], ACT.Silu,
                                             bias=u_bias[:, c:c + 1]).then_inc(gate_ready, 1)

                def take_norm(s, u):
                    g = 2 * s + u
                    act.wait_ge(nt_mm, g + 1)
                    act.wait_ge(nt_stored[u], s * 16)
                    nc.scalar.activation(n1_t[u][:, 0, :], o_ps[0][:, :CHUNK], ACT.Copy).then_inc(nt0_ready, 1)

                def store_norm(s, u):
                    g = 2 * s + u
                    act.wait_ge(nt0_ready, g + 1)
                    act.wait_ge(nt1_ready, g + 1)
                    act.dma_start(d["n1_t"][g], n1_t[u][:]).then_inc(nt_stored[u], 16)

                def roots(s, u):
                    g = 2 * s + u
                    act.wait_ge(var_ready, g + 1)
                    nc.scalar.activation(root[u][:], var[u][:], ACT.Sqrt).then_inc(rooted, 1)
                    act.wait_ge(t1_ready, 2 * g + 2)
                    act.dma_start(d["t1_tiles"][g], t1[u][:]).then_inc(t1_stored[u], 16)

                def step(before, now, after):
                    if after:
                        gates(*after, range(0, 2))
                    if before:
                        take_norm(*before)
                    if after:
                        gates(*after, range(2, BLOCKS))
                    if before:
                        store_norm(*before)
                    roots(*now)

                gates(0, 0, range(BLOCKS))
                all_steps(act, step)
                take_norm(PAIRS - 1, 1)
                store_norm(PAIRS - 1, 1)
                for u in range(2):
                    act.wait_ge(t1_stored[u], 16 * PAIRS)
                    act.wait_ge(nt_stored[u], 16 * PAIRS)

            @block.vector
            def _(dve):
                def mixes(s, u):
                    g = 2 * s + u
                    dve.wait_ge(gate_ready, g * BLOCKS + BLOCKS)
                    dve.wait_ge(o_mm, 2 * 2 * s)
                    for c in range(BLOCKS):
                        dve.wait_ge(y_mm, g * BLOCKS + c + 1)
                        nc.vector.tensor_tensor(mixed[u][:, c, :], gate[u][:, c, :], y_ps[c][:, :CHUNK],
                                                ALU.mult).then_inc(mixed_ready, 1)

                def take_norm(s, u):
                    g = 2 * s + u
                    dve.wait_ge(nt_mm, g + 1)
                    dve.wait_ge(nt_stored[u], s * 16)
                    nc.vector.tensor_copy(n1_t[u][:, 1, :], o_ps[1][:, :CHUNK]).then_inc(nt1_ready, 1)

                def residual_norm(s, u):
                    g = 2 * s + u
                    dve.wait_ge(resid_ready, g + 1)
                    dve.wait_ge(t1_stored[u], s * 16)
                    for pair in range(TILES // 2):
                        dve.wait_ge(o_mm, 2 * g + pair + 1)
                        nc.vector.tensor_tensor(t1[u][:, 2 * pair:2 * pair + 2, :],
                                                o_ps[pair][:TILE, :].rearrange("p (t c) -> p t c", t=2),
                                                resid[u][:, 2 * pair:2 * pair + 2, :], ALU.add).then_inc(t1_ready, 1)
                    dve.wait_ge(t1_ready, 2 * g + 2)
                    for t in range(TILES):
                        last = nc.vector.bn_stats(stats[:, t, :], t1[u][:, t, :])
                    last.then_inc(measured, 1)
                    dve.wait_ge(measured, g + 1)
                    dve.sem_inc(seen, 1)
                    for t in range(TILES):
                        last = nc.vector.bn_aggr(moments[u][:, t, :], stats[:, t, :])
                    last.then_inc(aggregated, 1)
                    dve.wait_ge(aggregated, g + 1)
                    nc.vector.tensor_scalar(var[u][:], moments[u][:, :, 1], LN_EPS, None, ALU.add).then_inc(var_ready, 1)

                def normalise(s, u):
                    g = 2 * s + u
                    dve.wait_ge(rooted, g + 1)
                    nc.vector.reciprocal(inv[u][:], root[u][:]).then_inc(inverted, 1)
                    dve.wait_ge(inverted, g + 1)
                    nc.vector.scalar_tensor_tensor(out=shift[u][:], in0=moments[u][:, :, 0], scalar=-1.0, in1=inv[u][:],
                                                   op0=ALU.mult, op1=ALU.mult).then_inc(shift_ready, 1)
                    dve.wait_ge(shift_ready, g + 1)
                    dve.wait_ge(nt_mm, 2 * s)
                    for t in range(TILES):
                        last = nc.vector.tensor_scalar(n1[u][:, t, :], t1[u][:, t, :], inv[u][:, t:t + 1], shift[u][:, t:t + 1],
                                                       ALU.mult, ALU.add)
                    last.then_inc(n1_ready, 1)

                def step(before, now, after):
                    if before:
                        take_norm(*before)
                    residual_norm(*now)
                    if after:
                        mixes(*after)
                    normalise(*now)

                mixes(0, 0)
                all_steps(dve, step)
                take_norm(PAIRS - 1, 1)


def attention_phase(nc, d):
    with Tools(nc, "at") as T:
        NT = CHUNKS * TILES
        HB = 128 // HEAD
        BLOCKS = 4
        SETS = BLOCKS * HB
        COMPACT = CHUNKS * SETS
        AHEAD = COMPACT - SETS
        STRIDE = 2 * COMPACT - SETS
        w_qkv = [T.sb(f"w_qkv_{part}", [128, HALVES, 3 * CH], F32R) for part in ("high", "low")]
        w_proj = T.sb("w_proj", [128, HALVES, CH])
        p_bias = T.sb("p_bias", [TILE, CH])
        ident = T.sb("ident", [128, 128])
        same_head = T.sb("same_head", [128, 128])
        row_head = T.sb("row_head", [128, SETS - HB + COMPACT])
        spread = T.sb("spread", [COMPACT, CHUNKS * BLOCKS, 128], F32R)
        z_rows = T.sb("z_rows", [COMPACT, HALVES, 128])
        n_raw = [T.sb(f"n_raw{i}", [128, HALVES, CHUNK]) for i in range(2)]
        n_t = [[T.sb(f"n_t{i}_{part}", [128, HALVES, CHUNK], F32R) for part in ("high", "low")] for i in range(2)]
        qk_t = T.sb("qk_t", [128, BLOCKS, TOKENS])
        k = T.sb("k", [TILE, NT, CH])
        v = T.sb("v", [TILE, NT, CH])
        part, part2 = (T.sb(n, [128, BLOCKS, CHUNKS]) for n in ("part", "part2"))
        total, total_eps, total2, total2_eps = (T.sb(n, [128, BLOCKS]) for n in ("total", "total_eps", "total2", "total2_eps"))
        sel = T.sb("sel", [128, AHEAD + BLOCKS * (STRIDE + HB)])
        const, const2 = T.sb("const", [COMPACT, 1]), T.sb("const2", [COMPACT, 1])
        flow, inv_flow, kept = (T.sb(n, [COMPACT, CHUNK]) for n in ("flow", "inv_flow", "kept"))
        clipped = source = flow
        factor = alloc = kept
        rows = [T.sb(f"rows_{part}", [COMPACT, CHUNK], F32R) for part in ("high", "low")]
        source_tok = T.sb("source_tok", [TILE, TILES, COMPACT])
        z_part, z_inv, z_factor = T.sb("z_part", [COMPACT, 1]), T.sb("z_inv", [128, HALVES]), T.sb("z_factor", [128, HALVES])
        kv = T.sb("kv", [128, HALVES, 128])
        fb = [T.sb(f"fb{i}", [128, CHUNK]) for i in range(2)]
        upd_t = [T.sb(f"upd_t{i}", [128, HALVES, CHUNK]) for i in range(2)]
        scratch = fb[0]
        t1 = [T.sb(f"t1{i}", [TILE, TILES, CH]) for i in range(2)]
        bank = [T.ps(f"bank{i}", [128, 512]) for i in range(8)]
        qt_ps, flow_ps, kept_ps, kt_ps = bank[0:2], bank[2], bank[3], bank[6:8]
        wide_ps = bank[0:2] + bank[4:6]
        turn_ps, z_ps, kv_ps = bank[0], bank[1], bank[2:4]
        fb_ps, upd_ps, proj_ps = bank[0:2], bank[4:6], bank[6:8]
        CONST = CHUNK
        (consts_in, cleared, raw_in, split_consts, high_ready, low_ready, qt_mm, qt_ready, kt_mm, k_ready, v_ready, v_ready_s, const_mm, flow_mm, spread_mm, sum_ready, kept_mm, link,
         alloc_ready, source_ready, turn_mm, turned, z_mm, v_scaled, kv_mm, fb_mm, fb_ready, upd_mm, upd_ready, proj_mm,
         t1_biased, t2_ready) = (T.sem(n) for n in (
             "consts_in", "cleared", "raw_in", "split_consts", "high_ready", "low_ready", "qt_mm", "qt_ready", "kt_mm", "k_ready", "v_ready", "v_ready_s", "const_mm", "flow_mm", "spread_mm",
             "sum_ready", "kept_mm", "link", "alloc_ready", "source_ready", "turn_mm", "turned", "z_mm", "v_scaled", "kv_mm",
             "fb_mm", "fb_ready", "upd_mm", "upd_ready", "proj_mm", "t1_biased", "t2_ready"))
        n_loaded, t1_loaded, t2_stored = ([T.sem(f"{n}{i}") for i in range(2)] for n in ("n_loaded", "t1_loaded", "t2_stored"))
        QT, UPDS, SUMS = CHUNKS * BLOCKS, CHUNKS * HALVES, CHUNKS * TILES // 2
        PER_SLOT = [(CHUNKS + 1) // 2, CHUNKS // 2]
        ALL_LINKS = {name: i + 1 for i, name in enumerate((
            "total", "total_eps", "sel", "const", "flow", "inv_flow", "inv_high", "inv_low", "total2", "total2_eps", "sel2", "const2",
            "kept", "clipped", "factor", "factor_high", "factor_low", "z_inv", "z_factor", "kv"))}
        V_ON_SCALAR = (2, 4, 6)
        LINKS = len(ALL_LINKS)
        raw_w = qk_t[:, 0, :HALVES * 3 * CH].rearrange("p (h c) -> p h c", h=HALVES)
        raw_spread = [qk_t[:COMPACT, 1 + i, :CHUNKS * BLOCKS // 2 * 128].rearrange("p (n c) -> p n c", c=128) for i in range(2)]
        loads = [(w_proj, "w_proj"), (p_bias, "p_bias"), (ident, "ident"), (same_head, "same_head"),
                 (row_head, "row_head"), (z_rows, "z_rows")]
        head_mask = same_head[:, 0:128:HEAD]

        def wait_link(eng, b, name):
            eng.wait_ge(link, b * LINKS + ALL_LINKS[name])

        def window(x, j):
            at = AHEAD + x * STRIDE - j * SETS
            return sel[:, at:at + COMPACT]

        def part_free(eng, b, i):
            if i < 2:
                eng.wait_ge(kt_mm, b * NT)
            elif i < CHUNKS + 2:
                eng.wait_ge(qt_mm, b * QT + (i - 1) * BLOCKS)
            else:
                eng.wait_ge(kt_mm, b * NT + (i - CHUNKS - 1) * TILES)

        def v_out(eng, b, n):
            own = V_ON_SCALAR if n // TILES in V_ON_SCALAR else [j for j in range(CHUNKS) if j not in V_ON_SCALAR]
            eng.wait_ge(v_ready_s if own is V_ON_SCALAR else v_ready, (b * len(own) + own.index(n // TILES)) * TILES + n % TILES + 1)

        def over_images(eng, image):
            with eng.Fori(0, BATCH - 1) as b:
                image(b, True)
            image(BATCH - 1, False)

        sel_heads = sel[:, AHEAD:].rearrange("p (x w) -> p x w", x=BLOCKS)[:, :, :HB]

        with nc.Block() as block:
            @block.sync
            def _(sp):
                for tile, name in loads:
                    sp.dma_start(tile[:], d[name]).then_inc(consts_in, 16)
                sp.dma_start(raw_w, d["w_qkv"]).then_inc(raw_in, 16)
                for i in range(2):
                    sp.dma_start(raw_spread[i], d["spread"][:, i * CHUNKS * BLOCKS // 2:(i + 1) * CHUNKS * BLOCKS // 2]
                                 ).then_inc(raw_in, 16)
                def load(b, i):
                    sp.wait_ge(high_ready, b * 2 * CHUNKS + max(i - 1, 0))
                    sp.wait_ge(low_ready, b * 2 * CHUNKS + max(i - 1, 0))
                    sp.dma_start(n_raw[i % 2][:], d["n1_t"][b * CHUNKS + i % CHUNKS]).then_inc(n_loaded[i % 2], 16)

                load(0, 0)
                load(0, 1)

                def image(b, more):
                    for i in range(2, 2 * CHUNKS):
                        load(b, i)
                    for i in range(2 if more else 0):
                        load(b + 1, i)
                    for j in range(CHUNKS):
                        sp.wait_ge(t2_stored[j % 2], (b * PER_SLOT[j % 2] + j // 2) * 16)
                        sp.dma_start(t1[j % 2][:], d["t1_tiles"][b * CHUNKS + j]).then_inc(t1_loaded[j % 2], 16)

                over_images(sp, image)

            @block.gpsimd
            def _(pool):
                nc.gpsimd.memset(sel[:], 0.0).then_inc(cleared, 1)
                pool.wait_ge(consts_in, 16 * len(loads))
                def image(b, more):
                    for j in range(CHUNKS):
                        pool.wait_ge(t1_loaded[j % 2], (b * PER_SLOT[j % 2] + j // 2 + 1) * 16)
                        nc.gpsimd.tensor_tensor(t1[j % 2][:], t1[j % 2][:], p_bias[:].unsqueeze(1).to_broadcast([TILE, TILES, CH]),
                                                ALU.add).then_inc(t1_biased, 1)

                over_images(pool, image)

            @block.tensor
            def _(pe):
                pe.wait_ge(consts_in, 16 * len(loads))
                pe.wait_ge(split_consts, 4)
                def image(b, more):
                    def split_done(i):
                        pe.wait_ge(low_ready, b * 2 * CHUNKS + i + 1)

                    def project_t(j):
                        split_done(j)
                        for x in range(BLOCKS):
                            n = BLOCKS * j + x
                            if n >= 2:
                                pe.wait_ge(qt_ready, b * QT + n - 1)
                            else:
                                pe.wait_ge(qt_ready, b * QT)
                                pe.wait_ge(fb_ready, b * UPDS)
                            for h in range(HALVES):
                                last = product(nc, qt_ps[n % 2][:, :CHUNK], [w[:, h, x * 128:(x + 1) * 128] for w in w_qkv],
                                               [part[:, h, :] for part in n_t[j % 2]], start=h == 0, stop=h == HALVES - 1)
                            last.then_inc(qt_mm, 1)

                    def project(j):
                        i = CHUNKS + j
                        split_done(i)
                        for n in range(j * TILES, (j + 1) * TILES):
                            t = n % TILES
                            if n >= 2:
                                pe.wait_ge(k_ready, b * NT + n - 1)
                                v_out(pe, b, n - 2)
                            for h in range(HALVES):
                                last = product(nc, kt_ps[n % 2][:TILE, :],
                                               [part[:, h, t * TILE:(t + 1) * TILE] for part in n_t[i % 2]],
                                               [w[:, h, CH:] for w in w_qkv], start=h == 0, stop=h == HALVES - 1)
                            last.then_inc(kt_mm, 1)

                    def head_sums(sums, out_bank, done):
                        for x in range(BLOCKS):
                            y = (x + 2) % BLOCKS
                            last = nc.tensor.matmul(out_bank[:COMPACT, CONST:CONST + 1], row_head[:, SETS - HB * (x + 1):SETS - HB * (x + 1) + COMPACT], sums[:, y:y + 1],
                                                    start=x == 0, stop=x == BLOCKS - 1)
                        last.then_inc(const_mm, 1)
                        for j in range(CHUNKS):
                            for x in range(BLOCKS):
                                last = nc.tensor.matmul(out_bank[:COMPACT, :CHUNK], window(x, j),
                                                        qk_t[:, x, j * CHUNK:(j + 1) * CHUNK],
                                                        start=j == 0 and x == 0, stop=j == CHUNKS - 1 and x == BLOCKS - 1)
                        last.then_inc(done, 1)

                    for j in range(CHUNKS):
                        project_t(j)
                    pe.wait_ge(t2_ready, b * SUMS)
                    project(0)
                    project(1)
                    wait_link(pe, b, "sel")
                    head_sums(total_eps, flow_ps, flow_mm)
                    project(2)
                    def spread_rows(out, n):
                        nc.tensor.matmul(out, spread[:, n, :], rows[0][:], start=True, stop=False)
                        return nc.tensor.matmul(out, spread[:, n, :], rows[1][:], start=False, stop=True)

                    wait_link(pe, b, "inv_low")
                    for n in range(QT):
                        pe.wait_ge(sum_ready, b * QT + max(n - 3, 0))
                        spread_rows(wide_ps[n % 4][:, :CHUNK], n).then_inc(spread_mm, 1)
                    project(3)
                    wait_link(pe, b, "sel2")
                    head_sums(total2_eps, kept_ps, kept_mm)
                    project(4)
                    project(5)
                    pe.wait_ge(source_ready, b + 1)
                    for t in range(TILES):
                        last = nc.tensor.transpose(turn_ps[:TILE, t * COMPACT:(t + 1) * COMPACT],
                                                   source[:, t * TILE:(t + 1) * TILE], ident[:COMPACT, :COMPACT])
                    last.then_inc(turn_mm, 1)
                    for h in range(HALVES):
                        last = nc.tensor.matmul(z_ps[:, h:h + 1], z_rows[:, h, :], z_part[:], start=True, stop=True)
                    last.then_inc(z_mm, 1)
                    project(6)
                    for n in range(NT):
                        if n % TILES == 0:
                            pe.wait_ge(v_scaled, b * CHUNKS + n // TILES + 1)
                        for h in range(HALVES):
                            last = nc.tensor.matmul(kv_ps[h][:, :128], k[:, n, h * 128:(h + 1) * 128],
                                                    v[:, n, h * 128:(h + 1) * 128], start=n == 0, stop=n == NT - 1)
                    last.then_inc(kv_mm, 1)

                    def update(j):
                        for h in range(HALVES):
                            n = HALVES * j + h
                            if n >= 2:
                                pe.wait_ge(fb_ready, b * UPDS + n - 1)
                            spread_rows(fb_ps[n % 2][:, :CHUNK], BLOCKS * j + h).then_inc(fb_mm, 1)
                        for h in range(HALVES):
                            n = HALVES * j + h
                            if n == 0:
                                wait_link(pe, b, "kv")
                            if n >= 2:
                                pe.wait_ge(upd_ready, b * UPDS + n - 1)
                            nc.tensor.matmul(upd_ps[n % 2][:, :CHUNK], kv[:, h, :], qk_t[:, h, j * CHUNK:(j + 1) * CHUNK],
                                             start=True, stop=True).then_inc(upd_mm, 1)

                    def output(j):
                        pe.wait_ge(upd_ready, b * UPDS + HALVES * (j + 1))
                        for pair in range(TILES // 2):
                            n = j * TILES // 2 + pair
                            if n >= 2:
                                pe.wait_ge(t2_ready, b * SUMS + n - 1)
                            for t in (2 * pair, 2 * pair + 1):
                                for h in range(HALVES):
                                    last = nc.tensor.matmul(proj_ps[n % 2][:TILE, (t % 2) * CH:(t % 2 + 1) * CH],
                                                            upd_t[j % 2][:, h, t * TILE:(t + 1) * TILE], w_proj[:, h, :],
                                                            start=h == 0, stop=h == HALVES - 1)
                            last.then_inc(proj_mm, 1)

                    wait_link(pe, b, "factor_low")
                    pe.wait_ge(turned, b + 1)
                    wait_link(pe, b, "z_inv")
                    v_out(pe, b, NT - 1)
                    v_out(pe, b, NT - TILES - 1)
                    pe.wait_ge(k_ready, (b + 1) * NT)
                    for j in range(CHUNKS):
                        update(j)
                        if j:
                            output(j - 1)
                    output(CHUNKS - 1)

                over_images(pe, image)

            @block.scalar
            def _(act):
                act.wait_ge(raw_in, 16 * 3)
                nc.scalar.activation(w_qkv[0][:], raw_w, ACT.Copy).then_inc(split_consts, 1)
                for i in range(2):
                    nc.scalar.activation(spread[:, i * CHUNKS * BLOCKS // 2:(i + 1) * CHUNKS * BLOCKS // 2, :], raw_spread[i],
                                         ACT.Copy).then_inc(split_consts, 1)
                act.wait_ge(split_consts, 4)

                def high_part(b, i):
                    act.wait_ge(n_loaded[i % 2], (b * CHUNKS + i // 2 + 1) * 16)
                    part_free(act, b, i)
                    nc.scalar.activation(n_t[i % 2][0][:], n_raw[i % 2][:], ACT.Copy).then_inc(high_ready, 1)

                high_part(0, 0)
                high_part(0, 1)

                def image(b, more):
                    def take_k(j):
                        for n in range(j * TILES, (j + 1) * TILES):
                            act.wait_ge(kt_mm, b * NT + n + 1)
                            nc.scalar.activation(k[:, n, :], kt_ps[n % 2][:TILE, :CH], ACT.Sigmoid).then_inc(k_ready, 1)
                            if j in V_ON_SCALAR:
                                nc.scalar.activation(v[:, n, :], kt_ps[n % 2][:TILE, CH:], ACT.Copy).then_inc(v_ready_s, 1)

                    act.wait_ge(upd_mm, b * UPDS)
                    act.wait_ge(kv_mm, b)
                    for n in range(QT):
                        j, x = divmod(n, BLOCKS)
                        act.wait_ge(qt_mm, b * QT + n + 1)
                        nc.scalar.activation(qk_t[:, x, j * CHUNK:(j + 1) * CHUNK], qt_ps[n % 2][:, :CHUNK], ACT.Sigmoid,
                                             accum_out=part[:, x, j:j + 1]).then_inc(qt_ready, 1)
                        if x == BLOCKS - 1:
                            high_part(b, j + 2)
                    for j in range(4):
                        take_k(j)
                        high_part(b, CHUNKS + j + 2)
                    take_k(4)
                    high_part(b, CHUNKS + 6)
                    wait_link(act, b, "clipped")
                    nc.scalar.activation(alloc[:], kept[:], ACT.Sigmoid).then_inc(alloc_ready, 1)
                    nc.scalar.activation(source[:], clipped[:], ACT.Exp, accum_out=z_part[:]).then_inc(source_ready, 1)
                    take_k(5)
                    act.wait_ge(turn_mm, b + 1)
                    nc.scalar.activation(source_tok[:].rearrange("p t r -> p (t r)"), turn_ps[:TILE, :TILES * COMPACT], ACT.Copy
                                         ).then_inc(turned, 1)
                    take_k(6)
                    for n in range(UPDS):
                        j = n // HALVES
                        act.wait_ge(fb_mm, b * UPDS + n + 1)
                        act.wait_ge(upd_ready, b * UPDS + max(n - 1, 0))
                        nc.scalar.activation(fb[n % 2][:], fb_ps[n % 2][:, :CHUNK], ACT.Copy).then_inc(fb_ready, 1)
                        if more and n % HALVES == 1 and j < 2:
                            high_part(b + 1, j)
                        if n % HALVES == 1 and j >= 2:
                            act.wait_ge(t2_ready, b * SUMS + (j - 1) * TILES // 2)
                            act.dma_start(d["t2_tiles"][b * CHUNKS + j - 2], t1[j % 2][:]).then_inc(t2_stored[j % 2], 16)
                    for j in range(CHUNKS - 2, CHUNKS):
                        act.wait_ge(t2_ready, b * SUMS + (j + 1) * TILES // 2)
                        act.dma_start(d["t2_tiles"][b * CHUNKS + j], t1[j % 2][:]).then_inc(t2_stored[j % 2], 16)

                over_images(act, image)
                for i in range(2):
                    act.wait_ge(t2_stored[i], 16 * BATCH * PER_SLOT[i])

            @block.vector
            def _(dve):
                dve.wait_ge(consts_in, 16 * len(loads))
                dve.wait_ge(cleared, 1)
                dve.wait_ge(raw_in, 16 * 3)
                dve.wait_ge(split_consts, 1)
                nc.vector.tensor_tensor(w_qkv[1][:], raw_w, w_qkv[0][:].bitcast(F32), ALU.subtract).then_inc(split_consts, 1)
                def low_part(b, i):
                    dve.wait_ge(high_ready, b * 2 * CHUNKS + i + 1)
                    high, low = n_t[i % 2]
                    nc.vector.tensor_tensor(low[:], n_raw[i % 2][:], high[:].bitcast(F32), ALU.subtract).then_inc(low_ready, 1)

                low_part(0, 0)
                low_part(0, 1)

                def image(b, more):
                    def take_v(j):
                        for n in range(j * TILES, (j + 1) * TILES):
                            dve.wait_ge(kt_mm, b * NT + n + 1)
                            dve.wait_ge(k_ready, b * NT + n + 1)
                            nc.vector.tensor_copy(v[:, n, :], kt_ps[n % 2][:TILE, CH:]).then_inc(v_ready, 1)

                    def step(name, instruction):
                        instruction.then_inc(link, 1)

                    def split_rows(name, values):
                        step(name + "_high", nc.vector.tensor_copy(rows[0][:], values[:]))
                        wait_link(dve, b, name + "_high")
                        step(name + "_low", nc.vector.tensor_tensor(rows[1][:], values[:], rows[0][:].bitcast(F32), ALU.subtract))

                    mask3 = head_mask.unsqueeze(1).to_broadcast([128, 2, HB])

                    def select(name, sums):
                        for x in (0, 2):
                            y = (x + 2) % BLOCKS
                            last = nc.vector.tensor_tensor(sel_heads[:, x:x + 2, :], mask3,
                                                           sums[:, y:y + 2].unsqueeze(2).to_broadcast([128, 2, HB]), ALU.mult)
                        step(name, last)

                    for i in range(2, CHUNKS + 2):
                        low_part(b, i)
                    dve.wait_ge(qt_ready, (b + 1) * QT)
                    step("total", nc.vector.reduce_sum(total[:], part[:], axis=AX.X))
                    wait_link(dve, b, "total")
                    step("total_eps", nc.vector.tensor_scalar(total_eps[:], total[:], ATT_EPS, None, ALU.add))
                    wait_link(dve, b, "total_eps")
                    select("sel", total_eps)
                    take_v(0)
                    low_part(b, CHUNKS + 2)
                    take_v(1)
                    low_part(b, CHUNKS + 3)
                    dve.wait_ge(const_mm, 2 * b + 1)
                    dve.wait_ge(flow_mm, b + 1)
                    step("const", nc.vector.tensor_scalar(const[:], flow_ps[:COMPACT, CONST:CONST + 1], ATT_EPS, ATT_EPS,
                                                          ALU.mult, ALU.add))
                    wait_link(dve, b, "const")
                    step("flow", nc.vector.tensor_scalar(flow[:], flow_ps[:COMPACT, :CHUNK], const[:, 0:1], None, ALU.add))
                    wait_link(dve, b, "flow")
                    step("inv_flow", nc.vector.reciprocal(inv_flow[:], flow[:]))
                    wait_link(dve, b, "inv_flow")
                    split_rows("inv", inv_flow)
                    low_part(b, CHUNKS + 4)
                    for n in range(QT):
                        j, x = divmod(n, BLOCKS)
                        dve.wait_ge(spread_mm, b * QT + n + 1)
                        dve.wait_ge(sum_ready, b * QT + n)
                        nc.vector.scalar_tensor_tensor(out=scratch[:], in0=wide_ps[n % 4][:, :CHUNK], scalar=1.0,
                                                       in1=qk_t[:, x, j * CHUNK:(j + 1) * CHUNK], op0=ALU.mult, op1=ALU.mult,
                                                       accum_out=part2[:, x, j:j + 1]).then_inc(sum_ready, 1)
                    dve.wait_ge(sum_ready, (b + 1) * QT)
                    step("total2", nc.vector.reduce_sum(total2[:], part2[:], axis=AX.X))
                    wait_link(dve, b, "total2")
                    step("total2_eps", nc.vector.tensor_scalar(total2_eps[:], total2[:], ATT_EPS, None, ALU.add))
                    wait_link(dve, b, "total2_eps")
                    select("sel2", total2_eps)
                    take_v(3)
                    low_part(b, CHUNKS + 5)
                    dve.wait_ge(const_mm, 2 * b + 2)
                    dve.wait_ge(kept_mm, b + 1)
                    step("const2", nc.vector.tensor_scalar(const2[:], kept_ps[:COMPACT, CONST:CONST + 1], ATT_EPS, ATT_EPS,
                                                           ALU.mult, ALU.add))
                    wait_link(dve, b, "const2")
                    step("kept", nc.vector.tensor_scalar(kept[:], kept_ps[:COMPACT, :CHUNK], const2[:, 0:1], None, ALU.add))
                    wait_link(dve, b, "kept")
                    step("clipped", nc.vector.tensor_scalar(clipped[:], kept[:], 1.0, -1.0, ALU.min, ALU.max))
                    low_part(b, CHUNKS + 6)
                    take_v(5)
                    dve.wait_ge(alloc_ready, b + 1)
                    step("factor", nc.vector.tensor_tensor(factor[:], inv_flow[:], alloc[:], ALU.mult))
                    wait_link(dve, b, "factor")
                    split_rows("factor", factor)

                    def scale_v(j):
                        v_out(dve, b, (j + 1) * TILES - 1)
                        for t in range(TILES):
                            heads = v[:, j * TILES + t, :].rearrange("p (h c) -> p h c", c=HEAD)
                            each = source_tok[:, t, j * SETS + 2 * HB:(j + 1) * SETS].unsqueeze(2).to_broadcast([TILE, 2 * HB, HEAD])
                            last = nc.vector.tensor_tensor(heads, heads, each, ALU.mult)
                        last.then_inc(v_scaled, 1)

                    dve.wait_ge(turned, b + 1)
                    for j in range(CHUNKS):
                        scale_v(j)
                    dve.wait_ge(z_mm, b + 1)
                    step("z_inv", nc.vector.reciprocal(z_inv[:], z_ps[:, :HALVES]))
                    wait_link(dve, b, "z_inv")
                    step("z_factor", nc.vector.tensor_scalar(z_factor[:], z_inv[:], TOKENS / V_SCALE, None, ALU.mult))
                    wait_link(dve, b, "z_factor")
                    dve.wait_ge(kv_mm, b + 1)
                    for h in range(HALVES):
                        last = nc.vector.scalar_tensor_tensor(out=kv[:, h, :], in0=kv_ps[h][:, :128], scalar=z_factor[:, h:h + 1],
                                                              in1=same_head[:], op0=ALU.mult, op1=ALU.mult)
                    step("kv", last)

                    def take_update(j):
                        for h in range(HALVES):
                            n = HALVES * j + h
                            dve.wait_ge(upd_mm, b * UPDS + n + 1)
                            dve.wait_ge(fb_ready, b * UPDS + n + 1)
                            if j >= 2:
                                dve.wait_ge(proj_mm, b * SUMS + (j - 1) * TILES // 2)
                            nc.vector.tensor_tensor(upd_t[j % 2][:, h, :], upd_ps[n % 2][:, :CHUNK], fb[n % 2][:], ALU.mult
                                                    ).then_inc(upd_ready, 1)

                    def add_residual(j):
                        dve.wait_ge(t1_biased, b * CHUNKS + j + 1)
                        for pair in range(TILES // 2):
                            n = j * TILES // 2 + pair
                            dve.wait_ge(proj_mm, b * SUMS + n + 1)
                            nc.vector.tensor_tensor(t1[j % 2][:, 2 * pair:2 * pair + 2, :],
                                                    proj_ps[n % 2][:TILE, :].rearrange("p (t c) -> p t c", t=2),
                                                    t1[j % 2][:, 2 * pair:2 * pair + 2, :], ALU.add).then_inc(t2_ready, 1)

                    for j in range(CHUNKS):
                        take_update(j)
                        if more and j in (2, 3):
                            low_part(b + 1, j - 2)
                        if j:
                            add_residual(j - 1)
                    add_residual(CHUNKS - 1)

                over_images(dve, image)


def ffn_phase(nc, d):
    with Tools(nc, "ff") as T:
        NB = HIDDEN // 128
        PAIRS_T = CHUNK // 2
        fc1_raw = T.sb("fc1_raw", [128, HALVES, HIDDEN])
        interp = T.sb("interp", [128, HALVES, 128])
        fc1 = T.sb("fc1", [128, HIDDEN])
        fc1_bias = T.sb("fc1_bias", [128, NB])
        fc2 = T.sb("fc2", [128, NB, 128])
        fc2_bias = T.sb("fc2_bias", [128, 1])
        pair_tok = T.sb("pair_tok", [TILE, SIDE])
        pair_up = T.sb("pair_up", [128, CH])
        t2 = [T.sb(f"t2{u}", [TILE, TILES, CH]) for u in range(2)]
        stats = T.sb("stats", [TILE, 2 * TILES, 6])
        moments = T.sb("moments", [TILE, 2 * TILES, 2])
        var, root = T.sb("var", [TILE, 2 * TILES]), T.sb("root", [TILE, 2 * TILES])
        inv, shift = ([T.sb(f"{n}{u}", [TILE, TILES]) for u in range(2)] for n in ("inv", "shift"))
        n2 = [T.sb(f"n2{u}", [TILE, TILES, CH]) for u in range(2)]
        base = [T.sb(f"base{u}", [TILE, TILES, CH]) for u in range(2)]
        sums = [T.sb(f"sums{u}", [TILE, TILES, CH // 2]) for u in range(2)]
        low = [T.sb(f"low{u}", [128, PAIRS_T]) for u in range(2)]
        hid = T.sb("hid", [128, NB, PAIRS_T])
        change = T.sb("change", [128, CHUNK])
        out = [T.sb(f"out{u}", [TILE, TILES, CH]) for u in range(2)]
        low_ps, new_ps = T.ps("low", [128, 512]), T.ps("new", [128, 512])
        FB = 4
        hid_ps = [T.ps(f"hid{i}", [128, 512]) for i in range(FB)]
        up_ps = [T.ps(f"up{i}", [128, 512]) for i in range(2)]
        (consts_in, fc1_mm, fc1_ready, measured, aggregated, var_ready, rooted, inverted, shift_ready, n2_ready, base_ready,
         sums_ready, low_mm, low_ready, hid_mm, hid_ready, new_mm, change_ready, up_mm, out_ready) = (
            T.sem(n) for n in ("consts_in", "fc1_mm", "fc1_ready", "measured", "aggregated", "var_ready", "rooted", "inverted",
                               "shift_ready", "n2_ready", "base_ready", "sums_ready", "low_mm", "low_ready",
                               "hid_mm", "hid_ready", "new_mm", "change_ready", "up_mm", "out_ready"))
        loaded, stored = ([T.sem(f"{n}{u}") for u in range(2)] for n in ("loaded", "stored"))
        seen = T.sem("seen")
        PAIRS = BATCH * CHUNKS // 2
        loads = [(fc1_raw, "fc1"), (interp, "interp"), (fc1_bias, "fc1_bias"), (fc2, "fc2"), (fc2_bias, "fc2_bias"),
                 (pair_tok, "pair_tok"), (pair_up, "pair_up")]

        def buffer_used(eng, sem, s, u):
            if u or not (isinstance(s, int) and s == 0):
                eng.wait_ge(sem, 2 * s + u - 1)

        def all_steps(eng, front, step):
            front(0, 0)
            with eng.Fori(0, PAIRS - 1) as s:
                step((s, 0), (s, 1), s + 1)
                step((s, 1), (s + 1, 0))
            step((PAIRS - 1, 0), (PAIRS - 1, 1))
            step((PAIRS - 1, 1), None)

        with nc.Block() as block:
            @block.sync
            def _(sp):
                for tile, name in loads:
                    sp.dma_start(tile[:], d[name]).then_inc(consts_in, 16)
                for u in range(2):
                    sp.dma_start(t2[u][:], d["t2_tiles"][u]).then_inc(loaded[u], 16)

                def store(s, u):
                    sp.wait_ge(out_ready, 2 * (2 * s + u + 1))
                    sp.dma_start(d["out"][2 * s + u], out[u][:]).then_inc(stored[u], 16)

                with sp.Fori(0, PAIRS - 1) as s:
                    for u in range(2):
                        sp.wait_ge(base_ready, s * 2 + u + 1)
                        sp.wait_ge(n2_ready, s * 2 + u + 1)
                        sp.dma_start(t2[u][:], d["t2_tiles"][(s + 1) * 2 + u]).then_inc(loaded[u], 16)
                    for u in range(2):
                        store(s, u)
                for u in range(2):
                    store(PAIRS - 1, u)
                for u in range(2):
                    sp.wait_ge(stored[u], 16 * PAIRS)

            @block.gpsimd
            def _(pool):
                def add(s, u):
                    pool.wait_ge(n2_ready, s * 2 + u + 1)
                    nc.gpsimd.tensor_tensor(base[u][:], t2[u][:], n2[u][:], ALU.add).then_inc(base_ready, 1)

                add(0, 0)
                add(0, 1)
                with pool.Fori(0, PAIRS - 1) as s:
                    for u in range(2):
                        pool.wait_ge(out_ready, 2 * (2 * s + u + 1))
                        add(s + 1, u)

            @block.tensor
            def _(pe):
                pe.wait_ge(consts_in, 16 * len(loads))
                for i in range(2):
                    for h in range(HALVES):
                        last = nc.tensor.matmul(up_ps[i][:], interp[:, h, :], fc1_raw[:, h, i * 512:(i + 1) * 512],
                                                start=h == 0, stop=h == HALVES - 1)
                    last.then_inc(fc1_mm, 1)

                def hidden(s, u, m):
                    nc.tensor.matmul(hid_ps[m % FB][:, :PAIRS_T], fc1[:, m * 128:(m + 1) * 128], low[u][:],
                                     start=True, stop=True).then_inc(hid_mm, 1)

                def first_hidden(s, u):
                    pe.wait_ge(low_ready, 2 * s + u + 1)
                    for m in range(FB):
                        hidden(s, u, m)

                def low_band(s, u):
                    g = 2 * s + u
                    pe.wait_ge(sums_ready, g + 1)
                    pe.wait_ge(low_ready, g)
                    for t in range(TILES):
                        last = nc.tensor.matmul(low_ps[:, t * SIDE:(t + 1) * SIDE], sums[u][:, t, :], pair_tok[:],
                                                start=True, stop=True)
                    last.then_inc(low_mm, 1)

                def front(s, u):
                    low_band(s, u)
                    first_hidden(s, u)

                def step(now, after, next_pair=None):
                    s, u = now
                    g = 2 * s + u

                    def second(m):
                        pe.wait_ge(hid_ready, g * NB + m + 1)
                        if m == 0:
                            pe.wait_ge(change_ready, g)
                        last = nc.tensor.matmul(new_ps[:, :PAIRS_T], fc2[:, m, :], hid[:, m, :], start=m == 0, stop=m == NB - 1)
                        if m == NB - 1:
                            last.then_inc(new_mm, 1)

                    for m in range(FB, NB):
                        second(m - FB)
                        hidden(s, u, m)
                    if after:
                        low_band(*after)
                    for m in range(NB - FB, NB):
                        second(m)
                    if after:
                        first_hidden(*after)
                    pe.wait_ge(change_ready, g + 1)
                    for pair in range(TILES // 2):
                        pe.wait_ge(out_ready, 2 * g)
                        for t in (2 * pair, 2 * pair + 1):
                            last = nc.tensor.matmul(up_ps[pair][:TILE, (t % 2) * CH:(t % 2 + 1) * CH],
                                                    change[:, t * TILE:(t + 1) * TILE], pair_up[:], start=True, stop=True)
                        last.then_inc(up_mm, 1)

                pe.wait_ge(fc1_ready, 2)
                all_steps(pe, front, step)

            @block.scalar
            def _(act):
                act.wait_ge(consts_in, 16 * len(loads))
                for i in range(2):
                    act.wait_ge(fc1_mm, i + 1)
                    nc.scalar.activation(fc1[:, i * 512:(i + 1) * 512], up_ps[i][:], ACT.Copy).then_inc(fc1_ready, 1)

                def roots(s):
                    act.wait_ge(var_ready, s + 1)
                    nc.scalar.activation(root[:], var[:], ACT.Sqrt).then_inc(rooted, 1)

                def take_low(s, u):
                    act.wait_ge(low_mm, 2 * s + u + 1)
                    buffer_used(act, change_ready, s, u)
                    nc.scalar.activation(low[u][:], low_ps[:, :PAIRS_T], ACT.Copy).then_inc(low_ready, 1)

                def front(s, u):
                    roots(s)
                    take_low(s, u)

                def step(now, after, next_pair=None):
                    s, u = now
                    g = 2 * s + u
                    act.wait_ge(new_mm, g)
                    for m in range(NB):
                        act.wait_ge(hid_mm, g * NB + m + 1)
                        nc.scalar.activation(hid[:, m, :], hid_ps[m % FB][:, :PAIRS_T], ACT.Gelu,
                                             bias=fc1_bias[:, m:m + 1]).then_inc(hid_ready, 1)
                    if after:
                        take_low(*after)
                    if next_pair is not None:
                        roots(next_pair)

                all_steps(act, front, step)
            @block.vector
            def _(dve):
                dve.wait_ge(consts_in, 16 * len(loads))

                def measure(s, u):
                    dve.wait_ge(loaded[u], s * 16 + 16)
                    for t in range(TILES):
                        last = nc.vector.bn_stats(stats[:, u * TILES + t, :], t2[u][:, t, :])
                    last.then_inc(measured, 1)

                def moments_of(s):
                    measure(s, 1)
                    dve.wait_ge(measured, 2 * s + 2)
                    dve.wait_ge(shift_ready, 2 * s)
                    dve.sem_inc(seen, 1)
                    for t in range(2 * TILES):
                        last = nc.vector.bn_aggr(moments[:, t, :], stats[:, t, :])
                    last.then_inc(aggregated, 1)
                    dve.wait_ge(aggregated, s + 1)
                    nc.vector.tensor_scalar(var[:], moments[:, :, 1], LN_EPS, None, ALU.add).then_inc(var_ready, 1)

                def normalise(s, u):
                    g = 2 * s + u
                    tiles = slice(u * TILES, (u + 1) * TILES)
                    dve.wait_ge(rooted, s + 1)
                    nc.vector.reciprocal(inv[u][:], root[:, tiles]).then_inc(inverted, 1)
                    dve.wait_ge(inverted, g + 1)
                    nc.vector.scalar_tensor_tensor(out=shift[u][:], in0=moments[:, tiles, 0], scalar=-1.0, in1=inv[u][:],
                                                   op0=ALU.mult, op1=ALU.mult).then_inc(shift_ready, 1)
                    dve.wait_ge(shift_ready, g + 1)
                    buffer_used(dve, base_ready, s, u)
                    for t in range(TILES):
                        last = nc.vector.tensor_scalar(n2[u][:, t, :], t2[u][:, t, :], inv[u][:, t:t + 1], shift[u][:, t:t + 1],
                                                       ALU.mult, ALU.add)
                    last.then_inc(n2_ready, 1)
                    dve.wait_ge(n2_ready, g + 1)
                    buffer_used(dve, low_mm, s, u)
                    pair = n2[u][:].rearrange("p t (c r) -> p (t c) r", r=2)
                    nc.vector.tensor_tensor(sums[u][:].rearrange("p t c -> p (t c)"), pair[:, :, 0], pair[:, :, 1], ALU.add
                                            ).then_inc(sums_ready, 1)

                def front(s, u):
                    measure(s, 0)
                    moments_of(s)
                    normalise(s, u)

                def step(now, after, next_pair=None):
                    s, u = now
                    g = 2 * s + u
                    if after:
                        normalise(*after)
                    if next_pair is not None:
                        measure(next_pair, 0)
                    dve.wait_ge(new_mm, g + 1)
                    dve.wait_ge(up_mm, 2 * g)
                    twice = [128, PAIRS_T, 2]
                    nc.vector.scalar_tensor_tensor(out=change[:].rearrange("p (t r) -> p t r", r=2),
                                                   in0=new_ps[:, :PAIRS_T].unsqueeze(2).to_broadcast(twice), scalar=fc2_bias[:, 0:1],
                                                   in1=low[u][:].unsqueeze(2).to_broadcast(twice), op0=ALU.add, op1=ALU.subtract
                                                   ).then_inc(change_ready, 1)
                    if next_pair is not None:
                        moments_of(next_pair)
                    dve.wait_ge(base_ready, g + 1)
                    dve.wait_ge(stored[u], s * 16)
                    for pair in range(TILES // 2):
                        dve.wait_ge(up_mm, 2 * g + pair + 1)
                        nc.vector.tensor_tensor(out[u][:, 2 * pair:2 * pair + 2, :],
                                                up_ps[pair][:TILE, :].rearrange("p (t c) -> p t c", t=2),
                                                base[u][:, 2 * pair:2 * pair + 2, :], ALU.add).then_inc(out_ready, 1)

                all_steps(dve, front, step)


def program(nc, d):
    def scratch(name, shape):
        d[name] = nc.dram_tensor(name, shape, F32, kind="Internal").ap()

    chunks = BATCH * CHUNKS
    scratch("kern_rows", (ROWS, TAPS_PAD, WIDE))
    scratch("gn_rows", (chunks, 1, 2 * CH))
    scratch("xn_t", (chunks, 128, HALVES, CHUNK))
    scratch("v_rows", (ROWS, BATCH, SIDE, WIDE))
    scratch("y_rows", (ROWS, BATCH, SIDE, WIDE))
    scratch("t1_tiles", (chunks, TILE, TILES, CH))
    scratch("n1_t", (chunks, 128, HALVES, CHUNK))
    scratch("t2_tiles", (chunks, TILE, TILES, CH))
    flat = "b i j c -> (b i j) c"
    d["x_tiles"] = d["x"].rearrange(flat).rearrange("(g t p) c -> g p t c", t=TILES, p=TILE)
    d["out"] = d["result"].rearrange(flat).rearrange("(g t p) c -> g p t c", t=TILES, p=TILE)
    for phase in (kernel_rows_phase, stats_phase, project_phase, columns_phase, mix_phase, attention_phase, ffn_phase):
        phase(nc, d)


def kernel(**inputs):
    import concourse.bacc as bacc
    from concourse.bass_utils import run_bass_kernel_spmd

    a = {k: np.asarray(v) for k, v in inputs.items()}

    def on_partitions(w):
        return w.reshape(-1, 128, *w.shape[1:]).swapaxes(0, 1)

    def every_row(b, rows):
        return np.broadcast_to(b, (rows, b.shape[0]))

    conv, att, ffn = "L0_conv_", "L1_attn_", "L1_ffn_"
    rpe_bias = np.concatenate([a[conv + "rpe_in_b"][None], a[conv + "rpe_h_b"]], 0)
    arrays = {
        "x": a["x"],
        "w_u": on_partitions(a[conv + "W_u"].T), "u_bias": a[conv + "b_u"].reshape(-1, 128).T,
        "w_v": on_partitions(a[conv + "W_v"].T), "v_bias": every_row(a[conv + "b_v"], TILE),
        "w_o": on_partitions(a[conv + "W_o"].T), "o_bias": every_row(a[conv + "b_o"], TILE),
        "rpe_in": a[conv + "rpe_in_w"].T,
        "rpe_h": a[conv + "rpe_h_w"].transpose(0, 2, 1).reshape(RPE_LAYERS, HALVES, 128, CH).transpose(2, 0, 1, 3),
        "rpe_bias": rpe_bias.reshape(RPE_LAYERS + 1, HALVES, 128).transpose(2, 0, 1),
        "rpe_out": on_partitions(a[conv + "rpe_out_w"].T), "rpe_out_b": every_row(a[conv + "rpe_out_b"], TAPS),
        "w_qkv": on_partitions(a[att + "W_qkv"].T), "w_proj": on_partitions(a[att + "W_proj"].T),
        "p_bias": every_row(a[att + "b_proj"], TILE),
        "fc1": on_partitions(a[ffn + "fc1_w"].T), "fc1_bias": a[ffn + "fc1_b"].reshape(-1, 128).T,
        "fc2": on_partitions(a[ffn + "fc2_w"].T), "fc2_bias": a[ffn + "fc2_b"][:, None],
        **shape_constants(),
    }
    arrays = {k: np.ascontiguousarray(v) for k, v in arrays.items()}
    nc = bacc.Bacc("TRN2", target_bir_lowering=False, num_devices=1)
    d = {k: nc.dram_tensor(k, v.shape, mybir.dt.from_np(v.dtype), kind="ExternalInput").ap() for k, v in arrays.items()}
    d["result"] = nc.dram_tensor("result", (BATCH, SIDE, SIDE, CH), F32, kind="ExternalOutput").ap()
    program(nc, d)
    return run_bass_kernel_spmd(nc, [arrays], core_ids=[0]).results[0]["result"]
```

```python
from contextlib import ExitStack

import numpy as np

import concourse.bass as bass
from concourse import mybir

F32 = mybir.dt.float32
F32R = mybir.dt.float32r
ACT = mybir.ActivationFunctionType
ALU = mybir.AluOpType
AX = mybir.AxisListType

BATCH, SIDE, CH = 8, 56, 256
TOKENS = SIDE * SIDE
WIDE = 512
POINTS = 2 * SIDE
FREQ = SIDE + 1
ROWS = 2 * FREQ
TAPS = 2 * SIDE - 1
TAPS_PAD = 112
HALVES = CH // 128
CHUNK_ROWS = 8
CHUNK = CHUNK_ROWS * SIDE
CHUNKS = TOKENS // CHUNK
TILE = 2 * SIDE
TILES = CHUNK // TILE
RPE_ROWS = 4
RPE_CHUNK = RPE_ROWS * TAPS
RPE_LAYERS = 3
HEAD = 32
HIDDEN = 1024
V_SCALE = float((HEAD ** -0.5) * CH // 8)
RMS_EPS = 1e-08
GN_EPS = 1e-05
ATT_EPS = 1e-06
LN_EPS = 1e-05


def angles(a, b):
    return 2.0 * np.pi * ((np.outer(a, b) % POINTS) / POINTS)


def shape_constants():
    pos, freq, full = np.arange(SIDE), np.arange(FREQ), np.arange(POINTS)
    tap = np.arange(TAPS) - (SIDE - 1)
    c = {}
    w = angles(pos, freq)
    row = np.concatenate([np.cos(w), -np.sin(w)], 1)
    fwd = np.zeros((TILE, 2, ROWS))
    fwd[:SIDE, 0], fwd[SIDE:, 1] = row, row
    c["row_fwd"] = fwd
    w = angles(tap, freq)
    c["row_taps"] = np.concatenate([np.cos(w), -np.sin(w)], 1)
    w = angles(pos, full)
    c["col_fwd"] = np.stack([np.concatenate([np.cos(w), np.sin(w)], 0), np.concatenate([-np.sin(w), np.cos(w)], 0)], 1)
    w = angles(tap, full)
    c["col_taps"] = np.stack([np.cos(w), np.sin(w), -np.sin(w)], 1)
    w = angles(full, pos)
    c["col_inv"] = np.stack([np.concatenate([np.cos(w), np.sin(w)], 1), np.concatenate([-np.sin(w), np.cos(w)], 1)], 1) / POINTS
    w = angles(freq, pos)
    weight = np.where((freq == 0) | (freq == SIDE), 1.0, 2.0)[:, None] / POINTS
    edge = np.where((freq == 0) | (freq == SIDE), 0.0, 1.0)[:, None]
    c["row_inv"] = np.concatenate([weight * np.cos(w), -weight * edge * np.sin(w)], 0)
    c["ident"] = np.eye(128)
    c["ones"] = np.ones((128, 128))
    c["mean_ch"] = np.full((128, 128), 1.0 / CH)
    c["group_mean"] = np.kron(np.eye(16), np.full((8, 8), 1.0 / 8))
    c["same_head"] = np.kron(np.eye(128 // HEAD), np.ones((HEAD, HEAD)))
    heads = np.kron(np.eye(128 // HEAD), np.ones((1, HEAD)))
    blocks = np.stack([np.kron(np.eye(4)[x][:, None], heads) for x in range(4)], 0)
    c["row_head"] = np.concatenate([np.zeros((12, 128)), np.tile(blocks[0], (CHUNKS, 1))], 0).T
    spread = np.stack([np.kron(np.eye(CHUNKS)[j][:, None], blocks[x]) for j in range(CHUNKS) for x in range(4)], 1)
    c["spread"] = spread
    c["z_rows"] = spread.reshape(-1, CHUNKS, 4, 128).sum(1)[:, 2:]
    p, q = np.meshgrid(np.arange(TAPS_PAD) - (SIDE - 1), tap, indexing="ij")
    c["coords"] = np.stack([p.ravel(), q.ravel()], 0)
    c["pair_up"] = np.kron(np.eye(CH // 2), np.ones((1, 2))) * 0.5
    c["pair_tok"] = np.kron(np.eye(SIDE), np.ones((2, 1))) * 0.5
    at = np.linspace(0.0, 1.0, CH, dtype=np.float32) * np.float32(CH // 2 - 1)
    lo = np.clip(np.floor(at).astype(np.int32), 0, CH // 2 - 2)
    frac = at - lo.astype(np.float32)
    interp = np.zeros((CH, CH // 2), np.float32)
    interp[np.arange(CH), lo] += np.float32(1.0) - frac
    interp[np.arange(CH), lo + 1] += frac
    c["interp"] = interp.reshape(HALVES, 128, 128).transpose(1, 0, 2)
    return {k: np.ascontiguousarray(v, dtype=np.float32) for k, v in c.items()}


def rows_of_chunk(rows, g):
    return rows.rearrange("k b i c -> k (b i) c")[:, bass.ds(g * CHUNK_ROWS, CHUNK_ROWS), :]


def product(nc, out, weights, data, start, stop):
    passes = [(0, 0), (0, 1), (1, 0)]
    for i, (a, b) in enumerate(passes):
        last = nc.tensor.matmul(out, weights[a], data[b], start=start and i == 0, stop=stop and i == len(passes) - 1)
    return last


class Tools:

    def __init__(self, nc, tag):
        self.nc, self.tag, self.phase, self.semaphores = nc, tag, ExitStack(), []

    def __enter__(self):
        return self

    def __exit__(self, kind, *a):
        if kind is None:
            self.phase.close()
            self.nc.clear_and_free_semaphores(self.semaphores)
            self.nc.all_engine_barrier()

    def sb(self, name, shape, dtype=F32):
        return self.phase.enter_context(self.nc.sbuf_tensor(f"{self.tag}_{name}", shape, dtype))

    def ps(self, name, shape):
        return self.phase.enter_context(self.nc.psum_tensor(f"{self.tag}_{name}_ps", shape, F32))

    def sem(self, name):
        self.semaphores.append(self.nc.alloc_semaphore(name=f"{self.tag}_{name}"))
        return self.semaphores[-1]


def kernel_rows_phase(nc, d):
    with Tools(nc, "kr") as T:
        w_in = T.sb("w_in", [2, CH])
        raw_h = T.sb("raw_h", [128, RPE_LAYERS, HALVES, CH])
        raw_out = T.sb("raw_out", [128, HALVES, WIDE])
        w_h = [T.sb(f"w_h_{part}", [128, RPE_LAYERS, HALVES, CH], F32R) for part in ("high", "low")]
        w_out = [T.sb(f"w_out_{part}", [128, HALVES, WIDE], F32R) for part in ("high", "low")]
        bias = T.sb("bias", [128, RPE_LAYERS + 1, HALVES])
        out_bias = T.sb("out_bias", [TAPS, WIDE])
        row_taps = T.sb("row_taps", [TAPS, ROWS])
        mean_ch = T.sb("mean_ch", [128, 128])
        one = T.sb("one", [1, 1])
        coords = T.sb("coords", [2, TAPS_PAD * TAPS])
        t = [T.sb(f"t{u}", [128, HALVES, RPE_CHUNK]) for u in range(2)]
        square = [T.sb(f"square{u}", [128, HALVES, RPE_CHUNK]) for u in range(2)]
        rect = [[T.sb(f"rect{u}_{part}", [128, HALVES, RPE_CHUNK], F32R) for part in ("high", "low")] for u in range(2)]
        root = [T.sb(f"root{u}", [128, RPE_CHUNK]) for u in range(2)]
        scale = [T.sb(f"scale{u}", [128, RPE_CHUNK]) for u in range(2)]
        inv = [T.sb(f"inv{u}", [TAPS, RPE_ROWS]) for u in range(2)]
        coef = [T.sb(f"coef{i}", [TAPS, WIDE]) for i in range(2)]
        rows_out = [T.sb(f"rows_out{u}", [ROWS, RPE_ROWS, WIDE]) for u in range(2)]
        t_ps = [[T.ps(f"t{u}{h}", [128, 512]) for h in range(2)] for u in range(2)]
        ms_ps = [T.ps(f"ms{u}", [128, 512]) for u in range(2)]
        row_ps = [T.ps(f"row{i}", [128, 512]) for i in range(2)]
        COLUMN = 448

        (consts_in, high_consts, low_consts, layer_done, t_ready, high_ready, low_ready, squared, mean_done, rooted,
         scale_ready, column_mm, inverted, coef_mm, coef_done, row_mm, row_out) = (T.sem(n) for n in (
             "consts_in", "high_consts", "low_consts", "layer_done", "t_ready", "high_ready", "low_ready", "squared",
             "mean_done", "rooted", "scale_ready", "column_mm", "inverted", "coef_mm", "coef_done", "row_mm", "row_out"))
        stored = [T.sem(f"stored{u}") for u in range(2)]
        STEPS = TAPS_PAD // RPE_ROWS // 2
        LAYERS = RPE_LAYERS + 1
        PER, TAIL = 2 * LAYERS, 2 * RPE_ROWS
        loads = [(w_in, "rpe_in"), (raw_h, "rpe_h"), (raw_out, "rpe_out"), (bias, "rpe_bias"), (out_bias, "rpe_out_b"),
                 (row_taps, "row_taps"), (mean_ch, "mean_ch"), (coords, "coords")]
        with nc.Block() as block:
            @block.sync
            def _(sp):
                for tile, name in loads:
                    sp.dma_start(tile[:], d[name]).then_inc(consts_in, 16)
                sp.dma_start(one[:], d["ones"][:1, :1]).then_inc(consts_in, 16)
                with sp.Fori(0, STEPS) as s:
                    for u in range(2):
                        sp.wait_ge(row_out, s * TAIL + RPE_ROWS * (u + 1))
                        sp.dma_start(d["kern_rows"][:, bass.ds((s * 2 + u) * RPE_ROWS, RPE_ROWS), :],
                                     rows_out[u][:]).then_inc(stored[u], 16)
                for u in range(2):
                    sp.wait_ge(stored[u], 16 * STEPS)

            @block.tensor
            def _(pe):
                pe.wait_ge(consts_in, 16 * (len(loads) + 1))
                pe.wait_ge(low_consts, 2)
                with pe.Fori(0, STEPS) as s:
                    def mean(n):
                        u = n % 2
                        pe.wait_ge(squared, s * PER + n + 1)
                        if n >= 2:
                            pe.wait_ge(rooted, s * PER + n - 1)
                        for h in range(HALVES):
                            last = nc.tensor.matmul(ms_ps[u][:, :RPE_CHUNK], mean_ch[:], square[u][:, h, :],
                                                    start=h == 0, stop=h == HALVES - 1)
                        last.then_inc(mean_done, 1)

                    for layer in range(LAYERS):
                        for u in range(2):
                            n = 2 * layer + u
                            if layer == 0:
                                pe.wait_ge(coef_done, s * TAIL)
                                for h in range(HALVES):
                                    last = nc.tensor.matmul(t_ps[u][h][:, :RPE_CHUNK], w_in[:, h * 128:(h + 1) * 128],
                                                            coords[:, bass.ds((s * 2 + u) * RPE_CHUNK, RPE_CHUNK)],
                                                            start=True, stop=True)
                            else:
                                for k in range(HALVES):
                                    pe.wait_ge(low_ready, (s * PER + n - 2) * HALVES + k + 1)
                                    for h in range(HALVES):
                                        last = product(nc, t_ps[u][h][:, :RPE_CHUNK],
                                                       [w[:, layer - 1, k, h * 128:(h + 1) * 128] for w in w_h],
                                                       [part[:, k, :] for part in rect[u]], start=k == 0, stop=k == HALVES - 1)
                                    if k == 0:
                                        mean(n - 2)
                            last.then_inc(layer_done, 1)

                    def row_pass(m):
                        pe.wait_ge(coef_done, s * TAIL + m + 1)
                        pe.wait_ge(row_out, s * TAIL + max(m - 1, 0))
                        nc.tensor.matmul(row_ps[m % 2][:ROWS, :], row_taps[:], coef[m % 2][:],
                                         start=True, stop=True).then_inc(row_mm, 1)

                    mean(PER - 2)
                    for u in range(2):
                        pe.wait_ge(low_ready, (s * PER + PER - 1 + u) * HALVES)
                        for r in range(RPE_ROWS):
                            m = RPE_ROWS * u + r
                            if r >= 2:
                                pe.wait_ge(coef_done, s * TAIL + m - 1)
                            for k in range(HALVES):
                                last = product(nc, t_ps[u][r % 2][:TAPS, :],
                                               [part[:, k, r * TAPS:(r + 1) * TAPS] for part in rect[u]],
                                               [w[:, k, :] for w in w_out], start=k == 0, stop=k == HALVES - 1)
                            last.then_inc(coef_mm, 1)
                            if r == 0:
                                if u == 0:
                                    mean(PER - 1)
                                pe.wait_ge(scale_ready, s * PER + PER - 1 + u)
                                for i in range(RPE_ROWS):
                                    last = nc.tensor.matmul(ms_ps[u][:TAPS, COLUMN + i:COLUMN + i + 1],
                                                            scale[u][:1, i * TAPS:(i + 1) * TAPS], one[:], start=True, stop=True)
                                last.then_inc(column_mm, 1)
                            if m:
                                row_pass(m - 1)
                    row_pass(TAIL - 1)

            @block.scalar
            def _(act):
                act.wait_ge(consts_in, 16 * (len(loads) + 1))
                nc.scalar.activation(w_h[0][:], raw_h[:], ACT.Copy).then_inc(high_consts, 1)
                nc.scalar.activation(w_out[0][:], raw_out[:], ACT.Copy).then_inc(high_consts, 1)
                with act.Fori(0, STEPS) as s:
                    def roots(n):
                        act.wait_ge(mean_done, s * PER + n + 1)
                        nc.scalar.activation(root[n % 2][:], ms_ps[n % 2][:, :RPE_CHUNK], ACT.Sqrt).then_inc(rooted, 1)

                    for layer in range(LAYERS):
                        for u in range(2):
                            n = 2 * layer + u
                            for h in range(HALVES):
                                act.wait_ge(t_ready, (s * PER + n) * HALVES + h + 1)
                                nc.scalar.activation(rect[u][0][:, h, :], t[u][:, h, :], ACT.Relu).then_inc(high_ready, 1)
                            nc.scalar.activation(square[u][:], t[u][:], ACT.Square).then_inc(squared, 1)
                            if n:
                                roots(n - 1)
                    roots(PER - 1)
                    for m in range(TAIL):
                        u, r = divmod(m, RPE_ROWS)
                        act.wait_ge(row_mm, s * TAIL + m + 1)
                        if r == 0:
                            act.wait_ge(stored[u], s * 16)
                        nc.scalar.activation(rows_out[u][:, r, :], row_ps[m % 2][:ROWS, :], ACT.Copy).then_inc(row_out, 1)

            @block.vector
            def _(dve):
                dve.wait_ge(consts_in, 16 * (len(loads) + 1))
                for i, (raw, w) in enumerate(((raw_h, w_h), (raw_out, w_out))):
                    dve.wait_ge(high_consts, i + 1)
                    nc.vector.tensor_tensor(w[1][:], raw[:], w[0][:].bitcast(F32), ALU.subtract).then_inc(low_consts, 1)
                with dve.Fori(0, STEPS) as s:
                    def next_scale(n):
                        u = n % 2
                        dve.wait_ge(rooted, s * PER + n + 1)
                        dve.wait_ge(t_ready, (s * PER + n + 1) * HALVES)
                        if n < 2:
                            dve.wait_ge(column_mm, s * 2)
                            nc.vector.tensor_scalar(scale[u][:], root[u][:], RMS_EPS, None, ALU.add).then_inc(scale_ready, 1)
                        else:
                            nc.vector.scalar_tensor_tensor(out=scale[u][:], in0=scale[u][:], scalar=RMS_EPS, in1=root[u][:],
                                                           op0=ALU.mult, op1=ALU.add).then_inc(scale_ready, 1)

                    for layer in range(LAYERS):
                        for u in range(2):
                            n = 2 * layer + u
                            if layer:
                                next_scale(n - 2)
                                dve.wait_ge(scale_ready, s * PER + n - 1)
                            dve.wait_ge(layer_done, s * PER + n + 1)
                            dve.wait_ge(squared, s * PER + max(n - 1, 0))
                            dve.wait_ge(low_ready, (s * PER + max(n - 1, 0)) * HALVES)
                            for h in range(HALVES):
                                if layer == 0:
                                    last = nc.vector.tensor_scalar(t[u][:, h, :], t_ps[u][h][:, :RPE_CHUNK],
                                                                   bias[:, 0, h:h + 1], None, ALU.add)
                                else:
                                    last = nc.vector.scalar_tensor_tensor(
                                        out=t[u][:, h, :], in0=scale[u][:], scalar=bias[:, layer, h:h + 1],
                                        in1=t_ps[u][h][:, :RPE_CHUNK], op0=ALU.mult, op1=ALU.add)
                                last.then_inc(t_ready, 1)
                            for h in range(HALVES):
                                dve.wait_ge(high_ready, (s * PER + n) * HALVES + h + 1)
                                nc.vector.scalar_tensor_tensor(out=rect[u][1][:, h, :], in0=t[u][:, h, :], scalar=0.0,
                                                               in1=rect[u][0][:, h, :].bitcast(F32), op0=ALU.max,
                                                               op1=ALU.subtract).then_inc(low_ready, 1)
                    next_scale(PER - 2)
                    next_scale(PER - 1)
                    for m in range(TAIL):
                        u, r = divmod(m, RPE_ROWS)
                        if r == 0:
                            dve.wait_ge(column_mm, s * 2 + u + 1)
                            nc.vector.reciprocal(inv[u][:], ms_ps[u][:TAPS, COLUMN:COLUMN + RPE_ROWS]).then_inc(inverted, 1)
                            dve.wait_ge(inverted, s * 2 + u + 1)
                        dve.wait_ge(coef_mm, s * TAIL + m + 1)
                        dve.wait_ge(row_mm, s * TAIL + max(m - 1, 0))
                        nc.vector.scalar_tensor_tensor(out=coef[m % 2][:], in0=t_ps[u][r % 2][:TAPS, :], scalar=inv[u][:, r:r + 1],
                                                       in1=out_bias[:], op0=ALU.mult, op1=ALU.add).then_inc(coef_done, 1)


def columns_phase(nc, d):
    with Tools(nc, "co") as T:
        raw_fwd = T.sb("raw_fwd", [2 * SIDE, 2, POINTS])
        raw_taps = T.sb("raw_taps", [TAPS, 3, POINTS])
        parts = ("high", "low")
        col_fwd = [T.sb(f"col_fwd_{part}", [2 * SIDE, 2, POINTS], F32R) for part in parts]
        col_taps = [T.sb(f"col_taps_{part}", [TAPS, 3, POINTS], F32R) for part in parts]
        col_inv = T.sb("col_inv", [POINTS, 2, 2 * SIDE])
        taps_in = T.sb("taps_in", [TAPS, 2, WIDE])
        taps = [T.sb(f"taps_{part}", [TAPS, 2, WIDE], F32R) for part in parts]
        v_in = T.sb("v_in", [2 * SIDE, BATCH, WIDE])
        v = [T.sb(f"v_{part}", [2 * SIDE, BATCH, WIDE], F32R) for part in parts]
        y_out = T.sb("y_out", [2 * SIDE, BATCH, WIDE])
        spec = [T.sb(f"spec{i}", [POINTS, 3 * WIDE]) for i in range(2)]
        direct = [T.sb(f"direct{i}", [POINTS, 2 * WIDE]) for i in range(2)]
        cross = [T.sb(f"cross{i}", [POINTS, 2 * WIDE]) for i in range(2)]
        prod = [T.sb(f"prod{i}", [POINTS, 2 * WIDE]) for i in range(2)]
        v_ps = [T.ps(f"v{i}", [128, 2 * WIDE]) for i in range(2)]
        taps_ps = T.ps("taps", [128, 2 * WIDE])
        y_ps = [T.ps(f"y{i}", [128, WIDE]) for i in range(2)]
        names = ("consts_in", "high_consts", "low_consts", "taps_loaded", "high_taps", "low_taps", "high_v", "low_v", "taps_mm", "spec_ready", "fwd_mm", "multiplied", "combined", "inv_mm", "y_ready")
        (consts_in, high_consts, low_consts, taps_loaded, high_taps, low_taps, high_v, low_v, taps_mm, spec_ready, fwd_mm,
         multiplied, combined, inv_mm, y_ready) = (T.sem(n) for n in names)
        PAIRS = BATCH // 2
        LAG = 2
        v_loaded = [T.sem(f"v_loaded{i}") for i in range(PAIRS)]
        y_stored = [T.sem(f"y_stored{i}") for i in range(PAIRS)]
        HIGH_AHEAD, LOW_AHEAD = 3, 2
        loads = [(raw_fwd, "col_fwd"), (raw_taps, "col_taps"), (col_inv, "col_inv")]
        splits = [(raw_fwd, col_fwd), (raw_taps, col_taps)]

        SLOTS = 2

        def buffer_free(eng, sem, n):
            eng.wait_ge(sem, n + 1)

        def done(eng, sem, n):
            eng.wait_ge(sem, SLOTS + n + 1)

        def pair_ahead(k, b, more, ahead):
            pair = b // 2 + ahead
            if b % 2 == 0 and pair < PAIRS:
                return k, pair
            return (k + 1, pair - PAIRS) if b % 2 == 0 and more else None

        def load_taps(eng, k):
            for part in range(2):
                eng.dma_start(taps_in[:, part, :], d["kern_rows"][k + FREQ * part, 0:TAPS, :]).then_inc(taps_loaded, 16)

        def load_v(eng, k, pair):
            for part in range(2):
                eng.dma_start(v_in[part * SIDE:(part + 1) * SIDE, 2 * pair:2 * pair + 2, :],
                              d["v_rows"][k + FREQ * part, 2 * pair:2 * pair + 2, :, :].rearrange("b i c -> i b c")
                              ).then_inc(v_loaded[pair], 16)

        def store_y(eng, k, pair):
            for part in range(2):
                eng.dma_start(d["y_rows"][k + FREQ * part, 2 * pair:2 * pair + 2, :, :].rearrange("b i c -> i b c"),
                              y_out[part * SIDE:(part + 1) * SIDE, 2 * pair:2 * pair + 2, :]).then_inc(y_stored[pair], 16)

        with nc.Block() as block:
            @block.sync
            def _(sp):
                for tile, name in loads:
                    sp.dma_start(tile[:], d[name]).then_inc(consts_in, 16)
                load_taps(sp, 0)
                for pair in range(PAIRS):
                    load_v(sp, 0, pair)

                def step(k, more):
                    if more:
                        sp.wait_ge(low_taps, k + 1)
                        load_taps(sp, k + 1)
                    for pair in range(PAIRS):
                        if more:
                            sp.wait_ge(low_v, k * PAIRS + pair + 1)
                            load_v(sp, k + 1, pair)
                        done(sp, y_ready, k * BATCH + 2 * pair + 1)
                        store_y(sp, k, pair)

                with sp.Fori(0, FREQ // 2) as s:
                    for i in range(2):
                        step(s * 2 + i, True)
                step(FREQ - 1, False)
                for pair in range(PAIRS):
                    sp.wait_ge(y_stored[pair], 32 * FREQ)

            @block.tensor
            def _(pe):
                pe.wait_ge(consts_in, 16 * len(loads))
                pe.wait_ge(low_consts, len(splits))

                def spectrum(k):
                    pe.wait_ge(low_taps, k + 1)
                    pe.wait_ge(spec_ready, k)
                    for out, (real, imag) in enumerate(((0, 1), (2, 0))):
                        for part, matrix in enumerate((real, imag)):
                            last = product(nc, taps_ps[:POINTS, bass.ts(out, WIDE)], [w[:, matrix, :] for w in col_taps],
                                           [x[:, part, :] for x in taps], start=part == 0, stop=part == 1)
                    last.then_inc(taps_mm, 1)

                def forward(k, b):
                    n = k * BATCH + b
                    pe.wait_ge(low_v, k * PAIRS + b // 2 + 1)
                    buffer_free(pe, multiplied, n)
                    for out in range(2):
                        last = product(nc, v_ps[b % 2][:POINTS, bass.ts(out, WIDE)], [w[:, out, :] for w in col_fwd],
                                       [x[:, b, :] for x in v], start=True, stop=True)
                    last.then_inc(fwd_mm, 1)

                def inverse(k, b):
                    n = k * BATCH + b
                    done(pe, combined, n)
                    buffer_free(pe, y_ready, n)
                    nc.tensor.matmul(y_ps[b % 2][:2 * SIDE, :], col_inv[:, 0, :], prod[b % 2][:, :WIDE], start=True, stop=False)
                    nc.tensor.matmul(y_ps[b % 2][:2 * SIDE, :], col_inv[:, 1, :], prod[b % 2][:, WIDE:],
                                     start=False, stop=True).then_inc(inv_mm, 1)

                def step(k, more):
                    for b in range(LAG, BATCH):
                        if b == BATCH // 2 and more:
                            spectrum(k + 1)
                        forward(k, b)
                        inverse(k, b - LAG)
                    for b in range(LAG):
                        if more:
                            forward(k + 1, b)
                        inverse(k, BATCH - LAG + b)

                pe.sem_inc(inv_mm, SLOTS)
                spectrum(0)
                for b in range(LAG):
                    forward(0, b)
                with pe.Fori(0, FREQ // 2) as s:
                    for i in range(2):
                        step(s * 2 + i, True)
                step(FREQ - 1, False)

            @block.scalar
            def _(act):
                def split_v(k, pair):
                    act.wait_ge(v_loaded[pair], k * 32 + 32)
                    images = slice(2 * pair, 2 * pair + 2)
                    nc.scalar.activation(v[0][:, images, :], v_in[:, images, :], ACT.Copy).then_inc(high_v, 1)

                def split_taps(k):
                    act.wait_ge(taps_loaded, k * 32 + 32)
                    nc.scalar.activation(taps[0][:], taps_in[:], ACT.Copy).then_inc(high_taps, 1)

                def spectrum(k, i):
                    act.wait_ge(taps_mm, k + 1)
                    for col, part in ((0, 0), (1, 1), (2, 0)):
                        last = nc.scalar.activation(spec[i][:, bass.ts(col, WIDE)], taps_ps[:POINTS, bass.ts(part, WIDE)], ACT.Copy)
                    last.then_inc(spec_ready, 1)

                def step(k, i, more):
                    for b in range(BATCH):
                        if b == 0 and more:
                            split_taps(k + 1)
                        if b == BATCH // 2 and more:
                            spectrum(k + 1, 1 - i)
                        ahead = pair_ahead(k, b, more, HIGH_AHEAD)
                        if ahead:
                            split_v(*ahead)
                        done(act, inv_mm, k * BATCH + b)
                        if b % 2 == 0:
                            act.wait_ge(y_stored[b // 2], k * 32)
                        nc.scalar.activation(y_out[:, b, :], y_ps[b % 2][:2 * SIDE, :], ACT.Copy).then_inc(y_ready, 1)

                act.sem_inc(y_ready, SLOTS)
                act.wait_ge(consts_in, 16 * len(loads))
                for raw, split in splits:
                    nc.scalar.activation(split[0][:], raw[:], ACT.Copy).then_inc(high_consts, 1)
                split_taps(0)
                for pair in range(HIGH_AHEAD):
                    split_v(0, pair)
                spectrum(0, 0)
                with act.Fori(0, FREQ // 2) as s:
                    for i in range(2):
                        step(s * 2 + i, i, True)
                step(FREQ - 1, 0, False)

            @block.vector
            def _(dve):
                def split_v(k, pair):
                    dve.wait_ge(high_v, k * PAIRS + pair + 1)
                    images = slice(2 * pair, 2 * pair + 2)
                    nc.vector.tensor_tensor(v[1][:, images, :], v_in[:, images, :], v[0][:, images, :].bitcast(F32),
                                            ALU.subtract).then_inc(low_v, 1)

                def split_taps(k):
                    dve.wait_ge(high_taps, k + 1)
                    nc.vector.tensor_tensor(taps[1][:], taps_in[:], taps[0][:].bitcast(F32), ALU.subtract).then_inc(low_taps, 1)

                dve.sem_inc(multiplied, SLOTS)
                for i, (raw, split) in enumerate(splits):
                    dve.wait_ge(high_consts, i + 1)
                    nc.vector.tensor_tensor(split[1][:], raw[:], split[0][:].bitcast(F32), ALU.subtract).then_inc(low_consts, 1)
                split_taps(0)
                for pair in range(LOW_AHEAD):
                    split_v(0, pair)

                def step(k, i, more):
                    dve.wait_ge(spec_ready, k + 1)
                    for b in range(BATCH):
                        dve.wait_ge(fwd_mm, k * BATCH + b + 1)
                        buffer_free(dve, combined, k * BATCH + b)
                        nc.vector.tensor_tensor(direct[b % 2][:], v_ps[b % 2][:POINTS, :], spec[i][:, :2 * WIDE], ALU.mult)
                        nc.vector.tensor_tensor(cross[b % 2][:], v_ps[b % 2][:POINTS, :], spec[i][:, WIDE:],
                                                ALU.mult).then_inc(multiplied, 1)
                        if b == 2 and more:
                            split_taps(k + 1)
                        ahead = pair_ahead(k, b, more, LOW_AHEAD)
                        if ahead:
                            split_v(*ahead)

                with dve.Fori(0, FREQ // 2) as s:
                    for i in range(2):
                        step(s * 2 + i, i, True)
                step(FREQ - 1, 0, False)

            @block.gpsimd
            def _(pool):
                pool.sem_inc(combined, SLOTS)

                def step(k):
                    for b in range(BATCH):
                        done(pool, multiplied, k * BATCH + b)
                        buffer_free(pool, inv_mm, k * BATCH + b)
                        nc.gpsimd.tensor_tensor(prod[b % 2][:, :WIDE], direct[b % 2][:, :WIDE], direct[b % 2][:, WIDE:], ALU.subtract)
                        nc.gpsimd.tensor_tensor(prod[b % 2][:, WIDE:], cross[b % 2][:, :WIDE], cross[b % 2][:, WIDE:],
                                                ALU.add).then_inc(combined, 1)

                with pool.Fori(0, FREQ // 2) as s:
                    for i in range(2):
                        step(s * 2 + i)
                step(FREQ - 1)


def stats_phase(nc, d):
    with Tools(nc, "st") as T:
        ident, group_mean = T.sb("ident", [128, 128]), T.sb("group_mean", [128, 128])
        x_in = [T.sb(f"x_in{i}", [TILE, TILES, CH]) for i in range(CHUNKS)]
        stats = T.sb("stats", [128, HALVES, CHUNKS, 6])
        moments = T.sb("moments", [128, HALVES, 2])
        off, off2 = T.sb("off", [128, HALVES]), T.sb("off2", [128, HALVES])
        var, root, scale, shift = (T.sb(n, [128, HALVES]) for n in ("var", "root", "scale", "shift"))
        rows = T.sb("rows", [128, 2 * CH])
        x_ps = [[T.ps(f"x{i}{h}", [128, 512]) for h in range(2)] for i in range(2)]
        group_ps, row_ps = T.ps("group", [128, 512]), T.ps("row", [128, 512])
        consts_in, transposed, measured, chain, group_mm, rooted, row_mm, rows_made, rows_stored = (
            T.sem(n) for n in ("consts_in", "transposed", "measured", "chain", "group_mm", "rooted", "row_mm",
                               "rows_made", "rows_stored"))
        seen = T.sem("seen")
        x_loaded = [T.sem(f"x_loaded{i}") for i in range(CHUNKS)]
        LINKS = 8

        def over_images(eng, image, finish):
            image(0, False)
            with eng.Fori(1, BATCH) as b:
                image(b, True)
            finish(BATCH - 1)

        with nc.Block() as block:
            @block.sync
            def _(sp):
                sp.dma_start(ident[:], d["ident"]).then_inc(consts_in, 16)
                sp.dma_start(group_mean[:], d["group_mean"]).then_inc(consts_in, 16)
                for j in range(CHUNKS):
                    sp.dma_start(x_in[j][:], d["x_tiles"][j]).then_inc(x_loaded[j], 16)
                with sp.Fori(1, BATCH) as b:
                    for j in range(CHUNKS):
                        sp.wait_ge(transposed, (b - 1) * CHUNKS + j + 1)
                        sp.dma_start(x_in[j][:], d["x_tiles"][b * CHUNKS + j]).then_inc(x_loaded[j], 16)

            @block.tensor
            def _(pe):
                pe.wait_ge(consts_in, 32)

                def group_means(b, step):
                    if step == 0:
                        pe.wait_ge(chain, b * LINKS + 1)
                        nc.tensor.matmul(group_ps[:, 0:4], group_mean[:], moments[:].rearrange("p h m -> p (h m)"),
                                         start=True, stop=True).then_inc(group_mm, 1)
                    elif step == 2:
                        pe.wait_ge(chain, b * LINKS + 3)
                        nc.tensor.matmul(group_ps[:, 4:6], group_mean[:], off2[:], start=True, stop=True).then_inc(group_mm, 1)
                    elif step == 5:
                        pe.wait_ge(chain, b * LINKS + 8)
                        for i, col in enumerate((scale, shift)):
                            for h in range(HALVES):
                                at = (i * HALVES + h) * 128
                                last = nc.tensor.matmul(row_ps[:, at:at + 128], col[:, h:h + 1].to_broadcast([128, 128]),
                                                        ident[:], start=True, stop=True)
                        last.then_inc(row_mm, 1)

                def image(b, before):
                    for j in range(CHUNKS):
                        pe.wait_ge(x_loaded[j], b * 16 + 16)
                        pe.wait_ge(measured, b * CHUNKS + max(j - 1, 0))
                        for t in range(TILES):
                            for h in range(HALVES):
                                last = nc.tensor.transpose(x_ps[j % 2][h][:, t * TILE:(t + 1) * TILE],
                                                           x_in[j][:, t, h * 128:(h + 1) * 128], ident[:TILE, :TILE])
                        last.then_inc(transposed, 1)
                        if before:
                            group_means(b - 1, j)

                def finish(b):
                    for j in range(CHUNKS):
                        group_means(b, j)

                over_images(pe, image, finish)

            @block.scalar
            def _(act):
                with act.Fori(0, BATCH) as b:
                    act.wait_ge(chain, b * LINKS + 5)
                    nc.scalar.activation(root[:], var[:], ACT.Sqrt).then_inc(rooted, 1)
                    act.wait_ge(rows_made, b + 1)
                    for j in range(CHUNKS):
                        act.dma_start(d["gn_rows"][b * CHUNKS + j], rows[0:1, :]).then_inc(rows_stored, 16)
                act.wait_ge(rows_stored, 16 * BATCH * CHUNKS)

            @block.vector
            def _(dve):
                group = group_ps[:, 0:4].rearrange("p (h m) -> p h m", m=2)

                def normalisers(b, step):
                    if step == 1:
                        dve.wait_ge(group_mm, b * 2 + 1)
                        nc.vector.tensor_tensor(off[:], moments[:, :, 0], group[:, :, 0], ALU.subtract).then_inc(chain, 1)
                        dve.wait_ge(chain, b * LINKS + 2)
                        nc.vector.tensor_tensor(off2[:], off[:], off[:], ALU.mult).then_inc(chain, 1)
                    elif step == 3:
                        dve.wait_ge(group_mm, b * 2 + 2)
                        nc.vector.tensor_scalar(var[:], group_ps[:, 4:6], GN_EPS, None, ALU.add).then_inc(chain, 1)
                        dve.wait_ge(chain, b * LINKS + 4)
                        nc.vector.tensor_tensor(var[:], var[:], group[:, :, 1], ALU.add).then_inc(chain, 1)
                    elif step == 4:
                        dve.wait_ge(rooted, b + 1)
                        nc.vector.reciprocal(scale[:], root[:]).then_inc(chain, 1)
                        dve.wait_ge(chain, b * LINKS + 6)
                        nc.vector.tensor_tensor(shift[:], scale[:], group[:, :, 0], ALU.mult).then_inc(chain, 1)
                        dve.wait_ge(chain, b * LINKS + 7)
                        nc.vector.tensor_scalar(shift[:], shift[:], -1.0, None, ALU.mult).then_inc(chain, 1)
                    elif step == 6:
                        dve.wait_ge(row_mm, b + 1)
                        dve.wait_ge(rows_stored, b * 16 * CHUNKS)
                        nc.vector.tensor_copy(rows[:], row_ps[:, :2 * CH]).then_inc(rows_made, 1)

                def image(b, before):
                    if before:
                        dve.wait_ge(chain, (b - 1) * LINKS + 1)
                    for j in range(CHUNKS):
                        dve.wait_ge(transposed, b * CHUNKS + j + 1)
                        for h in range(HALVES):
                            last = nc.vector.bn_stats(stats[:, h, j, :], x_ps[j % 2][h][:, :CHUNK])
                        last.then_inc(measured, 1)
                        if before:
                            normalisers(b - 1, j)
                    dve.wait_ge(measured, b * CHUNKS + CHUNKS)
                    dve.sem_inc(seen, 1)
                    nc.vector.bn_aggr(moments[:, 0, :], stats[:, 0, :, :])
                    nc.vector.bn_aggr(moments[:, 1, :], stats[:, 1, :, :]).then_inc(chain, 1)

                def finish(b):
                    for j in range(CHUNKS):
                        normalisers(b, j)

                over_images(dve, image, finish)


def project_phase(nc, d):
    with Tools(nc, "pr") as T:
        parts = ("high", "low")
        raw_v = T.sb("raw_v", [128, HALVES, WIDE])
        raw_fwd = T.sb("raw_fwd", [TILE, 2, ROWS])
        w_v = [T.sb(f"w_v_{part}", [128, HALVES, WIDE], F32R) for part in parts]
        row_fwd = [T.sb(f"row_fwd_{part}", [TILE, 2, ROWS], F32R) for part in parts]
        v_bias = T.sb("v_bias", [TILE, WIDE])
        ident = T.sb("ident", [128, 128])
        x_in = [T.sb(f"x_in{u}", [TILE, TILES, CH]) for u in range(2)]
        gn = [T.sb(f"gn{u}", [TILE, 2, CH]) for u in range(2)]
        gx = [T.sb(f"gx{u}", [TILE, TILES, CH]) for u in range(2)]
        xn = [T.sb(f"xn{u}", [TILE, TILES, CH]) for u in range(2)]
        junk = T.sb("junk", [TILE, TILES, CH])
        ssum, root, guarded, inv = (T.sb(n, [TILE, 2 * TILES]) for n in ("ssum", "root", "guarded", "inv"))
        xn_t = [T.sb(f"xn_t{u}", [128, HALVES, CHUNK]) for u in range(2)]
        xn_parts = [[T.sb(f"xn_t{u}_{part}", [128, HALVES, CHUNK], F32R) for part in parts] for u in range(2)]
        v_pre = [T.sb(f"v_pre{i}", [TILE, WIDE]) for i in range(2)]
        v = [T.sb(f"v{t}", [TILE, WIDE]) for t in range(TILES)]
        v_parts = [[T.sb(f"v{t}_{part}", [TILE, WIDE], F32R) for part in parts] for t in range(TILES)]
        rows_out = [T.sb(f"rows_out{u}", [ROWS, CHUNK_ROWS, WIDE]) for u in range(2)]
        xt_ps = [T.ps(f"xt{h}", [128, 512]) for h in range(2)]
        v_ps = [T.ps(f"v{i}", [128, 512]) for i in range(2)]
        row_ps = [[T.ps(f"row{i}{r}", [128, 512]) for r in range(2)] for i in range(2)]
        (consts_in, high_consts, low_consts, scaled, gx_ready, squared, rooted, eps_added, inverted, xn_ready, xt_mm, xt_ready,
         high_x, low_x, v_mm, biased, v_ready, high_v, low_v, row_mm, row0_out, row1_out) = (T.sem(n) for n in (
             "consts_in", "high_consts", "low_consts", "scaled", "gx_ready", "squared", "rooted", "eps_added", "inverted",
             "xn_ready", "xt_mm", "xt_ready", "high_x", "low_x", "v_mm", "biased", "v_ready", "high_v", "low_v", "row_mm",
             "row0_out", "row1_out"))
        loaded, xn_stored, rows_stored = ([T.sem(f"{n}{u}") for u in range(2)] for n in ("loaded", "xn_stored", "rows_stored"))
        PAIRS = BATCH * CHUNKS // 2
        LAG = 2
        loads = [(raw_v, "w_v"), (raw_fwd, "row_fwd"), (v_bias, "v_bias"), (ident, "ident")]
        splits = [(raw_v, w_v), (raw_fwd, row_fwd)]

        SLOTS = 2

        def number(chunk):
            return 2 * chunk[0] + chunk[1]

        def buffer_free(eng, sem, n):
            eng.wait_ge(sem, n + 1)

        def done(eng, sem, n):
            eng.wait_ge(sem, SLOTS + n + 1)

        def all_steps(eng, step):
            with eng.Fori(0, PAIRS - 2) as s:
                step((s, 0), (s, 1), (s + 1, 1), s + 1)
                step((s, 1), (s + 1, 0), (s + 2, 0), None)
            last = PAIRS - 1
            step((last - 1, 0), (last - 1, 1), (last, 1), last)
            step((last - 1, 1), (last, 0), None, None)
            step((last, 0), (last, 1), None, None)
            step((last, 1), None, None, None)

        with nc.Block() as block:
            @block.sync
            def _(sp):
                def load(s, u, first=False):
                    if not first:
                        sp.wait_ge(gx_ready, 2 * s + u - 1)
                    sp.dma_start(x_in[u][:], d["x_tiles"][2 * s + u]).then_inc(loaded[u], 16)
                    sp.dma_start(gn[u][:].rearrange("p a c -> p (a c)"), d["gn_rows"][2 * s + u].to_broadcast([TILE, 2 * CH])
                                 ).then_inc(loaded[u], 16)

                def store_xn(s, u):
                    sp.wait_ge(xt_ready, 2 * s + u + 1)
                    sp.dma_start(d["xn_t"][2 * s + u], xn_t[u][:]).then_inc(xn_stored[u], 16)

                def store_rows(s, u):
                    done(sp, row0_out, (2 * s + u) * TILES + TILES - 1)
                    done(sp, row1_out, (2 * s + u) * TILES + TILES - 1)
                    sp.dma_start(rows_of_chunk(d["v_rows"], 2 * s + u), rows_out[u][:]).then_inc(rows_stored[u], 16)

                load(0, 0, first=True)
                load(0, 1, first=True)
                for tile, name in loads:
                    sp.dma_start(tile[:], d[name]).then_inc(consts_in, 16)
                load(1, 0)
                load(1, 1)
                store_xn(0, 0)
                with sp.Fori(0, PAIRS - 2) as s:
                    for u in range(2):
                        load(s + 2, u)
                        store_xn(s + u, 1 - u)
                        store_rows(s, u)
                for s in (PAIRS - 2, PAIRS - 1):
                    for u in range(2):
                        if (s, u) != (PAIRS - 1, 1):
                            store_xn(s + u, 1 - u)
                        store_rows(s, u)
                for u in range(2):
                    sp.wait_ge(xn_stored[u], 16 * PAIRS)
                    sp.wait_ge(rows_stored[u], 16 * PAIRS)

            @block.gpsimd
            def _(pool):
                def normalise(s, u):
                    g = 2 * s + u
                    pool.wait_ge(loaded[u], s * 32 + 32)
                    nc.gpsimd.tensor_tensor(gx[u][:], x_in[u][:], gn[u][:, 0:1, :].to_broadcast([TILE, TILES, CH]),
                                            ALU.mult).then_inc(scaled, 1)
                    pool.wait_ge(scaled, g + 1)
                    nc.gpsimd.tensor_tensor(gx[u][:], gx[u][:], gn[u][:, 1:2, :].to_broadcast([TILE, TILES, CH]),
                                            ALU.add).then_inc(gx_ready, 1)

                def scale(s, u, first=False):
                    g = 2 * s + u
                    pool.wait_ge(inverted, s + 1)
                    if not first:
                        pool.wait_ge(xt_mm, g - 1)
                    each = inv[:, u * TILES:(u + 1) * TILES].unsqueeze(2).to_broadcast([TILE, TILES, CH])
                    nc.gpsimd.tensor_tensor(xn[u][:], gx[u][:], each, ALU.mult).then_inc(xn_ready, 1)
                    pool.wait_ge(xn_ready, g + 1)

                normalise(0, 0)
                normalise(0, 1)
                for u in range(2):
                    scale(0, u, first=True)
                    normalise(1, u)
                with pool.Fori(0, PAIRS - 2) as s:
                    for u in range(2):
                        scale(s + 1, u)
                        normalise(s + 2, u)
                for u in range(2):
                    scale(PAIRS - 1, u)

            @block.tensor
            def _(pe):
                pe.wait_ge(consts_in, 16 * len(loads))
                pe.wait_ge(low_consts, len(splits))

                def front(s, u):
                    g = 2 * s + u
                    pe.wait_ge(xn_ready, g + 1)
                    pe.wait_ge(xt_ready, g)
                    pe.wait_ge(high_x, g)
                    for h in range(HALVES):
                        for t in range(TILES):
                            last = nc.tensor.transpose(xt_ps[h][:, t * TILE:(t + 1) * TILE], xn[u][:, t, h * 128:(h + 1) * 128],
                                                       ident[:TILE, :TILE])
                    last.then_inc(xt_mm, 1)

                def project(s, u, t):
                    g = 2 * s + u
                    pe.wait_ge(low_x, g + 1)
                    buffer_free(pe, biased, g * TILES + t)
                    for h in range(HALVES):
                        last = product(nc, v_ps[t % 2][:TILE, :], [x[:, h, t * TILE:(t + 1) * TILE] for x in xn_parts[u]],
                                       [w[:, h, :] for w in w_v], start=h == 0, stop=h == HALVES - 1)
                    last.then_inc(v_mm, 1)

                def row_pass(s, u, t):
                    n = (2 * s + u) * TILES + t
                    pe.wait_ge(low_v, n + 1)
                    buffer_free(pe, row0_out, n)
                    buffer_free(pe, row1_out, n)
                    for r in range(2):
                        last = product(nc, row_ps[t % 2][r][:ROWS, :], [w[:, r, :] for w in row_fwd],
                                       [x[:] for x in v_parts[t]], start=True, stop=True)
                    last.then_inc(row_mm, 1)

                def step(now, after, squares_of, roots_of):
                    if after:
                        front(*after)
                    for t in range(LAG, TILES):
                        project(*now, t)
                        row_pass(*now, t - LAG)
                    for t in range(LAG):
                        if after:
                            project(*after, t)
                        row_pass(*now, t + TILES - LAG)

                front(0, 0)
                for t in range(LAG):
                    project(0, 0, t)
                all_steps(pe, step)

            @block.scalar
            def _(act):
                act.sem_inc(v_ready, SLOTS)
                act.sem_inc(row0_out, SLOTS)
                def squares(s, u):
                    g = 2 * s + u
                    act.wait_ge(gx_ready, g + 1)
                    act.wait_ge(rooted, s)
                    act.wait_ge(squared, g)
                    for t in range(TILES):
                        last = nc.scalar.activation(junk[:, t, :], gx[u][:, t, :], ACT.Square,
                                                    accum_out=ssum[:, u * TILES + t:u * TILES + t + 1])
                    last.then_inc(squared, 1)

                def roots(s):
                    act.wait_ge(squared, 2 * s + 2)
                    act.wait_ge(eps_added, s)
                    nc.scalar.activation(root[:], ssum[:], ACT.Sqrt, scale=1.0 / CH).then_inc(rooted, 1)

                def take_xt(s, u, first=False):
                    g = 2 * s + u
                    act.wait_ge(xt_mm, g + 1)
                    if not first:
                        act.wait_ge(v_mm, (g - 1) * TILES)
                        act.wait_ge(low_x, g - 1)
                    act.wait_ge(xn_stored[u], s * 16)
                    for h in range(HALVES):
                        last = nc.scalar.activation(xn_parts[u][0][:, h, :], xt_ps[h][:, :CHUNK], ACT.Copy)
                    last.then_inc(high_x, 1)
                    for h in range(HALVES):
                        last = nc.scalar.activation(xn_t[u][:, h, :], xt_ps[h][:, :CHUNK], ACT.Copy)
                    last.then_inc(xt_ready, 1)

                def gate(chunk, t, rows_before):
                    n = number(chunk) * TILES + t
                    done(act, biased, n)
                    act.wait_ge(row_mm, rows_before)
                    nc.scalar.activation(v[t][:], v_pre[t % 2][:], ACT.Silu).then_inc(v_ready, 1)
                    done(act, v_ready, n)
                    nc.scalar.activation(v_parts[t][0][:], v[t][:], ACT.Copy).then_inc(high_v, 1)

                def take_row(s, u, t):
                    act.wait_ge(row_mm, (2 * s + u) * TILES + t + 1)
                    if t == 0:
                        act.wait_ge(rows_stored[u], s * 16)
                    nc.scalar.activation(rows_out[u][:, 2 * t, :], row_ps[t % 2][0][:ROWS, :], ACT.Copy).then_inc(row0_out, 1)

                def step(now, after, squares_of, roots_of):
                    g = number(now)
                    if after:
                        take_xt(*after)
                    for t in range(LAG, TILES):
                        gate(now, t, g * TILES)
                        take_row(*now, t - LAG)
                        if t == LAG and squares_of:
                            squares(*squares_of)
                        if t == LAG and roots_of is not None:
                            roots(roots_of)
                    for t in range(LAG):
                        if after:
                            gate(after, t, g * TILES + t + 1)
                        take_row(*now, t + TILES - LAG)

                squares(0, 0)
                squares(0, 1)
                roots(0)
                act.wait_ge(consts_in, 16 * len(loads))
                for raw, split in splits:
                    nc.scalar.activation(split[0][:], raw[:], ACT.Copy).then_inc(high_consts, 1)
                take_xt(0, 0, first=True)
                for t in range(LAG):
                    gate((0, 0), t, 0)
                squares(1, 0)
                all_steps(act, step)

            @block.vector
            def _(dve):
                dve.sem_inc(biased, SLOTS)
                dve.sem_inc(row1_out, SLOTS)
                def invert(s):
                    dve.wait_ge(rooted, s + 1)
                    nc.vector.tensor_scalar(guarded[:], root[:], RMS_EPS, None, ALU.add).then_inc(eps_added, 1)
                    dve.wait_ge(eps_added, s + 1)
                    dve.wait_ge(xn_ready, 2 * s)
                    nc.vector.reciprocal(inv[:], guarded[:]).then_inc(inverted, 1)

                def low_xn(s, u):
                    g = 2 * s + u
                    dve.wait_ge(high_x, g + 1)
                    dve.wait_ge(xt_ready, g + 1)
                    high, low = xn_parts[u]
                    nc.vector.tensor_tensor(low[:], xn_t[u][:], high[:].bitcast(F32), ALU.subtract).then_inc(low_x, 1)

                def bias(chunk, t):
                    n = number(chunk) * TILES + t
                    dve.wait_ge(v_mm, n + 1)
                    buffer_free(dve, v_ready, n)
                    nc.vector.tensor_tensor(v_pre[t % 2][:], v_ps[t % 2][:TILE, :], v_bias[:], ALU.add).then_inc(biased, 1)

                def low_part(chunk, t):
                    dve.wait_ge(high_v, number(chunk) * TILES + t + 1)
                    high, low = v_parts[t]
                    nc.vector.tensor_tensor(low[:], v[t][:], high[:].bitcast(F32), ALU.subtract).then_inc(low_v, 1)

                def take_row(s, u, t):
                    dve.wait_ge(row_mm, (2 * s + u) * TILES + t + 1)
                    if t == 0:
                        dve.wait_ge(rows_stored[u], s * 16)
                    nc.vector.tensor_copy(rows_out[u][:, 2 * t + 1, :], row_ps[t % 2][1][:ROWS, :]).then_inc(row1_out, 1)

                def step(now, after, squares_of, roots_of):
                    bias(now, 2)
                    low_part(now, 1)
                    if after:
                        low_xn(*after)
                    take_row(*now, 0)
                    bias(now, 3)
                    low_part(now, 2)
                    take_row(*now, 1)
                    if roots_of is not None:
                        invert(roots_of)
                    if after:
                        bias(after, 0)
                    low_part(now, 3)
                    take_row(*now, 2)
                    if after:
                        bias(after, 1)
                        low_part(after, 0)
                    take_row(*now, 3)

                invert(0)
                dve.wait_ge(consts_in, 16 * len(loads))
                for i, (raw, split) in enumerate(splits):
                    dve.wait_ge(high_consts, i + 1)
                    nc.vector.tensor_tensor(split[1][:], raw[:], split[0][:].bitcast(F32), ALU.subtract).then_inc(low_consts, 1)
                low_xn(0, 0)
                bias((0, 0), 0)
                bias((0, 0), 1)
                low_part((0, 0), 0)
                all_steps(dve, step)


def mix_phase(nc, d):
    with Tools(nc, "mx") as T:
        parts = ("high", "low")
        w_u = [T.sb(f"w_u_{part}", [128, HALVES, WIDE], F32R) for part in parts]
        u_bias = T.sb("u_bias", [128, WIDE // 128])
        w_o = [T.sb(f"w_o_{part}", [128, WIDE // 128, CH], F32R) for part in parts]
        o_bias = T.sb("o_bias", [TILE, CH])
        row_inv = T.sb("row_inv", [ROWS, SIDE])
        ident = T.sb("ident", [128, 128])
        y_in = [T.sb(f"y_in{u}", [ROWS, CHUNK_ROWS, WIDE]) for u in range(2)]
        xn_in = [T.sb(f"xn_in{u}", [128, HALVES, CHUNK]) for u in range(2)]
        xn_t = [[T.sb(f"xn_t{u}_{part}", [128, HALVES, CHUNK], F32R) for part in parts] for u in range(2)]
        x_in = [T.sb(f"x_in{u}", [TILE, TILES, CH]) for u in range(2)]
        gn = [T.sb(f"gn{u}", [TILE, 2, CH]) for u in range(2)]
        scale1, shift1 = ([T.sb(f"{n}{u}", [TILE, CH]) for u in range(2)] for n in ("scale1", "shift1"))
        resid = [T.sb(f"resid{u}", [TILE, TILES, CH]) for u in range(2)]
        gate = [T.sb(f"gate{u}", [128, WIDE // 128, CHUNK]) for u in range(2)]
        gated = [T.sb(f"gated{u}", [128, WIDE // 128, CHUNK]) for u in range(2)]
        mixed = [[T.sb(f"mixed{u}_{part}", [128, WIDE // 128, CHUNK], F32R) for part in parts] for u in range(2)]
        t1 = [T.sb(f"t1{u}", [TILE, TILES, CH]) for u in range(2)]
        stats = T.sb("stats", [TILE, TILES, 6])
        moments = [T.sb(f"moments{u}", [TILE, TILES, 2]) for u in range(2)]
        var, root, inv, shift = ([T.sb(f"{n}{u}", [TILE, TILES]) for u in range(2)] for n in ("var", "root", "inv", "shift"))
        n1 = [T.sb(f"n1{u}", [TILE, TILES, CH]) for u in range(2)]
        n1_t = [T.sb(f"n1_t{u}", [128, HALVES, CHUNK]) for u in range(2)]
        BLOCKS = WIDE // 128
        y_ps = [T.ps(f"y{c}", [128, 512]) for c in range(BLOCKS)]
        u_ps = [T.ps(f"u{i}", [128, 512]) for i in range(2)]
        o_ps = [T.ps(f"o{i}", [128, 512]) for i in range(2)]
        (high_consts, low_consts, high_x, low_x, high_mixed, low_mixed, consts_in, row_prep, scaled_x, resid_ready, u_mm, gate_ready, y_mm, mixed_ready, o_mm, t1_ready, measured, aggregated,
         var_ready, rooted, inverted, shift_ready, n1_ready, nt_mm, nt0_ready, nt1_ready) = (T.sem(n) for n in (
             "high_consts", "low_consts", "high_x", "low_x", "high_mixed", "low_mixed", "consts_in", "row_prep", "scaled_x", "resid_ready", "u_mm", "gate_ready", "y_mm", "mixed_ready", "o_mm", "t1_ready",
             "measured", "aggregated", "var_ready", "rooted", "inverted", "shift_ready", "n1_ready", "nt_mm", "nt0_ready",
             "nt1_ready"))
        xn_loaded, y_loaded, x_loaded, t1_stored, nt_stored = (
            [T.sem(f"{n}{u}") for u in range(2)] for n in ("xn_loaded", "y_loaded", "x_loaded", "t1_stored", "nt_stored"))
        seen = T.sem("seen")
        PAIRS = BATCH * CHUNKS // 2
        raw_u = gate[0][:].rearrange("p c t -> p (c t)")[:, :HALVES * WIDE].rearrange("p (h c) -> p h c", h=HALVES)
        raw_o = gate[1][:].rearrange("p c t -> p (c t)")[:, :WIDE // 128 * CH].rearrange("p (b c) -> p b c", b=WIDE // 128)
        splits = [(raw_u, w_u), (raw_o, w_o)]
        loads = [(u_bias, "u_bias"), (o_bias, "o_bias"), (row_inv, "row_inv"), (ident, "ident")]

        def all_steps(eng, step):
            last = PAIRS - 1
            step(None, (0, 0), (0, 1), (1, 0))
            step((0, 0), (0, 1), (1, 0), (1, 1))
            with eng.Fori(1, last) as s:
                step((s - 1, 1), (s, 0), (s, 1), (s + 1, 0))
                step((s, 0), (s, 1), (s + 1, 0), (s + 1, 1))
            step((last - 1, 1), (last, 0), (last, 1), None)
            step((last, 0), (last, 1), None, None)

        with nc.Block() as block:
            @block.sync
            def _(sp):
                for tile, name in loads:
                    sp.dma_start(tile[:], d[name]).then_inc(consts_in, 16)
                sp.dma_start(raw_u, d["w_u"]).then_inc(consts_in, 16)
                sp.dma_start(raw_o, d["w_o"]).then_inc(consts_in, 16)
                with sp.Fori(0, PAIRS) as s:
                    for u in range(2):
                        g = s * 2 + u
                        sp.wait_ge(low_x, s * 2)
                        sp.dma_start(xn_in[u][:], d["xn_t"][g]).then_inc(xn_loaded[u], 16)
                        sp.wait_ge(resid_ready, s * 2)
                        sp.dma_start(x_in[u][:], d["x_tiles"][g]).then_inc(x_loaded[u], 16)
                        sp.dma_start(gn[u][:].rearrange("p a c -> p (a c)"), d["gn_rows"][g].to_broadcast([TILE, 2 * CH])
                                     ).then_inc(x_loaded[u], 16)
                        sp.wait_ge(y_mm, s * 2 * BLOCKS)
                        sp.dma_start(y_in[u][:], rows_of_chunk(d["y_rows"], g)).then_inc(y_loaded[u], 16)

            @block.gpsimd
            def _(pool):
                pool.wait_ge(consts_in, 16 * (len(loads) + 2))
                with pool.Fori(0, PAIRS) as s:
                    for u in range(2):
                        g = s * 2 + u
                        pool.wait_ge(x_loaded[u], s * 32 + 32)
                        pool.wait_ge(t1_ready, s * 2 * 2)
                        nc.gpsimd.tensor_tensor(shift1[u][:], gn[u][:, 1, :], o_bias[:], ALU.add)
                        nc.gpsimd.tensor_scalar(scale1[u][:], gn[u][:, 0, :], 1.0, 1.0, ALU.mult, ALU.add).then_inc(row_prep, 1)
                        pool.wait_ge(row_prep, g + 1)
                        nc.gpsimd.tensor_tensor(resid[u][:], x_in[u][:], scale1[u][:].unsqueeze(1).to_broadcast([TILE, TILES, CH]),
                                                ALU.mult).then_inc(scaled_x, 1)
                        pool.wait_ge(scaled_x, g + 1)
                        nc.gpsimd.tensor_tensor(resid[u][:], resid[u][:], shift1[u][:].unsqueeze(1).to_broadcast([TILE, TILES, CH]),
                                                ALU.add).then_inc(resid_ready, 1)

            @block.tensor
            def _(pe):
                pe.wait_ge(consts_in, 16 * (len(loads) + 2))

                pe.wait_ge(low_consts, len(splits))

                def gate_mm(s, u, blocks):
                    g = 2 * s + u
                    pe.wait_ge(low_x, g + 1)
                    for c in blocks:
                        pe.wait_ge(gate_ready, g * BLOCKS + max(c - 1, 0))
                        for h in range(HALVES):
                            last = product(nc, u_ps[c % 2][:, :CHUNK], [w[:, h, c * 128:(c + 1) * 128] for w in w_u],
                                           [x[:, h, :] for x in xn_t[u]], start=h == 0, stop=h == HALVES - 1)
                        last.then_inc(u_mm, 1)

                def inverse_rows(s, u, first=False):
                    g = 2 * s + u
                    pe.wait_ge(y_loaded[u], s * 16 + 16)
                    for c in range(BLOCKS):
                        if not first:
                            pe.wait_ge(mixed_ready, (g - 1) * BLOCKS + c + 1)
                        for r in range(CHUNK_ROWS):
                            last = nc.tensor.matmul(y_ps[c][:, r * SIDE:(r + 1) * SIDE], y_in[u][:, r, c * 128:(c + 1) * 128],
                                                    row_inv[:], start=True, stop=True)
                        last.then_inc(y_mm, 1)

                def transpose_norm(s, u):
                    g = 2 * s + u
                    pe.wait_ge(n1_ready, g + 1)
                    pe.wait_ge(t1_ready, 2 * g + 2)
                    for h in range(HALVES):
                        for t in range(TILES):
                            last = nc.tensor.transpose(o_ps[h][:, t * TILE:(t + 1) * TILE], n1[u][:, t, h * 128:(h + 1) * 128],
                                                       ident[:TILE, :TILE])
                    last.then_inc(nt_mm, 1)

                def output_mm(s, u):
                    g = 2 * s + u
                    pe.wait_ge(low_mixed, (g + 1) * BLOCKS)
                    for pair in range(TILES // 2):
                        pe.wait_ge(nt0_ready if pair == 0 else nt1_ready, g)
                        for t in (2 * pair, 2 * pair + 1):
                            for c in range(BLOCKS):
                                last = product(nc, o_ps[pair][:TILE, (t % 2) * CH:(t % 2 + 1) * CH],
                                               [x[:, c, t * TILE:(t + 1) * TILE] for x in mixed[u]], [w[:, c, :] for w in w_o],
                                               start=c == 0, stop=c == BLOCKS - 1)
                        last.then_inc(o_mm, 1)

                def step(before, now, after, later):
                    if after:
                        gate_mm(*after, range(0, 2))
                    if before:
                        transpose_norm(*before)
                    if after:
                        gate_mm(*after, range(2, BLOCKS))
                    output_mm(*now)
                    if after:
                        inverse_rows(*after)

                gate_mm(0, 0, range(BLOCKS))
                inverse_rows(0, 0, first=True)
                all_steps(pe, step)
                transpose_norm(PAIRS - 1, 1)

            @block.scalar
            def _(act):
                act.wait_ge(consts_in, 16 * (len(loads) + 2))

                for raw, split in splits:
                    nc.scalar.activation(split[0][:], raw, ACT.Copy).then_inc(high_consts, 1)
                act.wait_ge(low_consts, len(splits))

                def split_x(s, u):
                    act.wait_ge(xn_loaded[u], s * 16 + 16)
                    act.wait_ge(u_mm, s * 2 * BLOCKS)
                    nc.scalar.activation(xn_t[u][0][:], xn_in[u][:], ACT.Copy).then_inc(high_x, 1)

                def split_mixed(s, u):
                    g = 2 * s + u
                    act.wait_ge(o_mm, 2 * 2 * s)
                    for c in range(BLOCKS):
                        act.wait_ge(mixed_ready, g * BLOCKS + c + 1)
                        nc.scalar.activation(mixed[u][0][:, c, :], gated[u][:, c, :], ACT.Copy).then_inc(high_mixed, 1)

                def gates(s, u, blocks):
                    g = 2 * s + u
                    for c in blocks:
                        act.wait_ge(u_mm, g * BLOCKS + c + 1)
                        if c == 0:
                            act.wait_ge(mixed_ready, 2 * s * BLOCKS)
                        nc.scalar.activation(gate[u][:, c, :], u_ps[c % 2][:, :CHUNK], ACT.Silu,
                                             bias=u_bias[:, c:c + 1]).then_inc(gate_ready, 1)

                def take_norm(s, u):
                    g = 2 * s + u
                    act.wait_ge(nt_mm, g + 1)
                    act.wait_ge(nt_stored[u], s * 16)
                    nc.scalar.activation(n1_t[u][:, 0, :], o_ps[0][:, :CHUNK], ACT.Copy).then_inc(nt0_ready, 1)

                def store_norm(s, u):
                    g = 2 * s + u
                    act.wait_ge(nt0_ready, g + 1)
                    act.wait_ge(nt1_ready, g + 1)
                    act.dma_start(d["n1_t"][g], n1_t[u][:]).then_inc(nt_stored[u], 16)

                def roots(s, u):
                    g = 2 * s + u
                    act.wait_ge(var_ready, g + 1)
                    nc.scalar.activation(root[u][:], var[u][:], ACT.Sqrt).then_inc(rooted, 1)
                    act.wait_ge(t1_ready, 2 * g + 2)
                    act.dma_start(d["t1_tiles"][g], t1[u][:]).then_inc(t1_stored[u], 16)

                def step(before, now, after, later):
                    if after:
                        gates(*after, range(0, 2))
                    if before:
                        take_norm(*before)
                    if after:
                        gates(*after, range(2, BLOCKS))
                    if before:
                        store_norm(*before)
                    if later:
                        split_x(*later)
                    roots(*now)
                    if after:
                        split_mixed(*after)

                split_x(0, 0)
                split_x(0, 1)
                gates(0, 0, range(BLOCKS))
                split_mixed(0, 0)
                all_steps(act, step)
                take_norm(PAIRS - 1, 1)
                store_norm(PAIRS - 1, 1)
                for u in range(2):
                    act.wait_ge(t1_stored[u], 16 * PAIRS)
                    act.wait_ge(nt_stored[u], 16 * PAIRS)

            @block.vector
            def _(dve):
                dve.wait_ge(consts_in, 16 * (len(loads) + 2))
                for i, (raw, split) in enumerate(splits):
                    dve.wait_ge(high_consts, i + 1)
                    nc.vector.tensor_tensor(split[1][:], raw, split[0][:].bitcast(F32), ALU.subtract).then_inc(low_consts, 1)

                def split_x(s, u):
                    dve.wait_ge(high_x, 2 * s + u + 1)
                    nc.vector.tensor_tensor(xn_t[u][1][:], xn_in[u][:], xn_t[u][0][:].bitcast(F32), ALU.subtract
                                            ).then_inc(low_x, 1)

                def split_mixed(s, u):
                    g = 2 * s + u
                    for c in range(BLOCKS):
                        dve.wait_ge(high_mixed, g * BLOCKS + c + 1)
                        nc.vector.tensor_tensor(mixed[u][1][:, c, :], gated[u][:, c, :], mixed[u][0][:, c, :].bitcast(F32),
                                                ALU.subtract).then_inc(low_mixed, 1)

                def mixes(s, u):
                    g = 2 * s + u
                    dve.wait_ge(gate_ready, g * BLOCKS + BLOCKS)
                    dve.wait_ge(o_mm, 2 * 2 * s)
                    dve.wait_ge(low_mixed, 2 * s * BLOCKS)
                    for c in range(BLOCKS):
                        dve.wait_ge(y_mm, g * BLOCKS + c + 1)
                        nc.vector.tensor_tensor(gated[u][:, c, :], gate[u][:, c, :], y_ps[c][:, :CHUNK],
                                                ALU.mult).then_inc(mixed_ready, 1)

                def take_norm(s, u):
                    g = 2 * s + u
                    dve.wait_ge(nt_mm, g + 1)
                    dve.wait_ge(nt_stored[u], s * 16)
                    nc.vector.tensor_copy(n1_t[u][:, 1, :], o_ps[1][:, :CHUNK]).then_inc(nt1_ready, 1)

                def residual_norm(s, u):
                    g = 2 * s + u
                    dve.wait_ge(resid_ready, g + 1)
                    dve.wait_ge(t1_stored[u], s * 16)
                    for pair in range(TILES // 2):
                        dve.wait_ge(o_mm, 2 * g + pair + 1)
                        nc.vector.tensor_tensor(t1[u][:, 2 * pair:2 * pair + 2, :],
                                                o_ps[pair][:TILE, :].rearrange("p (t c) -> p t c", t=2),
                                                resid[u][:, 2 * pair:2 * pair + 2, :], ALU.add).then_inc(t1_ready, 1)
                    dve.wait_ge(t1_ready, 2 * g + 2)
                    for t in range(TILES):
                        last = nc.vector.bn_stats(stats[:, t, :], t1[u][:, t, :])
                    last.then_inc(measured, 1)
                    dve.wait_ge(measured, g + 1)
                    dve.sem_inc(seen, 1)
                    for t in range(TILES):
                        last = nc.vector.bn_aggr(moments[u][:, t, :], stats[:, t, :])
                    last.then_inc(aggregated, 1)
                    dve.wait_ge(aggregated, g + 1)
                    nc.vector.tensor_scalar(var[u][:], moments[u][:, :, 1], LN_EPS, None, ALU.add).then_inc(var_ready, 1)

                def normalise(s, u):
                    g = 2 * s + u
                    dve.wait_ge(rooted, g + 1)
                    nc.vector.reciprocal(inv[u][:], root[u][:]).then_inc(inverted, 1)
                    dve.wait_ge(inverted, g + 1)
                    nc.vector.scalar_tensor_tensor(out=shift[u][:], in0=moments[u][:, :, 0], scalar=-1.0, in1=inv[u][:],
                                                   op0=ALU.mult, op1=ALU.mult).then_inc(shift_ready, 1)
                    dve.wait_ge(shift_ready, g + 1)
                    dve.wait_ge(nt_mm, 2 * s)
                    for t in range(TILES):
                        last = nc.vector.tensor_scalar(n1[u][:, t, :], t1[u][:, t, :], inv[u][:, t:t + 1], shift[u][:, t:t + 1],
                                                       ALU.mult, ALU.add)
                    last.then_inc(n1_ready, 1)

                def step(before, now, after, later):
                    if before:
                        take_norm(*before)
                    if later:
                        split_x(*later)
                    residual_norm(*now)
                    if after:
                        mixes(*after)
                    normalise(*now)
                    if after:
                        split_mixed(*after)

                split_x(0, 0)
                split_x(0, 1)
                mixes(0, 0)
                split_mixed(0, 0)
                all_steps(dve, step)
                take_norm(PAIRS - 1, 1)


def attention_phase(nc, d):
    with Tools(nc, "at") as T:
        NT = CHUNKS * TILES
        HB = 128 // HEAD
        BLOCKS = 4
        SETS = BLOCKS * HB
        COMPACT = CHUNKS * SETS
        AHEAD = COMPACT - SETS
        STRIDE = 2 * COMPACT - SETS
        w_qkv = [T.sb(f"w_qkv_{part}", [128, HALVES, 3 * CH], F32R) for part in ("high", "low")]
        w_proj = T.sb("w_proj", [128, HALVES, CH])
        p_bias = T.sb("p_bias", [TILE, CH])
        ident = T.sb("ident", [128, 128])
        same_head = T.sb("same_head", [128, 128])
        row_head = T.sb("row_head", [128, SETS - HB + COMPACT])
        spread = T.sb("spread", [COMPACT, CHUNKS * BLOCKS, 128], F32R)
        z_rows = T.sb("z_rows", [COMPACT, HALVES, 128])
        n_raw = [T.sb(f"n_raw{i}", [128, HALVES, CHUNK]) for i in range(2)]
        n_t = [[T.sb(f"n_t{i}_{part}", [128, HALVES, CHUNK], F32R) for part in ("high", "low")] for i in range(2)]
        qk_t = T.sb("qk_t", [128, BLOCKS, TOKENS])
        k_v = T.sb("k_v", [TILE, NT, 2 * CH])
        part, part2 = (T.sb(n, [128, BLOCKS, CHUNKS]) for n in ("part", "part2"))
        total, total_eps, total2, total2_eps = (T.sb(n, [128, BLOCKS]) for n in ("total", "total_eps", "total2", "total2_eps"))
        sel = T.sb("sel", [128, AHEAD + BLOCKS * (STRIDE + HB)])
        const, const2 = T.sb("const", [COMPACT, 1]), T.sb("const2", [COMPACT, 1])
        flow, inv_flow, kept = (T.sb(n, [COMPACT, CHUNK]) for n in ("flow", "inv_flow", "kept"))
        clipped = source = flow
        factor = alloc = kept
        rows = [T.sb(f"rows_{part}", [COMPACT, CHUNK], F32R) for part in ("high", "low")]
        source_tok = T.sb("source_tok", [TILE, TILES, COMPACT])
        z_part, z_inv, z_factor = T.sb("z_part", [COMPACT, 1]), T.sb("z_inv", [128, HALVES]), T.sb("z_factor", [128, HALVES])
        kv = T.sb("kv", [128, HALVES, 128])
        fb = [T.sb(f"fb{i}", [128, CHUNK]) for i in range(2)]
        upd_t = [T.sb(f"upd_t{i}", [128, HALVES, CHUNK]) for i in range(2)]
        scratch = fb[0]
        t1 = [T.sb(f"t1{i}", [TILE, TILES, CH]) for i in range(2)]
        stats = T.sb("stats", [TILE, NT, 6])
        moments = T.sb("moments", [TILE, NT, 2])
        bank = [T.ps(f"bank{i}", [128, 512]) for i in range(8)]
        qt_ps, flow_ps, kept_ps, kt_ps = bank[0:2], bank[2], bank[3], bank[6:8]
        wide_ps = bank[0:2] + bank[4:6]
        turn_ps, z_ps, kv_ps = bank[0], bank[1], bank[2:4]
        fb_ps, upd_ps, proj_ps = bank[0:2], bank[4:6], bank[6:8]
        CONST = CHUNK
        (consts_in, cleared, raw_in, split_consts, high_ready, low_ready, qt_mm, qt_ready, kt_mm, k_v_ready, const_mm, flow_mm, spread_mm, sum_ready, kept_mm, link,
         alloc_ready, source_ready, turn_mm, turned, z_mm, v_scaled, kv_mm, fb_mm, fb_ready, upd_mm, upd_ready, proj_mm,
         t1_biased, t2_ready, measured, aggregated, seen, moments_stored) = (T.sem(n) for n in (
             "consts_in", "cleared", "raw_in", "split_consts", "high_ready", "low_ready", "qt_mm", "qt_ready", "kt_mm", "k_v_ready", "const_mm", "flow_mm", "spread_mm",
             "sum_ready", "kept_mm", "link", "alloc_ready", "source_ready", "turn_mm", "turned", "z_mm", "v_scaled", "kv_mm",
             "fb_mm", "fb_ready", "upd_mm", "upd_ready", "proj_mm", "t1_biased", "t2_ready", "measured", "aggregated", "seen",
             "moments_stored"))
        n_loaded, t1_loaded, t2_stored = ([T.sem(f"{n}{i}") for i in range(2)] for n in ("n_loaded", "t1_loaded", "t2_stored"))
        QT, UPDS, SUMS = CHUNKS * BLOCKS, CHUNKS * HALVES, CHUNKS * TILES // 2
        PER_SLOT = [(CHUNKS + 1) // 2, CHUNKS // 2]
        ALL_LINKS = {name: i + 1 for i, name in enumerate((
            "total", "total_eps", "sel", "const", "flow", "inv_flow", "inv_high", "inv_low", "total2", "total2_eps", "sel2", "const2",
            "kept", "clipped", "factor", "factor_high", "factor_low", "z_inv", "z_factor", "kv"))}
        LINKS = len(ALL_LINKS)
        raw_w = qk_t[:, 0, :HALVES * 3 * CH].rearrange("p (h c) -> p h c", h=HALVES)
        raw_spread = [qk_t[:COMPACT, 1 + i, :CHUNKS * BLOCKS // 2 * 128].rearrange("p (n c) -> p n c", c=128) for i in range(2)]
        loads = [(w_proj, "w_proj"), (p_bias, "p_bias"), (ident, "ident"), (same_head, "same_head"),
                 (row_head, "row_head"), (z_rows, "z_rows")]
        head_mask = same_head[:, 0:128:HEAD]

        def wait_link(eng, b, name):
            eng.wait_ge(link, b * LINKS + ALL_LINKS[name])

        def window(x, j):
            at = AHEAD + x * STRIDE - j * SETS
            return sel[:, at:at + COMPACT]

        def part_free(eng, b, i):
            if i < 2:
                eng.wait_ge(kt_mm, b * NT)
            elif i < CHUNKS + 2:
                eng.wait_ge(qt_mm, b * QT + (i - 1) * BLOCKS)
            else:
                eng.wait_ge(kt_mm, b * NT + (i - CHUNKS - 1) * TILES)

        def over_images(eng, image):
            with eng.Fori(0, BATCH - 1) as b:
                image(b, True)
            image(BATCH - 1, False)

        sel_heads = sel[:, AHEAD:].rearrange("p (x w) -> p x w", x=BLOCKS)[:, :, :HB]

        with nc.Block() as block:
            @block.sync
            def _(sp):
                for tile, name in loads:
                    sp.dma_start(tile[:], d[name]).then_inc(consts_in, 16)
                sp.dma_start(raw_w, d["w_qkv"]).then_inc(raw_in, 16)
                for i in range(2):
                    sp.dma_start(raw_spread[i], d["spread"][:, i * CHUNKS * BLOCKS // 2:(i + 1) * CHUNKS * BLOCKS // 2]
                                 ).then_inc(raw_in, 16)
                def load(b, i):
                    sp.wait_ge(high_ready, b * 2 * CHUNKS + max(i - 1, 0))
                    sp.wait_ge(low_ready, b * 2 * CHUNKS + max(i - 1, 0))
                    sp.dma_start(n_raw[i % 2][:], d["n1_t"][b * CHUNKS + i % CHUNKS]).then_inc(n_loaded[i % 2], 16)

                load(0, 0)
                load(0, 1)

                def image(b, more):
                    for i in range(2, 2 * CHUNKS):
                        load(b, i)
                    for i in range(2 if more else 0):
                        load(b + 1, i)
                    def load_t1(j):
                        sp.wait_ge(measured, b * CHUNKS + max(j - 1, 0))
                        sp.wait_ge(t2_stored[j % 2], (b * PER_SLOT[j % 2] + j // 2) * 16)
                        sp.dma_start(t1[j % 2][:], d["t1_tiles"][b * CHUNKS + j]).then_inc(t1_loaded[j % 2], 16)

                    load_t1(0)
                    load_t1(1)
                    for j in range(CHUNKS):
                        sp.wait_ge(t2_ready, b * SUMS + (j + 1) * TILES // 2)
                        sp.dma_start(d["t2_tiles"][b * CHUNKS + j], t1[j % 2][:]).then_inc(t2_stored[j % 2], 16)
                        if j + 2 < CHUNKS:
                            load_t1(j + 2)
                    sp.wait_ge(aggregated, (b + 1) * CHUNKS)
                    sp.dma_start(d["t2_moments"][b], moments[:]).then_inc(moments_stored, 16)

                over_images(sp, image)
                for i in range(2):
                    sp.wait_ge(t2_stored[i], 16 * BATCH * PER_SLOT[i])
                sp.wait_ge(moments_stored, 16 * BATCH)

            @block.gpsimd
            def _(pool):
                nc.gpsimd.memset(sel[:], 0.0).then_inc(cleared, 1)
                pool.wait_ge(consts_in, 16 * len(loads))
                def image(b, more):
                    for j in range(CHUNKS):
                        pool.wait_ge(t1_loaded[j % 2], (b * PER_SLOT[j % 2] + j // 2 + 1) * 16)
                        nc.gpsimd.tensor_tensor(t1[j % 2][:], t1[j % 2][:], p_bias[:].unsqueeze(1).to_broadcast([TILE, TILES, CH]),
                                                ALU.add).then_inc(t1_biased, 1)

                over_images(pool, image)

            @block.tensor
            def _(pe):
                pe.wait_ge(consts_in, 16 * len(loads))
                pe.wait_ge(split_consts, 4)
                def image(b, more):
                    def split_done(i):
                        pe.wait_ge(low_ready, b * 2 * CHUNKS + i + 1)

                    def project_t(j):
                        split_done(j)
                        for x in range(BLOCKS):
                            n = BLOCKS * j + x
                            if n >= 2:
                                pe.wait_ge(qt_ready, b * QT + n - 1)
                            else:
                                pe.wait_ge(qt_ready, b * QT)
                                pe.wait_ge(fb_ready, b * UPDS)
                            for h in range(HALVES):
                                last = product(nc, qt_ps[n % 2][:, :CHUNK], [w[:, h, x * 128:(x + 1) * 128] for w in w_qkv],
                                               [part[:, h, :] for part in n_t[j % 2]], start=h == 0, stop=h == HALVES - 1)
                            last.then_inc(qt_mm, 1)

                    def project(j):
                        split_done(CHUNKS + j)
                        for t in range(TILES):
                            project_tile(j, t)

                    def project_tile(j, t):
                        i, n = CHUNKS + j, j * TILES + t
                        if n >= 2:
                            pe.wait_ge(k_v_ready, b * NT + n - 1)
                        for h in range(HALVES):
                            product(nc, kt_ps[n % 2][:TILE, CH:], [part[:, h, t * TILE:(t + 1) * TILE] for part in n_t[i % 2]],
                                    [w[:, h, 2 * CH:] for w in w_qkv], start=h == 0, stop=h == HALVES - 1)
                        pe.wait_ge(qt_ready, b * QT + (j + 1) * BLOCKS)
                        for h in range(HALVES):
                            last = nc.tensor.transpose(kt_ps[n % 2][:TILE, h * 128:(h + 1) * 128],
                                                       qk_t[:, 2 + h, n * TILE:(n + 1) * TILE], ident[:])
                        last.then_inc(kt_mm, 1)

                    def head_sums(sums, out_bank, done):
                        for x in range(BLOCKS):
                            y = (x + 2) % BLOCKS
                            last = nc.tensor.matmul(out_bank[:COMPACT, CONST:CONST + 1], row_head[:, SETS - HB * (x + 1):SETS - HB * (x + 1) + COMPACT], sums[:, y:y + 1],
                                                    start=x == 0, stop=x == BLOCKS - 1)
                        last.then_inc(const_mm, 1)
                        for j in range(CHUNKS):
                            for x in range(BLOCKS):
                                last = nc.tensor.matmul(out_bank[:COMPACT, :CHUNK], window(x, j),
                                                        qk_t[:, x, j * CHUNK:(j + 1) * CHUNK],
                                                        start=j == 0 and x == 0, stop=j == CHUNKS - 1 and x == BLOCKS - 1)
                        last.then_inc(done, 1)

                    for j in range(CHUNKS):
                        project_t(j)
                    pe.wait_ge(t2_ready, b * SUMS)
                    project(0)
                    project(1)
                    wait_link(pe, b, "sel")
                    head_sums(total_eps, flow_ps, flow_mm)
                    project(2)
                    def spread_rows(out, n):
                        nc.tensor.matmul(out, spread[:, n, :], rows[0][:], start=True, stop=False)
                        return nc.tensor.matmul(out, spread[:, n, :], rows[1][:], start=False, stop=True)

                    wait_link(pe, b, "inv_low")
                    for n in range(QT):
                        pe.wait_ge(sum_ready, b * QT + max(n - 3, 0))
                        spread_rows(wide_ps[n % 4][:, :CHUNK], n).then_inc(spread_mm, 1)
                        if n % 3 == 2 and n // 3 < 2 * TILES:
                            j, t = 3 + n // 3 // TILES, n // 3 % TILES
                            if t == 0:
                                split_done(CHUNKS + j)
                            project_tile(j, t)
                    split_done(CHUNKS + 5)
                    project_tile(5, 0)
                    project_tile(5, 1)
                    wait_link(pe, b, "sel2")
                    head_sums(total2_eps, kept_ps, kept_mm)
                    project_tile(5, 2)
                    project_tile(5, 3)
                    split_done(CHUNKS + 6)
                    for t in range(TILES - 1):
                        project_tile(6, t)
                    pe.wait_ge(source_ready, b + 1)
                    for t in range(TILES):
                        last = nc.tensor.transpose(turn_ps[:TILE, t * COMPACT:(t + 1) * COMPACT],
                                                   source[:, t * TILE:(t + 1) * TILE], ident[:COMPACT, :COMPACT])
                    last.then_inc(turn_mm, 1)
                    for h in range(HALVES):
                        last = nc.tensor.matmul(z_ps[:, h:h + 1], z_rows[:, h, :], z_part[:], start=True, stop=True)
                    last.then_inc(z_mm, 1)
                    project_tile(6, TILES - 1)
                    for n in range(NT):
                        if n % TILES == 0:
                            pe.wait_ge(v_scaled, b * CHUNKS + n // TILES + 1)
                        for h in range(HALVES):
                            last = nc.tensor.matmul(kv_ps[h][:, :128], k_v[:, n, h * 128:(h + 1) * 128],
                                                    k_v[:, n, CH + h * 128:CH + (h + 1) * 128], start=n == 0, stop=n == NT - 1)
                    last.then_inc(kv_mm, 1)

                    def update(j):
                        for h in range(HALVES):
                            n = HALVES * j + h
                            if n >= 2:
                                pe.wait_ge(fb_ready, b * UPDS + n - 1)
                            spread_rows(fb_ps[n % 2][:, :CHUNK], BLOCKS * j + h).then_inc(fb_mm, 1)
                        for h in range(HALVES):
                            n = HALVES * j + h
                            if n == 0:
                                wait_link(pe, b, "kv")
                            if n >= 2:
                                pe.wait_ge(upd_ready, b * UPDS + n - 1)
                            nc.tensor.matmul(upd_ps[n % 2][:, :CHUNK], kv[:, h, :], qk_t[:, h, j * CHUNK:(j + 1) * CHUNK],
                                             start=True, stop=True).then_inc(upd_mm, 1)

                    def output(j):
                        pe.wait_ge(upd_ready, b * UPDS + HALVES * (j + 1))
                        for pair in range(TILES // 2):
                            n = j * TILES // 2 + pair
                            if n >= 2:
                                pe.wait_ge(t2_ready, b * SUMS + n - 1)
                            for t in (2 * pair, 2 * pair + 1):
                                for h in range(HALVES):
                                    last = nc.tensor.matmul(proj_ps[n % 2][:TILE, (t % 2) * CH:(t % 2 + 1) * CH],
                                                            upd_t[j % 2][:, h, t * TILE:(t + 1) * TILE], w_proj[:, h, :],
                                                            start=h == 0, stop=h == HALVES - 1)
                            last.then_inc(proj_mm, 1)

                    wait_link(pe, b, "factor_low")
                    pe.wait_ge(turned, b + 1)
                    wait_link(pe, b, "z_inv")
                    for j in range(CHUNKS):
                        update(j)
                        if j:
                            output(j - 1)
                    output(CHUNKS - 1)

                over_images(pe, image)

            @block.scalar
            def _(act):
                act.wait_ge(raw_in, 16 * 3)
                nc.scalar.activation(w_qkv[0][:], raw_w, ACT.Copy).then_inc(split_consts, 1)
                for i in range(2):
                    nc.scalar.activation(spread[:, i * CHUNKS * BLOCKS // 2:(i + 1) * CHUNKS * BLOCKS // 2, :], raw_spread[i],
                                         ACT.Copy).then_inc(split_consts, 1)
                act.wait_ge(split_consts, 4)

                def high_part(b, i):
                    act.wait_ge(n_loaded[i % 2], (b * CHUNKS + i // 2 + 1) * 16)
                    part_free(act, b, i)
                    nc.scalar.activation(n_t[i % 2][0][:], n_raw[i % 2][:], ACT.Copy).then_inc(high_ready, 1)

                high_part(0, 0)
                high_part(0, 1)

                def image(b, more):
                    def take_k_v(tiles):
                        for n in tiles:
                            act.wait_ge(kt_mm, b * NT + n + 1)
                            nc.scalar.activation(k_v[:, n, :], kt_ps[n % 2][:TILE, :], ACT.Copy).then_inc(k_v_ready, 1)

                    act.wait_ge(upd_mm, b * UPDS)
                    act.wait_ge(kv_mm, b)
                    for n in range(QT):
                        j, x = divmod(n, BLOCKS)
                        act.wait_ge(qt_mm, b * QT + n + 1)
                        nc.scalar.activation(qk_t[:, x, j * CHUNK:(j + 1) * CHUNK], qt_ps[n % 2][:, :CHUNK], ACT.Sigmoid,
                                             accum_out=part[:, x, j:j + 1]).then_inc(qt_ready, 1)
                        if x == BLOCKS - 1:
                            high_part(b, j + 2)
                    for j in range(CHUNKS):
                        take_k_v(range(j * TILES, min((j + 1) * TILES, NT - 1)))
                        if j + 2 < CHUNKS:
                            high_part(b, CHUNKS + j + 2)
                    wait_link(act, b, "clipped")
                    nc.scalar.activation(alloc[:], kept[:], ACT.Sigmoid).then_inc(alloc_ready, 1)
                    nc.scalar.activation(source[:], clipped[:], ACT.Exp, accum_out=z_part[:]).then_inc(source_ready, 1)
                    act.wait_ge(turn_mm, b + 1)
                    nc.scalar.activation(source_tok[:].rearrange("p t r -> p (t r)"), turn_ps[:TILE, :TILES * COMPACT], ACT.Copy
                                         ).then_inc(turned, 1)
                    take_k_v([NT - 1])
                    for n in range(UPDS):
                        j = n // HALVES
                        act.wait_ge(fb_mm, b * UPDS + n + 1)
                        act.wait_ge(upd_ready, b * UPDS + max(n - 1, 0))
                        nc.scalar.activation(fb[n % 2][:], fb_ps[n % 2][:, :CHUNK], ACT.Copy).then_inc(fb_ready, 1)
                        if more and n % HALVES == 1 and j < 2:
                            high_part(b + 1, j)

                over_images(act, image)
            @block.vector
            def _(dve):
                dve.wait_ge(consts_in, 16 * len(loads))
                dve.wait_ge(cleared, 1)
                dve.wait_ge(raw_in, 16 * 3)
                dve.wait_ge(split_consts, 1)
                nc.vector.tensor_tensor(w_qkv[1][:], raw_w, w_qkv[0][:].bitcast(F32), ALU.subtract).then_inc(split_consts, 1)
                def low_part(b, i):
                    dve.wait_ge(high_ready, b * 2 * CHUNKS + i + 1)
                    high, low = n_t[i % 2]
                    nc.vector.tensor_tensor(low[:], n_raw[i % 2][:], high[:].bitcast(F32), ALU.subtract).then_inc(low_ready, 1)

                low_part(0, 0)
                low_part(0, 1)

                def image(b, more):
                    def step(name, instruction):
                        instruction.then_inc(link, 1)

                    def split_rows(name, values):
                        step(name + "_high", nc.vector.tensor_copy(rows[0][:], values[:]))
                        wait_link(dve, b, name + "_high")
                        step(name + "_low", nc.vector.tensor_tensor(rows[1][:], values[:], rows[0][:].bitcast(F32), ALU.subtract))

                    mask3 = head_mask.unsqueeze(1).to_broadcast([128, 2, HB])

                    def select(name, sums):
                        for x in (0, 2):
                            y = (x + 2) % BLOCKS
                            last = nc.vector.tensor_tensor(sel_heads[:, x:x + 2, :], mask3,
                                                           sums[:, y:y + 2].unsqueeze(2).to_broadcast([128, 2, HB]), ALU.mult)
                        step(name, last)

                    for i in range(2, CHUNKS + 2):
                        low_part(b, i)
                    dve.wait_ge(qt_ready, (b + 1) * QT)
                    step("total", nc.vector.reduce_sum(total[:], part[:], axis=AX.X))
                    wait_link(dve, b, "total")
                    step("total_eps", nc.vector.tensor_scalar(total_eps[:], total[:], ATT_EPS, None, ALU.add))
                    wait_link(dve, b, "total_eps")
                    select("sel", total_eps)
                    low_part(b, CHUNKS + 2)
                    low_part(b, CHUNKS + 3)
                    dve.wait_ge(const_mm, 2 * b + 1)
                    dve.wait_ge(flow_mm, b + 1)
                    step("const", nc.vector.tensor_scalar(const[:], flow_ps[:COMPACT, CONST:CONST + 1], ATT_EPS, ATT_EPS,
                                                          ALU.mult, ALU.add))
                    wait_link(dve, b, "const")
                    step("flow", nc.vector.tensor_scalar(flow[:], flow_ps[:COMPACT, :CHUNK], const[:, 0:1], None, ALU.add))
                    wait_link(dve, b, "flow")
                    step("inv_flow", nc.vector.reciprocal(inv_flow[:], flow[:]))
                    wait_link(dve, b, "inv_flow")
                    split_rows("inv", inv_flow)
                    low_part(b, CHUNKS + 4)
                    for n in range(QT):
                        j, x = divmod(n, BLOCKS)
                        if n == QT // 2 + 2:
                            low_part(b, CHUNKS + 5)
                        dve.wait_ge(spread_mm, b * QT + n + 1)
                        dve.wait_ge(sum_ready, b * QT + n)
                        nc.vector.scalar_tensor_tensor(out=scratch[:], in0=wide_ps[n % 4][:, :CHUNK], scalar=1.0,
                                                       in1=qk_t[:, x, j * CHUNK:(j + 1) * CHUNK], op0=ALU.mult, op1=ALU.mult,
                                                       accum_out=part2[:, x, j:j + 1]).then_inc(sum_ready, 1)
                    dve.wait_ge(sum_ready, (b + 1) * QT)
                    step("total2", nc.vector.reduce_sum(total2[:], part2[:], axis=AX.X))
                    wait_link(dve, b, "total2")
                    step("total2_eps", nc.vector.tensor_scalar(total2_eps[:], total2[:], ATT_EPS, None, ALU.add))
                    wait_link(dve, b, "total2_eps")
                    select("sel2", total2_eps)
                    low_part(b, CHUNKS + 6)
                    dve.wait_ge(const_mm, 2 * b + 2)
                    dve.wait_ge(kept_mm, b + 1)
                    step("const2", nc.vector.tensor_scalar(const2[:], kept_ps[:COMPACT, CONST:CONST + 1], ATT_EPS, ATT_EPS,
                                                           ALU.mult, ALU.add))
                    wait_link(dve, b, "const2")
                    step("kept", nc.vector.tensor_scalar(kept[:], kept_ps[:COMPACT, :CHUNK], const2[:, 0:1], None, ALU.add))
                    wait_link(dve, b, "kept")
                    step("clipped", nc.vector.tensor_scalar(clipped[:], kept[:], 1.0, -1.0, ALU.min, ALU.max))
                    dve.wait_ge(alloc_ready, b + 1)
                    step("factor", nc.vector.tensor_tensor(factor[:], inv_flow[:], alloc[:], ALU.mult))
                    wait_link(dve, b, "factor")
                    split_rows("factor", factor)

                    def scale_v(j):
                        dve.wait_ge(k_v_ready, b * NT + (j + 1) * TILES)
                        for t in range(TILES):
                            heads = k_v[:, j * TILES + t, CH:].rearrange("p (h c) -> p h c", c=HEAD)
                            each = source_tok[:, t, j * SETS + 2 * HB:(j + 1) * SETS].unsqueeze(2).to_broadcast([TILE, 2 * HB, HEAD])
                            last = nc.vector.tensor_tensor(heads, heads, each, ALU.mult)
                        last.then_inc(v_scaled, 1)

                    dve.wait_ge(turned, b + 1)
                    for j in range(CHUNKS):
                        scale_v(j)
                    dve.wait_ge(z_mm, b + 1)
                    step("z_inv", nc.vector.reciprocal(z_inv[:], z_ps[:, :HALVES]))
                    wait_link(dve, b, "z_inv")
                    step("z_factor", nc.vector.tensor_scalar(z_factor[:], z_inv[:], TOKENS / V_SCALE, None, ALU.mult))
                    wait_link(dve, b, "z_factor")
                    dve.wait_ge(kv_mm, b + 1)
                    for h in range(HALVES):
                        last = nc.vector.scalar_tensor_tensor(out=kv[:, h, :], in0=kv_ps[h][:, :128], scalar=z_factor[:, h:h + 1],
                                                              in1=same_head[:], op0=ALU.mult, op1=ALU.mult)
                    step("kv", last)

                    def take_update(j):
                        for h in range(HALVES):
                            n = HALVES * j + h
                            dve.wait_ge(upd_mm, b * UPDS + n + 1)
                            dve.wait_ge(fb_ready, b * UPDS + n + 1)
                            if j >= 2:
                                dve.wait_ge(proj_mm, b * SUMS + (j - 1) * TILES // 2)
                            nc.vector.tensor_tensor(upd_t[j % 2][:, h, :], upd_ps[n % 2][:, :CHUNK], fb[n % 2][:], ALU.mult
                                                    ).then_inc(upd_ready, 1)

                    def measure(j):
                        dve.wait_ge(t2_ready, b * SUMS + (j + 1) * TILES // 2)
                        for t in range(TILES):
                            last = nc.vector.bn_stats(stats[:, j * TILES + t, :], t1[j % 2][:, t, :])
                        last.then_inc(measured, 1)

                    def aggregate(j):
                        dve.wait_ge(moments_stored, b * 16)
                        dve.wait_ge(measured, b * CHUNKS + j + 1)
                        dve.sem_inc(seen, 1)
                        for n in range(j * TILES, (j + 1) * TILES):
                            last = nc.vector.bn_aggr(moments[:, n, :], stats[:, n, :])
                        last.then_inc(aggregated, 1)

                    def add_residual(j):
                        dve.wait_ge(t1_biased, b * CHUNKS + j + 1)
                        for pair in range(TILES // 2):
                            n = j * TILES // 2 + pair
                            dve.wait_ge(proj_mm, b * SUMS + n + 1)
                            nc.vector.tensor_tensor(t1[j % 2][:, 2 * pair:2 * pair + 2, :],
                                                    proj_ps[n % 2][:TILE, :].rearrange("p (t c) -> p t c", t=2),
                                                    t1[j % 2][:, 2 * pair:2 * pair + 2, :], ALU.add).then_inc(t2_ready, 1)

                    for j in range(CHUNKS):
                        take_update(j)
                        if more and j in (2, 3):
                            low_part(b + 1, j - 2)
                        if j:
                            add_residual(j - 1)
                            measure(j - 1)
                        if j >= 2:
                            aggregate(j - 2)
                    add_residual(CHUNKS - 1)
                    measure(CHUNKS - 1)
                    aggregate(CHUNKS - 2)
                    aggregate(CHUNKS - 1)

                over_images(dve, image)


def ffn_phase(nc, d):
    with Tools(nc, "ff") as T:
        NB = HIDDEN // 128
        PAIRS_T = CHUNK // 2
        fc1_raw = T.sb("fc1_raw", [128, HALVES, HIDDEN])
        interp = T.sb("interp", [128, HALVES, 128])
        fc1 = T.sb("fc1", [128, HIDDEN])
        fc1_bias = T.sb("fc1_bias", [128, NB])
        fc2 = T.sb("fc2", [128, NB, 128])
        fc2_bias = T.sb("fc2_bias", [128, 1])
        pair_tok = T.sb("pair_tok", [TILE, SIDE])
        pair_up = T.sb("pair_up", [128, CH])
        t2 = [T.sb(f"t2{u}", [TILE, TILES, CH]) for u in range(2)]
        NT = CHUNKS * TILES
        moments = T.sb("moments", [TILE, BATCH, NT, 2])
        var, root = T.sb("var", [TILE, BATCH, NT]), T.sb("root", [TILE, BATCH, NT])
        norms = T.sb("norms", [TILE, BATCH * NT, 2])
        norm = [T.sb(f"norm{u}", [TILE, TILES, 2]) for u in range(2)]
        n2 = [T.sb(f"n2{u}", [TILE, TILES, CH]) for u in range(2)]
        base = [T.sb(f"base{u}", [TILE, TILES, CH]) for u in range(2)]
        sums = [T.sb(f"sums{u}", [TILE, TILES, CH // 2]) for u in range(2)]
        low = [T.sb(f"low{u}", [128, PAIRS_T]) for u in range(2)]
        hid = T.sb("hid", [128, NB, PAIRS_T])
        change = T.sb("change", [128, CHUNK])
        out = [T.sb(f"out{u}", [TILE, TILES, CH]) for u in range(2)]
        low_ps, new_ps = T.ps("low", [128, 512]), T.ps("new", [128, 512])
        FB = 4
        hid_ps = [T.ps(f"hid{i}", [128, 512]) for i in range(FB)]
        up_ps = [T.ps(f"up{i}", [128, 512]) for i in range(2)]
        (consts_in, fc1_mm, fc1_ready, var_ready, rooted, inverted, shift_ready, norm_ready, n2_ready, base_ready,
         sums_ready, low_mm, low_ready, hid_mm, hid_ready, new_mm, change_ready, up_mm, out_ready) = (
            T.sem(n) for n in ("consts_in", "fc1_mm", "fc1_ready", "var_ready", "rooted", "inverted",
                               "shift_ready", "norm_ready", "n2_ready", "base_ready", "sums_ready", "low_mm", "low_ready",
                               "hid_mm", "hid_ready", "new_mm", "change_ready", "up_mm", "out_ready"))
        loaded, stored = ([T.sem(f"{n}{u}") for u in range(2)] for n in ("loaded", "stored"))
        PAIRS = BATCH * CHUNKS // 2
        loads = [(fc1_raw, "fc1"), (interp, "interp"), (fc1_bias, "fc1_bias"), (fc2, "fc2"), (fc2_bias, "fc2_bias"),
                 (pair_tok, "pair_tok"), (pair_up, "pair_up")]
        ALL_LOADS = len(loads) + BATCH

        def buffer_used(eng, sem, s, u):
            if u or not (isinstance(s, int) and s == 0):
                eng.wait_ge(sem, 2 * s + u - 1)

        def all_steps(eng, front, step):
            front(0, 0)
            with eng.Fori(0, PAIRS - 1) as s:
                step((s, 0), (s, 1))
                step((s, 1), (s + 1, 0))
            step((PAIRS - 1, 0), (PAIRS - 1, 1))
            step((PAIRS - 1, 1), None)

        with nc.Block() as block:
            @block.sync
            def _(sp):
                for tile, name in loads:
                    sp.dma_start(tile[:], d[name]).then_inc(consts_in, 16)
                for b in range(BATCH):
                    sp.dma_start(moments[:, b], d["t2_moments"][b]).then_inc(consts_in, 16)
                for u in range(2):
                    sp.dma_start(t2[u][:], d["t2_tiles"][u]).then_inc(loaded[u], 16)

                def store(s, u):
                    sp.wait_ge(out_ready, 2 * (2 * s + u + 1))
                    sp.dma_start(d["out"][2 * s + u], out[u][:]).then_inc(stored[u], 16)

                with sp.Fori(0, PAIRS - 1) as s:
                    for u in range(2):
                        sp.wait_ge(base_ready, s * 2 + u + 1)
                        sp.wait_ge(n2_ready, s * 2 + u + 1)
                        sp.dma_start(t2[u][:], d["t2_tiles"][(s + 1) * 2 + u]).then_inc(loaded[u], 16)
                    for u in range(2):
                        store(s, u)
                for u in range(2):
                    store(PAIRS - 1, u)
                for u in range(2):
                    sp.wait_ge(stored[u], 16 * PAIRS)

            @block.gpsimd
            def _(pool):
                def add(s, u):
                    pool.wait_ge(n2_ready, s * 2 + u + 1)
                    nc.gpsimd.tensor_tensor(base[u][:], t2[u][:], n2[u][:], ALU.add).then_inc(base_ready, 1)

                add(0, 0)
                add(0, 1)
                with pool.Fori(0, PAIRS - 1) as s:
                    for u in range(2):
                        pool.wait_ge(out_ready, 2 * (2 * s + u + 1))
                        add(s + 1, u)

            @block.tensor
            def _(pe):
                pe.wait_ge(consts_in, 16 * ALL_LOADS)
                for i in range(2):
                    for h in range(HALVES):
                        last = nc.tensor.matmul(up_ps[i][:], interp[:, h, :], fc1_raw[:, h, i * 512:(i + 1) * 512],
                                                start=h == 0, stop=h == HALVES - 1)
                    last.then_inc(fc1_mm, 1)

                def hidden(s, u, m):
                    nc.tensor.matmul(hid_ps[m % FB][:, :PAIRS_T], fc1[:, m * 128:(m + 1) * 128], low[u][:],
                                     start=True, stop=True).then_inc(hid_mm, 1)

                def first_hidden(s, u):
                    pe.wait_ge(low_ready, 2 * s + u + 1)
                    for m in range(FB):
                        hidden(s, u, m)

                def low_band(s, u):
                    g = 2 * s + u
                    pe.wait_ge(sums_ready, g + 1)
                    pe.wait_ge(low_ready, g)
                    for t in range(TILES):
                        last = nc.tensor.matmul(low_ps[:, t * SIDE:(t + 1) * SIDE], sums[u][:, t, :], pair_tok[:],
                                                start=True, stop=True)
                    last.then_inc(low_mm, 1)

                def front(s, u):
                    low_band(s, u)
                    first_hidden(s, u)

                def step(now, after):
                    s, u = now
                    g = 2 * s + u

                    def second(m):
                        pe.wait_ge(hid_ready, g * NB + m + 1)
                        if m == 0:
                            pe.wait_ge(change_ready, g)
                        last = nc.tensor.matmul(new_ps[:, :PAIRS_T], fc2[:, m, :], hid[:, m, :], start=m == 0, stop=m == NB - 1)
                        if m == NB - 1:
                            last.then_inc(new_mm, 1)

                    for m in range(FB, NB):
                        second(m - FB)
                        hidden(s, u, m)
                    if after:
                        low_band(*after)
                    for m in range(NB - FB, NB):
                        second(m)
                    if after:
                        first_hidden(*after)
                    pe.wait_ge(change_ready, g + 1)
                    for pair in range(TILES // 2):
                        pe.wait_ge(out_ready, 2 * g)
                        for t in (2 * pair, 2 * pair + 1):
                            last = nc.tensor.matmul(up_ps[pair][:TILE, (t % 2) * CH:(t % 2 + 1) * CH],
                                                    change[:, t * TILE:(t + 1) * TILE], pair_up[:], start=True, stop=True)
                        last.then_inc(up_mm, 1)

                pe.wait_ge(fc1_ready, 2)
                all_steps(pe, front, step)

            @block.scalar
            def _(act):
                act.wait_ge(consts_in, 16 * ALL_LOADS)
                for i in range(2):
                    act.wait_ge(fc1_mm, i + 1)
                    nc.scalar.activation(fc1[:, i * 512:(i + 1) * 512], up_ps[i][:], ACT.Copy).then_inc(fc1_ready, 1)

                act.wait_ge(var_ready, 1)
                nc.scalar.activation(root[:], var[:], ACT.Sqrt).then_inc(rooted, 1)

                def take_low(s, u):
                    act.wait_ge(low_mm, 2 * s + u + 1)
                    buffer_used(act, change_ready, s, u)
                    nc.scalar.activation(low[u][:], low_ps[:, :PAIRS_T], ACT.Copy).then_inc(low_ready, 1)

                def front(s, u):
                    take_low(s, u)

                def step(now, after):
                    s, u = now
                    g = 2 * s + u
                    act.wait_ge(new_mm, g)
                    for m in range(NB):
                        act.wait_ge(hid_mm, g * NB + m + 1)
                        nc.scalar.activation(hid[:, m, :], hid_ps[m % FB][:, :PAIRS_T], ACT.Gelu,
                                             bias=fc1_bias[:, m:m + 1]).then_inc(hid_ready, 1)
                    if after:
                        take_low(*after)

                all_steps(act, front, step)
            @block.vector
            def _(dve):
                dve.wait_ge(consts_in, 16 * ALL_LOADS)

                nc.vector.tensor_scalar(var[:], moments[:, :, :, 1], LN_EPS, None, ALU.add).then_inc(var_ready, 1)
                dve.wait_ge(rooted, 1)
                flat = "p b n -> p (b n)"
                nc.vector.reciprocal(norms[:, :, 0], root[:].rearrange(flat)).then_inc(inverted, 1)
                dve.wait_ge(inverted, 1)
                nc.vector.scalar_tensor_tensor(out=norms[:, :, 1], in0=moments[:, :, :, 0].rearrange(flat), scalar=-1.0,
                                               in1=norms[:, :, 0], op0=ALU.mult, op1=ALU.mult).then_inc(shift_ready, 1)
                dve.wait_ge(shift_ready, 1)

                def normalise(s, u):
                    g = 2 * s + u
                    buffer_used(dve, n2_ready, s, u)
                    nc.vector.tensor_copy(norm[u][:], norms[:, bass.ds(g * TILES, TILES), :]).then_inc(norm_ready, 1)
                    dve.wait_ge(norm_ready, g + 1)
                    dve.wait_ge(loaded[u], s * 16 + 16)
                    buffer_used(dve, base_ready, s, u)
                    for t in range(TILES):
                        last = nc.vector.tensor_scalar(n2[u][:, t, :], t2[u][:, t, :], norm[u][:, t, 0:1], norm[u][:, t, 1:2],
                                                       ALU.mult, ALU.add)
                    last.then_inc(n2_ready, 1)
                    dve.wait_ge(n2_ready, g + 1)
                    buffer_used(dve, low_mm, s, u)
                    pair = n2[u][:].rearrange("p t (c r) -> p (t c) r", r=2)
                    nc.vector.tensor_tensor(sums[u][:].rearrange("p t c -> p (t c)"), pair[:, :, 0], pair[:, :, 1], ALU.add
                                            ).then_inc(sums_ready, 1)

                def step(now, after):
                    s, u = now
                    g = 2 * s + u
                    if after:
                        normalise(*after)
                    dve.wait_ge(new_mm, g + 1)
                    dve.wait_ge(up_mm, 2 * g)
                    twice = [128, PAIRS_T, 2]
                    nc.vector.scalar_tensor_tensor(out=change[:].rearrange("p (t r) -> p t r", r=2),
                                                   in0=new_ps[:, :PAIRS_T].unsqueeze(2).to_broadcast(twice), scalar=fc2_bias[:, 0:1],
                                                   in1=low[u][:].unsqueeze(2).to_broadcast(twice), op0=ALU.add, op1=ALU.subtract
                                                   ).then_inc(change_ready, 1)
                    dve.wait_ge(base_ready, g + 1)
                    dve.wait_ge(stored[u], s * 16)
                    for pair in range(TILES // 2):
                        dve.wait_ge(up_mm, 2 * g + pair + 1)
                        nc.vector.tensor_tensor(out[u][:, 2 * pair:2 * pair + 2, :],
                                                up_ps[pair][:TILE, :].rearrange("p (t c) -> p t c", t=2),
                                                base[u][:, 2 * pair:2 * pair + 2, :], ALU.add).then_inc(out_ready, 1)

                all_steps(dve, normalise, step)


def program(nc, d):
    def scratch(name, shape):
        d[name] = nc.dram_tensor(name, shape, F32, kind="Internal").ap()

    chunks = BATCH * CHUNKS
    scratch("kern_rows", (ROWS, TAPS_PAD, WIDE))
    scratch("gn_rows", (chunks, 1, 2 * CH))
    scratch("xn_t", (chunks, 128, HALVES, CHUNK))
    scratch("v_rows", (ROWS, BATCH, SIDE, WIDE))
    scratch("y_rows", (ROWS, BATCH, SIDE, WIDE))
    scratch("t1_tiles", (chunks, TILE, TILES, CH))
    scratch("n1_t", (chunks, 128, HALVES, CHUNK))
    scratch("t2_tiles", (chunks, TILE, TILES, CH))
    scratch("t2_moments", (BATCH, TILE, CHUNKS * TILES, 2))
    flat = "b i j c -> (b i j) c"
    d["x_tiles"] = d["x"].rearrange(flat).rearrange("(g t p) c -> g p t c", t=TILES, p=TILE)
    d["out"] = d["result"].rearrange(flat).rearrange("(g t p) c -> g p t c", t=TILES, p=TILE)
    for phase in (kernel_rows_phase, stats_phase, project_phase, columns_phase, mix_phase, attention_phase, ffn_phase):
        phase(nc, d)


def kernel(**inputs):
    import concourse.bacc as bacc
    from concourse.bass_utils import run_bass_kernel_spmd

    a = {k: np.asarray(v) for k, v in inputs.items()}

    def on_partitions(w):
        return w.reshape(-1, 128, *w.shape[1:]).swapaxes(0, 1)

    def every_row(b, rows):
        return np.broadcast_to(b, (rows, b.shape[0]))

    conv, att, ffn = "L0_conv_", "L1_attn_", "L1_ffn_"
    rpe_bias = np.concatenate([a[conv + "rpe_in_b"][None], a[conv + "rpe_h_b"]], 0)
    arrays = {
        "x": a["x"],
        "w_u": on_partitions(a[conv + "W_u"].T), "u_bias": a[conv + "b_u"].reshape(-1, 128).T,
        "w_v": on_partitions(a[conv + "W_v"].T), "v_bias": every_row(a[conv + "b_v"], TILE),
        "w_o": on_partitions(a[conv + "W_o"].T), "o_bias": every_row(a[conv + "b_o"], TILE),
        "rpe_in": a[conv + "rpe_in_w"].T,
        "rpe_h": a[conv + "rpe_h_w"].transpose(0, 2, 1).reshape(RPE_LAYERS, HALVES, 128, CH).transpose(2, 0, 1, 3),
        "rpe_bias": rpe_bias.reshape(RPE_LAYERS + 1, HALVES, 128).transpose(2, 0, 1),
        "rpe_out": on_partitions(a[conv + "rpe_out_w"].T), "rpe_out_b": every_row(a[conv + "rpe_out_b"], TAPS),
        "w_qkv": on_partitions(a[att + "W_qkv"].T), "w_proj": on_partitions(a[att + "W_proj"].T),
        "p_bias": every_row(a[att + "b_proj"], TILE),
        "fc1": on_partitions(a[ffn + "fc1_w"].T), "fc1_bias": a[ffn + "fc1_b"].reshape(-1, 128).T,
        "fc2": on_partitions(a[ffn + "fc2_w"].T), "fc2_bias": a[ffn + "fc2_b"][:, None],
        **shape_constants(),
    }
    arrays = {k: np.ascontiguousarray(v) for k, v in arrays.items()}
    nc = bacc.Bacc("TRN2", target_bir_lowering=False, num_devices=1)
    d = {k: nc.dram_tensor(k, v.shape, mybir.dt.from_np(v.dtype), kind="ExternalInput").ap() for k, v in arrays.items()}
    d["result"] = nc.dram_tensor("result", (BATCH, SIDE, SIDE, CH), F32, kind="ExternalOutput").ap()
    program(nc, d)
    return run_bass_kernel_spmd(nc, [arrays], core_ids=[0]).results[0]["result"]
```
